# Optimizing a Trainium2 kernel written in Bass

```python
import numpy as np
import jax
import jax.numpy as jnp

def _softmax(x, axis=-1):
    return jax.nn.softmax(x, axis=axis)

def _gelu(x):
    return jax.nn.gelu(x, approximate=True)

def _silu(x):
    return jax.nn.silu(x)

def _sigmoid(x):
    return jax.nn.sigmoid(x)

def _layernorm(x, axis=-1, eps=1e-05):
    m = jnp.mean(x, axis=axis, keepdims=True)
    v = jnp.var(x, axis=axis, keepdims=True)
    return (x - m) / jnp.sqrt(v + eps)

def _scatter_add(tgt, idx, src, axis=0):
    return tgt.at[idx].add(src)

def _segment_sum(src, seg, n):
    return jax.ops.segment_sum(src, seg, n)
kernel_name = 'mk_decoder_postln_d1_seqx_r8_bb0b5a'

def setup_inputs(seed: int=0):
    np.random.seed(seed)
    _w = jnp.asarray

    def _rec_inputs():
        import jax
        import jax.numpy as jnp
        _rk = jax.random.key(seed)
        x = 7.22e-05 + 1 * jax.random.normal(jax.random.fold_in(_rk, 1), (16, 128, 128), jnp.float32)
        _lenS = 128 - jax.random.randint(jax.random.fold_in(_rk, 7), (16,), 0, max(1, 128 // 4) + 1, jnp.int32)
        _lenS2 = 128 - jax.random.randint(jax.random.fold_in(_rk, 8), (16,), 0, max(1, 128 // 4) + 1, jnp.int32)
        _ctx_1024P = jax.random.normal(jax.random.fold_in(_rk, 11), (16, 16, 128), jnp.float32)
        _ctx_1024c = jax.random.dirichlet(jax.random.fold_in(_rk, 511), 0.3 * jnp.ones((16,), jnp.float32), (16, 128))
        _ctx_1024t = jnp.einsum('bsk,bkd->bsd', _ctx_1024c, _ctx_1024P)
        _ctx_1024t = _ctx_1024t * jax.lax.rsqrt(jnp.mean(jnp.square(_ctx_1024t)) + 1e-12) * 0.953939
        ctx_1024 = 4.13588e-05 + 0.999923 * (_ctx_1024t + 0.3 * jax.random.normal(jax.random.fold_in(_rk, 611), (16, 128, 128), jnp.float32))
        return (x, ctx_1024)
    x, ctx_1024 = _rec_inputs()

    def _L0_attn_setup():
        import jax, jax.numpy as jnp
        import numpy as np
        import math
        B, S, D, H = (1, 256, 128, 16)
        HD = D // H
        SCALE = 1.0 / math.sqrt(HD)
        ENT = 0.5
        DECAY = 0.1
        SUP = 0.3
        EPS = 1e-05

        def _heads(x):
            b, s, _ = x.shape
            return x.reshape(b, s, H, HD).transpose(0, 2, 1, 3)
        key = jax.random.key(seed)
        ks = jax.random.split(key, 24)

        def w(k, shape, s=0.02):
            return jax.random.normal(k, shape, dtype=jnp.float32) * s
        return {'hidden_states': jax.random.normal(ks[0], (B, S, D), dtype=jnp.float32), 'Wq': w(ks[1], (D, D)), 'bq': jnp.zeros((D,), jnp.float32), 'Wk': w(ks[2], (D, D)), 'bk': jnp.zeros((D,), jnp.float32), 'Wv': w(ks[3], (D, D)), 'bv': jnp.zeros((D,), jnp.float32), 'Wo': w(ks[4], (D, D)), 'bo': jnp.zeros((D,), jnp.float32), 'Weq': w(ks[5], (D, D), 0.002), 'beq': jnp.zeros((D,), jnp.float32), 'Wek': w(ks[6], (D, D), 0.002), 'bek': jnp.zeros((D,), jnp.float32), 'amp_w': w(ks[7], (H, D)), 'amp_b': jnp.zeros((H,), jnp.float32), 'ph_w': w(ks[8], (H, D)), 'ph_b': jnp.zeros((H,), jnp.float32), 'mix_w': w(ks[9], (H, HD, HD)), 'mix_b': jnp.zeros((H, HD), jnp.float32), 'ln_g': jnp.ones((D,), jnp.float32), 'ln_b': jnp.zeros((D,), jnp.float32)}
    _L0_attn_all = _L0_attn_setup()
    _L0_attn_in = {k: v for k, v in _L0_attn_all.items() if k in ('Wq', 'bq', 'Wk', 'bk', 'Wv', 'bv', 'Wo', 'bo', 'Weq', 'beq', 'Wek', 'bek', 'amp_w', 'amp_b', 'ph_w', 'ph_b', 'mix_w', 'mix_b', 'ln_g', 'ln_b')}
    del _L0_attn_all

    def _L0_xattn_setup():
        import jax, jax.numpy as jnp
        import numpy as np
        B, L, D, H = (4, 256, 128, 16)
        HD = D // H
        key = jax.random.key(seed)
        ks = jax.random.split(key, 11)
        s = 1.0 / np.sqrt(D)
        return {'query': jax.random.normal(ks[0], (B, L, D), jnp.float32), 'key': jax.random.normal(ks[1], (B, L, D), jnp.float32), 'value': jax.random.normal(ks[2], (B, L, D), jnp.float32), 'Wq': jax.random.normal(ks[3], (D, D), jnp.float32) * s, 'bq': jnp.zeros((D,), jnp.float32), 'Wk': jax.random.normal(ks[4], (D, D), jnp.float32) * s, 'bk': jnp.zeros((D,), jnp.float32), 'Wv': jax.random.normal(ks[5], (D, D), jnp.float32) * s, 'bv': jnp.zeros((D,), jnp.float32), 'Wo': jax.random.normal(ks[6], (D, D), jnp.float32) * s, 'bo': jnp.zeros((D,), jnp.float32)}
    _L0_xattn_all = _L0_xattn_setup()
    _L0_xattn_in = {k: v for k, v in _L0_xattn_all.items() if k in ('Wq', 'bq', 'Wk', 'bk', 'Wv', 'bv', 'Wo', 'bo')}
    del _L0_xattn_all

    def _L0_ffn_setup():
        import jax, jax.numpy as jnp
        import numpy as np
        N_EXPERTS = 16
        TOP_K = 4
        HIDDEN = 128
        INTER = 64
        B, S = (2, 128)
        key = jax.random.key(seed)
        k1, k2, k3, k4, k5 = jax.random.split(key, 5)
        return {'hidden_states': jax.random.normal(k1, (B, S, HIDDEN), dtype=jnp.float32), 'gate_w': jax.random.normal(k2, (N_EXPERTS, HIDDEN), dtype=jnp.float32) * 0.02, 'w1': jax.random.normal(k3, (N_EXPERTS, HIDDEN, INTER), dtype=jnp.float32) * 0.02, 'w3': jax.random.normal(k4, (N_EXPERTS, HIDDEN, INTER), dtype=jnp.float32) * 0.02, 'w2': jax.random.normal(k5, (N_EXPERTS, INTER, HIDDEN), dtype=jnp.float32) * 0.02}
    _L0_ffn_all = _L0_ffn_setup()
    _L0_ffn_in = {k: v for k, v in _L0_ffn_all.items() if k in ('gate_w', 'w1', 'w3', 'w2')}
    del _L0_ffn_all
    return {'x': x, 'ctx_1024': ctx_1024, 'L0_attn_Wq': _L0_attn_in['Wq'], 'L0_attn_bq': _L0_attn_in['bq'], 'L0_attn_Wk': _L0_attn_in['Wk'], 'L0_attn_bk': _L0_attn_in['bk'], 'L0_attn_Wv': _L0_attn_in['Wv'], 'L0_attn_bv': _L0_attn_in['bv'], 'L0_attn_Wo': _L0_attn_in['Wo'], 'L0_attn_bo': _L0_attn_in['bo'], 'L0_attn_Weq': _L0_attn_in['Weq'], 'L0_attn_beq': _L0_attn_in['beq'], 'L0_attn_Wek': _L0_attn_in['Wek'], 'L0_attn_bek': _L0_attn_in['bek'], 'L0_attn_amp_w': _L0_attn_in['amp_w'], 'L0_attn_amp_b': _L0_attn_in['amp_b'], 'L0_attn_ph_w': _L0_attn_in['ph_w'], 'L0_attn_ph_b': _L0_attn_in['ph_b'], 'L0_attn_mix_w': _L0_attn_in['mix_w'], 'L0_attn_mix_b': _L0_attn_in['mix_b'], 'L0_attn_ln_g': _L0_attn_in['ln_g'], 'L0_attn_ln_b': _L0_attn_in['ln_b'], 'L0_xattn_Wq': _L0_xattn_in['Wq'], 'L0_xattn_bq': _L0_xattn_in['bq'], 'L0_xattn_Wk': _L0_xattn_in['Wk'], 'L0_xattn_bk': _L0_xattn_in['bk'], 'L0_xattn_Wv': _L0_xattn_in['Wv'], 'L0_xattn_bv': _L0_xattn_in['bv'], 'L0_xattn_Wo': _L0_xattn_in['Wo'], 'L0_xattn_bo': _L0_xattn_in['bo'], 'L0_ffn_gate_w': _L0_ffn_in['gate_w'], 'L0_ffn_w1': _L0_ffn_in['w1'], 'L0_ffn_w3': _L0_ffn_in['w3'], 'L0_ffn_w2': _L0_ffn_in['w2']}

def reference(x, ctx_1024, L0_attn_Wq, L0_attn_bq, L0_attn_Wk, L0_attn_bk, L0_attn_Wv, L0_attn_bv, L0_attn_Wo, L0_attn_bo, L0_attn_Weq, L0_attn_beq, L0_attn_Wek, L0_attn_bek, L0_attn_amp_w, L0_attn_amp_b, L0_attn_ph_w, L0_attn_ph_b, L0_attn_mix_w, L0_attn_mix_b, L0_attn_ln_g, L0_attn_ln_b, L0_xattn_Wq, L0_xattn_bq, L0_xattn_Wk, L0_xattn_bk, L0_xattn_Wv, L0_xattn_bv, L0_xattn_Wo, L0_xattn_bo, L0_ffn_gate_w, L0_ffn_w1, L0_ffn_w3, L0_ffn_w2):
    import jax
    import jax.numpy as jnp

    def _L0_attn_ref(hidden_states, Wq, bq, Wk, bk, Wv, bv, Wo, bo, Weq, beq, Wek, bek, amp_w, amp_b, ph_w, ph_b, mix_w, mix_b, ln_g, ln_b):
        import jax, jax.numpy as jnp
        import numpy as np
        import math
        B, S, D, H = (1, 256, 128, 16)
        HD = D // H
        SCALE = 1.0 / math.sqrt(HD)
        ENT = 0.5
        DECAY = 0.1
        SUP = 0.3
        EPS = 1e-05

        def _heads(x):
            b, s, _ = x.shape
            return x.reshape(b, s, H, HD).transpose(0, 2, 1, 3)
        hs = hidden_states
        b, s, _ = hs.shape
        q = _heads(hs @ Wq.T + bq)
        k = _heads(hs @ Wk.T + bk)
        v = _heads(hs @ Wv.T + bv)
        scores = jnp.einsum('bhqd,bhkd->bhqk', q, k) * SCALE
        eq = _heads(hs @ Weq.T + beq)
        ek = _heads(hs @ Wek.T + bek)
        pos = jnp.arange(s)
        decay = jnp.exp(-DECAY * jnp.abs(pos[:, None] - pos[None, :]).astype(jnp.float32))
        esc = jnp.einsum('bhqd,bhkd->bhqk', eq, ek) * (1.0 / math.sqrt(HD)) * decay
        attn = jax.nn.softmax(scores + ENT * esc, axis=-1)
        amps = jax.nn.sigmoid(hs @ amp_w.T + amp_b)
        phases = jnp.tanh(hs @ ph_w.T + ph_b) * math.pi
        a = amps.transpose(0, 2, 1)[..., None]
        p = phases.transpose(0, 2, 1)[..., None]
        sup = jnp.einsum('bhsd,hod->bhso', v, mix_w) + mix_b[None, :, None, :]
        mixed = v + SUP * a * jnp.cos(p) * sup + SUP * a * jnp.sin(p) * jnp.roll(sup, 1, axis=-1)
        ctx = jnp.einsum('bhqk,bhkd->bhqd', attn, mixed)
        ctx = ctx.transpose(0, 2, 1, 3).reshape(b, s, D)
        out = ctx @ Wo.T + bo
        res = hs + out
        mu = jnp.mean(res, axis=-1, keepdims=True)
        var = jnp.mean((res - mu) ** 2, axis=-1, keepdims=True)
        return (res - mu) * jax.lax.rsqrt(var + EPS) * ln_g + ln_b

    def _L0_xattn_ref(query, key, value, Wq, bq, Wk, bk, Wv, bv, Wo, bo):
        import jax, jax.numpy as jnp
        import numpy as np
        B, L, D, H = (4, 256, 128, 16)
        HD = D // H
        b = query.shape[0]
        Q = query @ Wq.T + bq
        K = key @ Wk.T + bk
        V = value @ Wv.T + bv
        Q = Q.reshape(b, -1, H, HD).transpose(0, 2, 1, 3)
        K = K.reshape(b, -1, H, HD).transpose(0, 2, 1, 3)
        V = V.reshape(b, -1, H, HD).transpose(0, 2, 1, 3)
        energy = jnp.einsum('bhqd,bhkd->bhqk', Q, K) / jnp.sqrt(jnp.float32(HD))
        attn = jax.nn.softmax(energy, axis=-1)
        x = jnp.einsum('bhqk,bhkd->bhqd', attn, V)
        x = x.transpose(0, 2, 1, 3).reshape(b, -1, D)
        return x @ Wo.T + bo

    def _L0_ffn_ref(hidden_states, gate_w, w1, w3, w2):
        import jax, jax.numpy as jnp
        import numpy as np
        N_EXPERTS = 16
        TOP_K = 4
        HIDDEN = 128
        INTER = 64
        B, S = (2, 128)
        'DeepseekV3 MoE adapter forward: router -> sparse scores -> expert GLU MLP -> combine.'
        b, s, h = hidden_states.shape
        x = hidden_states.reshape(-1, h)
        logits = jnp.einsum('th,eh->te', x, gate_w)
        probs = jax.nn.softmax(logits, axis=-1)
        topk_w, topk_idx = jax.lax.top_k(probs, TOP_K)
        topk_w = topk_w / jnp.sum(topk_w, axis=-1, keepdims=True)
        one_hot = (topk_idx[..., None] == jnp.arange(N_EXPERTS)).astype(topk_w.dtype)
        scores = jnp.einsum('tk,tke->te', topk_w, one_hot)
        g = jnp.einsum('th,ehi->tei', x, w1)
        u = jnp.einsum('th,ehi->tei', x, w3)
        act = jax.nn.silu(g) * u
        expert_out = jnp.einsum('tei,eih->teh', act, w2)
        out = jnp.einsum('teh,te->th', expert_out, scores)
        return out.reshape(b, s, h)
    x = _layernorm(x + _L0_attn_ref(x, L0_attn_Wq, L0_attn_bq, L0_attn_Wk, L0_attn_bk, L0_attn_Wv, L0_attn_bv, L0_attn_Wo, L0_attn_bo, L0_attn_Weq, L0_attn_beq, L0_attn_Wek, L0_attn_bek, L0_attn_amp_w, L0_attn_amp_b, L0_attn_ph_w, L0_attn_ph_b, L0_attn_mix_w, L0_attn_mix_b, L0_attn_ln_g, L0_attn_ln_b), axis=-1)
    x = _layernorm(x + _L0_xattn_ref(x, ctx_1024, ctx_1024, L0_xattn_Wq, L0_xattn_bq, L0_xattn_Wk, L0_xattn_bk, L0_xattn_Wv, L0_xattn_bv, L0_xattn_Wo, L0_xattn_bo), axis=-1)
    x = _layernorm(x + _L0_ffn_ref(x, L0_ffn_gate_w, L0_ffn_w1, L0_ffn_w3, L0_ffn_w2), axis=-1)
    return x

_drawn_inputs = setup_inputs


def setup_inputs(seed=0):
    import zlib

    import numpy as np

    out = dict(_drawn_inputs(seed))
    spreads = {'L0_attn_bq': (0.0, 0.8),
     'L0_attn_bk': (0.0, 0.8),
     'L0_attn_bv': (0.0, 0.8),
     'L0_attn_bo': (0.0, 0.1),
     'L0_attn_beq': (0.0, 0.8),
     'L0_attn_bek': (0.0, 0.8),
     'L0_attn_amp_b': (0.0, 0.8),
     'L0_attn_ph_b': (0.0, 0.8),
     'L0_attn_mix_b': (0.0, 0.8),
     'L0_attn_ln_g': (1.0, 0.2),
     'L0_attn_ln_b': (0.0, 0.1),
     'L0_xattn_bq': (0.0, 0.378),
     'L0_xattn_bk': (0.0, 0.8),
     'L0_xattn_bv': (0.0, 0.1),
     'L0_xattn_bo': (0.0, 0.1)}
    factors = {'L0_attn_Wq': 8.0,
     'L0_attn_Wk': 8.0,
     'L0_attn_Wv': 8.0,
     'L0_attn_Wo': 5.644,
     'L0_attn_Weq': 8.0,
     'L0_attn_Wek': 8.0,
     'L0_attn_amp_w': 8.0,
     'L0_attn_ph_w': 8.0,
     'L0_attn_mix_w': 8.0,
     'L0_ffn_gate_w': 8.0,
     'L0_ffn_w1': 8.0,
     'L0_ffn_w3': 8.0,
     'L0_ffn_w2': 8.0}
    for name, (base, spread) in spreads.items():
        noise = np.random.default_rng([zlib.crc32(name.encode()), seed]).standard_normal(out[name].shape)
        drawn = base * np.exp(spread * noise) if base else spread * noise
        out[name] = jnp.asarray(drawn.astype(out[name].dtype))
    for name, factor in factors.items():
        out[name] = (out[name] * factor).astype(out[name].dtype)
    return out
```

```python
import math
from contextlib import ExitStack

import concourse.bass as bass
from concourse import mybir

F32 = mybir.dt.float32
BF16 = mybir.dt.bfloat16
U8 = mybir.dt.uint8
ACT = mybir.ActivationFunctionType
ALU = mybir.AluOpType
AX = mybir.AxisListType

NB = 16
S = 128
D = 128
H = 16
HD = D // H
NE = 16
INTER = 64
TOPK = 4
EPS = 1e-5
SCALE = 1.0 / math.sqrt(HD)
ENT = 0.5
DECAY = 0.1
SUP = 0.3
GH = 4
NG = H // GH
KC = NE * INTER // 128
TC = 512
NCH = NB * S // TC
WQ, WEQ, WK, WEK, WV, WO, XQ, XK, XV, XO = range(10)
VSZ = 2 * D + 2 * H


class Batch:

    def __init__(self, pair, par):
        self.pair, self.par = pair, par
        self.n = pair * 2 + par

    def back(self, lag):
        p = self.par - lag
        return Batch(self.pair + p // 2, p % 2)

    @property
    def live(self):
        return not isinstance(self.n, int) or 0 <= self.n < NB


def unit_back(b, g, lag):
    q = g - lag
    return b.back(-(q // NG)), q % NG


def build(nc, a, k, out):
    with ExitStack() as ctx:
        def sb(name, shape, dt=F32):
            return ctx.enter_context(nc.sbuf_tensor(name, shape, dt))

        def sem(name):
            return ctx.enter_context(nc.semaphore(name))

        ident = sb("ident", [128, 128])
        neg_ident = sb("neg_ident", [128, 128], BF16)
        ident_bf = sb("ident_bf", [128, 128], BF16)
        feat = sb("feat", [128, 2, 2, 2, S])
        upper_f = sb("upper_f", [128, S])
        upper = sb("upper", [128, S], U8)
        head_mask = sb("head_mask", [128, H])
        sel_f = sb("sel_f", [128, KC, 128])
        sel = sb("sel", [128, KC, 128], BF16)
        wn = sb("wn", [128, 10, D])
        gates_n = sb("gates_n", [48, D])
        bias_rows = sb("bias_rows", [7, D])
        mix_n = sb("mix_n", [128, HD])
        mix_bd_n = sb("mix_bd_n", [128, H, HD])
        mix_bd = sb("mix_bd", [128, D])
        bv_cols = sb("bv_cols", [128, 128])
        wqk1 = sb("wqk1", [128, 2, H, 2, HD])
        wall = sb("wall", [128, VSZ])
        wo_t = sb("wo_t", [128, D])
        xw_t = sb("xw_t", [128, 4, D])
        gate_t = sb("gate_t", [128, NE])
        bias_t = sb("bias_t", [128, 8])
        bias_xq = sb("bias_xq", [128, 1])
        row_in = sb("row_in", [128, VSZ])
        row_bias = sb("row_bias", [128, VSZ])
        bo1 = sb("bo1", [128, D])
        ln_g = sb("ln_g", [128, D])
        ln_b = sb("ln_b", [128, D])
        bv2 = sb("bv2", [128, D])
        bo2 = sb("bo2", [128, D])
        x_tok = sb("x_tok", [128, NB, D])
        c_tok = sb("c_tok", [128, NB, D])
        x_t = sb("x_t", [128, NB * S])
        c_t = sb("c_t", [128, NB * S])
        xb_all = sb("xb_all", [128, NB, D])
        xl_all = sb("xl_all", [128, NB, D])
        vsz = sb("vsz", [128, NB, VSZ])
        v2_all = sb("v2_all", [128, NB, D])
        ph_t = sb("ph_t", [128, 6, NB, H])
        coef = sb("coef", [128, 2, NB, H])
        minus_half = sb("minus_half", [128, NB])
        waiter = sb("waiter", [128, 1])
        half_pi = sb("half_pi", [128, 1])
        w1 = sb("w1", [128, NE * INTER])
        w3 = sb("w3", [128, NE * INTER])
        w2 = sb("w2", [128, KC, D])
        proj = sb("proj", [128, 2, 2, S])
        qk = [sb(f"qk{p}", [128, 2, 2, 2, S]) for p in range(2)]
        kbd = [sb(f"kbd{p}", [128, 8, 2, 2, S]) for p in range(2)]
        vmix = [sb(f"vmix{p}", [128, H, 2, HD]) for p in range(2)]
        mixa = sb("mixa", [128, D])
        mixb = sb("mixb", [128, D])
        mixc = sb("mixc", [128, D])
        shift = sb("shift", [128, 2, GH], BF16)
        prob = [sb(f"prob{p}", [128, GH, S]) for p in range(2)]
        prob_t = [sb(f"prob_t{p}", [128, GH, S]) for p in range(2)]
        pvs = sb("pvs", [128, NG, S])
        rden = sb("rden", [128, H])
        attn_o = sb("attn_o", [128, D])
        attn_ot = sb("attn_ot", [128, D])
        res = sb("res", [128, D])
        res2 = sb("res2", [128, D])
        stats = sb("stats", [128, 2, 6])
        mv = sb("mv", [128, 2, 2])
        veps = sb("veps", [128, 2])
        rstd = sb("rstd", [128, 2])
        rt = vsz[:].rearrange("p b n -> p (b n)")[:, 0:8 * NB * NE].rearrange("p (a b e) -> p a b e", a=8, b=NB)
        r8 = sb("r8", [128, NB, 8])
        rsm = sb("rsm", [128, 4, NB])
        s3 = sb("s3", [128, NB, 3, NE], BF16)
        st = sb("st", [128, NB * S], BF16)
        scratch = kbd[0][:].rearrange("p a b c t -> p (a b c t)")
        sg = [scratch[:, TC * p:TC * p + TC] for p in range(2)]
        h1 = [scratch[:, TC * (2 + p):TC * (3 + p)] for p in range(2)]
        actt = [scratch[:, TC * (4 + p):TC * (5 + p)] for p in range(2)]
        fres = sb("fres", [128, 4, D])
        fstats = sb("fstats", [128, 4, 6])
        fmv = sb("fmv", [128, 4, 2])
        fveps = sb("fveps", [128, 4])
        frstd = sb("frstd", [128, 4])
        fout = sb("fout", [128, 4, D])

        x1 = x_tok
        x2 = c_tok
        bank = [ctx.enter_context(nc.psum_tensor(f"bank{i}", [128, 512], F32)) for i in range(8)]

        in_const = sem("in_const")
        in_w = sem("in_w")
        in_rows = sem("in_rows")
        in_small = sem("in_small")
        in_feat = sem("in_feat")
        in_x = sem("in_x")
        in_c = sem("in_c")
        in_ffn = sem("in_ffn")
        pool_const = sem("pool_const")
        pe_set = sem("pe_set")
        dve_set = sem("dve_set")
        act_set = sem("act_set")
        gate_step = sem("gate_step")
        pool_set = sem("pool_set")
        stored = sem("stored")

        class Layer:

            def __init__(self, n):
                self.proj_done = sem(f"proj_done{n}")
                self.proj_ev = sem(f"proj_ev{n}")
                self.qk_ready = sem(f"qk_ready{n}")
                self.kbd_in = [sem(f"kbd_in{n}{p}") for p in range(2)]
                self.scores = sem(f"scores{n}")
                self.picked = sem(f"picked{n}")
                self.maxed = sem(f"maxed{n}")
                self.shifted = sem(f"shifted{n}")
                self.exped = sem(f"exped{n}")
                self.turned = sem(f"turned{n}")
                self.turned_ev = sem(f"turned_ev{n}")
                self.v_ready = sem(f"v_ready{n}")
                self.v_step = sem(f"v_step{n}")
                self.pv = sem(f"pv{n}")
                self.pv_ev = sem(f"pv_ev{n}")
                self.o_tok = sem(f"o_tok{n}")
                self.normed = sem(f"normed{n}")
                self.norm_step = sem(f"norm_step{n}")
                self.o_t = sem(f"o_t{n}")
                self.o_t_ev = sem(f"o_t_ev{n}")
                self.o_out = sem(f"o_out{n}")
                self.tail = sem(f"tail{n}")
                self.rstd = sem(f"rstd{n}")
        L1, L2 = Layer(1), Layer(2)
        TAIL1, TAIL2 = 10, 5

        turn1 = sem("turn1")
        turn1_ev = sem("turn1_ev")
        xb2 = sem("xb2")
        turn2 = sem("turn2")
        turn2_ev = sem("turn2_ev")
        route_mm = sem("route_mm")
        route = sem("route")
        route_exp = sem("route_exp")
        route_t = sem("route_t")
        route_ev = sem("route_ev")
        gate_mm = sem("gate_mm")
        up_mm = sem("up_mm")
        silu = sem("silu")
        glu = sem("glu")
        glu_s = sem("glu_s")
        down = sem("down")
        ftail = sem("ftail")
        fst = sem("fst")
        inner_g = sem("inner_g")
        frs = sem("frs")
        FT = 10

        PE_X, PE_SUP, PE_C, PE_VSZ, PE_V2 = 4, 8, 9, 13, 13 + NB
        DV_MIX, DV_KBD0, DV_SUP, DV_WALL, DV_END = 4, 6, 23, 27, 49
        RT_S3 = 27
        block = ctx.enter_context(nc.Block())

        @block.sync
        def _(sp):
            sp.dma_start(ident[:], k["ident"]).then_inc(in_const, 16)
            for i, n in enumerate(["L0_attn_Wq", "L0_attn_Weq", "L0_attn_Wk", "L0_attn_Wek", "L0_attn_Wv",
                                   "L0_attn_Wo", "L0_xattn_Wq", "L0_xattn_Wk", "L0_xattn_Wv", "L0_xattn_Wo"]):
                sp.dma_start(wn[:, i, :], a[n]).then_inc(in_w, 16)
            for c in range(4):
                sp.dma_start(x_tok[:, 4 * c:4 * c + 4, :],
                             a["x"][4 * c:4 * c + 4].rearrange("b t d -> t b d")).then_inc(in_x, 16)
            for c in range(4):
                sp.dma_start(c_tok[:, 4 * c:4 * c + 4, :],
                             a["ctx_1024"][4 * c:4 * c + 4].rearrange("b t d -> t b d")).then_inc(in_c, 16)
            sp.dma_start(sel_f[:], k["sel"].rearrange("p (c m) -> p c m", c=KC)).then_inc(in_ffn, 16)
            sp.dma_start(w1[:].rearrange("p (e i) -> p e i", e=NE),
                         a["L0_ffn_w1"].rearrange("e h i -> h e i")).then_inc(in_ffn, 16)
            sp.dma_start(w3[:].rearrange("p (e i) -> p e i", e=NE),
                         a["L0_ffn_w3"].rearrange("e h i -> h e i")).then_inc(in_ffn, 16)
            sp.dma_start(w2[:], a["L0_ffn_w2"].rearrange("(c e) i h -> (e i) c h", e=2)).then_inc(in_ffn, 16)

            def spread_keys(b):
                if not b.live:
                    return
                sp.wait_ge(L1.qk_ready, b.n + 1)
                if not isinstance(b.n, int) or b.n >= 2:
                    sp.wait_ge(L1.scores, NG * b.n - NG)
                for h in range(8):
                    sp.dma_start(kbd[b.par][16 * h:16 * h + 16, h, :, :, :],
                                 qk[b.par][16 * h:16 * h + 16, 1, :, :, :]).then_inc(L1.kbd_in[b.par], 16)

            def pair(p):
                for par in range(2):
                    spread_keys(Batch(p, par))

            sp.wait_ge(dve_set, DV_KBD0)
            pair(0)
            with sp.Fori(1, NB // 2) as p:
                pair(p)

            with sp.Fori(0, NCH) as c:
                sp.wait_ge(ftail, c * FT + FT)
                sp.dma_start(out[bass.ds(c * 4, 4)].rearrange("b t d -> t b d"), fout[:]).then_inc(stored, 16)
            sp.wait_ge(stored, 16 * NCH)

        @block.gpsimd
        def _(pool):
            def rows(dst, src):
                n = src.shape[0]
                pool.dma_start(dst, src.unsqueeze(0).broadcast_to([128, n])).then_inc(in_rows, 16)

            for kind, names in enumerate([("L0_attn_bq", "L0_attn_beq"), ("L0_attn_bk", "L0_attn_bek")]):
                for half in range(2):
                    for e, n in enumerate(names):
                        r = 2 * kind + half
                        pool.dma_start(bias_rows[r:r + 1, :].rearrange("r (h e f) -> r h e f", h=8, e=2)[:, :, e, :],
                                       a[n][64 * half:64 * half + 64].rearrange("(r h f) -> r h f", r=1, f=HD)
                                       ).then_inc(in_small, 16)
            for r, n in ((4, "L0_xattn_bq"), (5, "L0_xattn_bk"), (6, "L0_attn_bv")):
                pool.dma_start(bias_rows[r:r + 1, :], a[n].unsqueeze(0)).then_inc(in_small, 16)
            for r, n in enumerate(("L0_attn_amp_w", "L0_attn_ph_w", "L0_ffn_gate_w")):
                pool.dma_start(gates_n[16 * r:16 * r + 16, :], a[n]).then_inc(in_small, 16)
            pool.dma_start(mix_n[:], a["L0_attn_mix_w"].rearrange("h o d -> (h o) d")).then_inc(in_small, 16)
            pool.dma_start(head_mask[:], k["head_mask"]).then_inc(in_small, 16)
            pool.dma_start(feat[:].rearrange("p a b c t -> p (a b c t)"), k["feat"]).then_inc(in_feat, 16)
            pool.dma_start(upper_f[:], k["upper"]).then_inc(in_feat, 16)
            rows(row_in[:, 0:D], a["L0_attn_bv"])
            rows(row_in[:, D:2 * D], a["L0_attn_mix_b"].rearrange("h o -> (h o)"))
            rows(row_in[:, 2 * D:2 * D + H], a["L0_attn_amp_b"])
            rows(row_in[:, 2 * D + H:VSZ], a["L0_attn_ph_b"])
            rows(bo1[:], a["L0_attn_bo"])
            rows(ln_g[:], a["L0_attn_ln_g"])
            rows(ln_b[:], a["L0_attn_ln_b"])
            rows(bv2[:], a["L0_xattn_bv"])
            rows(bo2[:], a["L0_xattn_bo"])
            pool.memset(minus_half[:], -0.5)
            for p in range(2):
                pool.memset(vmix[p][:, :, 1, :], 1.0)
            pool.wait_ge(in_rows, 9 * 16)
            pool.wait_ge(in_x, 4 * 16)
            pool.tensor_tensor(xb_all[:], x_tok[:], bo1[:].unsqueeze(1).broadcast_to([128, NB, D]),
                               ALU.add).then_inc(pool_set, 1)
            pool.tensor_tensor(xl_all[:], x_tok[:], ln_b[:].unsqueeze(1).broadcast_to([128, NB, D]),
                               ALU.add).then_inc(pool_set, 1)

            def scale_qk(b):
                pool.wait_ge(L1.proj_ev, b.n * 4 + 4)
                if not isinstance(b.n, int) or b.n >= 2:
                    pool.wait_ge(L1.scores, NG * b.n - NG)
                if isinstance(b.n, int) and b.n == 0:
                    pool.wait_ge(in_feat, 2 * 16)
                pool.tensor_tensor(
                    qk[b.par][:].rearrange("p k u h t -> p k u (h t)"),
                    proj[:].rearrange("p k h t -> p k (h t)").unsqueeze(2).broadcast_to([128, 2, 2, 2 * S]),
                    feat[:].rearrange("p k u h t -> p k u (h t)"), ALU.mult).then_inc(L1.qk_ready, 1)

            def mix_values(b):
                if isinstance(b.n, int) and b.n == 0:
                    pool.wait_ge(gate_step, 12)
                if not isinstance(b.n, int) or b.n >= 2:
                    pool.wait_ge(L1.pv, NG * b.n - NG)
                row = vsz[:, bass.ds(b.n, 1), :].rearrange("p b n -> p (b n)")
                val = row[:, 0:D]
                sup = row[:, D:2 * D].rearrange("p (h f) -> p h f", f=HD)
                c1 = coef[:, 0, bass.ds(b.n, 1), :].rearrange("p b h -> p (b h)").unsqueeze(2)
                c2 = coef[:, 1, bass.ds(b.n, 1), :].rearrange("p b h -> p (b h)").unsqueeze(2)
                ma = mixa[:].rearrange("p (h f) -> p h f", f=HD)
                mb = mixb[:].rearrange("p (h f) -> p h f", f=HD)
                pool.tensor_tensor(ma, sup, c1.broadcast_to([128, H, HD]), ALU.mult).then_inc(L1.v_step, 1)
                pool.tensor_tensor(mb[:, :, 1:HD], sup[:, :, 0:HD - 1], c2.broadcast_to([128, H, HD - 1]),
                                   ALU.mult).then_inc(L1.v_step, 1)
                pool.tensor_tensor(mb[:, :, 0:1], sup[:, :, HD - 1:HD], c2, ALU.mult).then_inc(L1.v_step, 1)
                pool.wait_ge(L1.v_step, b.n * 4 + 3)
                pool.tensor_tensor(mixc[:], mixa[:], mixb[:], ALU.add).then_inc(L1.v_step, 1)
                pool.wait_ge(L1.v_step, b.n * 4 + 4)
                pool.tensor_tensor(vmix[b.par][:, :, 0, :], mixc[:].rearrange("p (h f) -> p h f", f=HD),
                                   val.rearrange("p (h f) -> p h f", f=HD), ALU.add).then_inc(L1.v_ready, 1)

            def power(L, b, which, step, per, steps):
                pool.wait_ge(L.tail, b.n * steps + step)
                pool.tensor_tensor(rstd[:, which:which + 1], veps[:, which:which + 1], minus_half[:, 0:1],
                                   ALU.pow).then_inc(L.rstd, 1)

            def pair1(p):
                for par in range(2):
                    b = Batch(p, par)
                    if b.live:
                        scale_qk(b)
                    if b.back(1).live:
                        mix_values(b.back(1))
                    if b.back(3).live:
                        power(L1, b.back(3), 0, 4, 2, TAIL1)
                        power(L1, b.back(3), 1, 9, 2, TAIL1)

            pair1(0)
            pair1(1)
            with pool.Fori(2, 8) as p:
                pair1(p)
            pair1(8)
            pair1(9)

            pool.wait_ge(L1.tail, NB * TAIL1)
            pool.tensor_tensor(xb_all[:], x1[:], bo2[:].unsqueeze(1).broadcast_to([128, NB, D]),
                               ALU.add).then_inc(xb2, 1)

            def spread_keys2(b):
                pool.wait_ge(L2.proj_ev, b.n * 2 + 2)
                if isinstance(b.n, int) and b.n < 2:
                    pool.wait_ge(L1.scores, NG * NB)
                else:
                    pool.wait_ge(L2.scores, NG * b.n - NG)
                pool.tensor_tensor(
                    kbd[b.par][:].rearrange("p a b c t -> p (a b c t)")[:, 0:H * S].rearrange("p (h t) -> p h t", t=S),
                    qk[b.par][:, 1, 0, 0, :].unsqueeze(1).broadcast_to([128, H, S]),
                    head_mask[:].unsqueeze(2).broadcast_to([128, H, S]), ALU.mult).then_inc(L2.qk_ready, 1)

            def values2(b):
                if isinstance(b.n, int) and b.n < 2:
                    pool.wait_ge(L1.pv, NG * NB)
                else:
                    pool.wait_ge(L2.pv, NG * b.n - NG)
                pool.tensor_copy(vmix[b.par][:, :, 0, :],
                                 v2_all[:, bass.ds(b.n, 1), :].rearrange("p b (h f) -> p (b h) f", f=HD)
                                 ).then_inc(L2.v_ready, 1)

            def pair2(p):
                for par in range(2):
                    b = Batch(p, par)
                    if b.live:
                        spread_keys2(b)
                    if b.back(1).live:
                        values2(b.back(1))
                    if b.back(3).live:
                        power(L2, b.back(3), 0, 4, 1, TAIL2)

            pair2(0)
            pair2(1)
            with pool.Fori(2, 8) as p:
                pair2(p)
            pair2(8)
            pair2(9)

            with pool.Fori(0, NCH) as c:
                pool.wait_ge(ftail, c * FT + 6)
                pool.tensor_tensor(frstd[:], fveps[:], minus_half[:, 0:4], ALU.pow).then_inc(frs, 1)

        @block.tensor
        def _(pe):
            pe.wait_ge(in_const, 16)
            pe.wait_ge(in_feat, 2 * 16)
            pe.wait_ge(in_w, 10 * 16)
            pe.wait_ge(in_small, (8 + 3 + 3 + 2) * 16)
            for i, w in enumerate((WQ, WEQ, WK, WEK)):
                t = pe.transpose(bank[0][:, 128 * i:128 * i + 128], wn[:, w, :], ident[:])
            t.then_inc(pe_set, 1)
            for i, w in enumerate((WV, WO, XQ, XK)):
                t = pe.transpose(bank[1][:, 128 * i:128 * i + 128], wn[:, w, :], ident[:])
            t.then_inc(pe_set, 1)
            for i, w in enumerate((XV, XO)):
                pe.transpose(bank[2][:, 128 * i:128 * i + 128], wn[:, w, :], ident[:])
            pe.transpose(bank[2][:, 256:304], gates_n[:], ident[0:48, 0:48])
            pe.transpose(bank[2][:, 304:311], bias_rows[:], ident[0:7, 0:7]).then_inc(pe_set, 1)
            pe.wait_ge(dve_set, DV_MIX)
            pe.transpose(bank[3][:, 0:128], mix_bd_n[:].rearrange("p h f -> p (h f)"), ident[:]).then_inc(pe_set, 1)
            pe.wait_ge(in_x, 4 * 16)
            for c in range(4):
                for j in range(4):
                    t = pe.transpose(bank[4 + c][:, 128 * j:128 * j + 128], x_tok[:, 4 * c + j, :], ident[:])
                t.then_inc(pe_set, 1)
            pe.wait_ge(dve_set, DV_SUP)
            pe.matmul(bank[0][:, 0:128], wn[:, WV, :], mix_bd[:], start=True, stop=True)
            pe.matmul(bank[0][:, 128:256], bv_cols[:], mix_bd[:], start=True, stop=True).then_inc(pe_set, 1)
            pe.wait_ge(in_c, 4 * 16)
            for c in range(4):
                pe.wait_ge(act_set, c + 1)
                for j in range(4):
                    t = pe.transpose(bank[4 + c][:, 128 * j:128 * j + 128], c_tok[:, 4 * c + j, :], ident[:])
                t.then_inc(pe_set, 1)
            pe.wait_ge(dve_set, DV_WALL)
            pe.wait_ge(act_set, 4)
            for b in range(NB):
                if b >= 4:
                    pe.wait_ge(dve_set, DV_WALL + b - 3)
                pe.matmul(bank[b % 4][:, 0:VSZ], x_t[:, 128 * b:128 * b + 128], wall[:],
                          start=True, stop=True).then_inc(pe_set, 1)
            for c in range(4):
                pe.wait_ge(act_set, 5 + c)
                for j in range(4):
                    m = pe.matmul(bank[4 + c][:, 128 * j:128 * j + 128],
                                  c_t[:, 512 * c + 128 * j:512 * c + 128 * j + 128], xw_t[:, 2, :],
                                  start=True, stop=True)
                m.then_inc(pe_set, 1)

            def project(L, b, decayed):
                if not isinstance(b.n, int) or b.n >= 1:
                    pe.wait_ge(L.proj_ev, b.n * (4 if decayed else 2))
                if decayed:
                    xt = x_t[:, bass.ds(b.n * S, S)]
                    for kind in range(2):
                        for half in range(2):
                            m = pe.matmul(bank[6][:, 256 * kind + 128 * half:256 * kind + 128 * half + 128],
                                          wqk1[:, kind, 8 * half:8 * half + 8, :, :].rearrange("p h e f -> p (h e f)"),
                                          xt, start=True, stop=True)
                else:
                    pe.matmul(bank[6][:, 0:128], xw_t[:, 0, :], x_t[:, bass.ds(b.n * S, S)], start=True, stop=True)
                    m = pe.matmul(bank[6][:, 128:256], xw_t[:, 1, :], c_t[:, bass.ds(b.n * S, S)],
                                  start=True, stop=True)
                m.then_inc(L.proj_done, 1)

            def score(L, b, g, decayed):
                u = b.n * NG + g
                if g == 0:
                    pe.wait_ge(L.qk_ready, b.n + 1)
                    if decayed:
                        pe.wait_ge(L.kbd_in[b.par], b.pair * 128 + 128)
                if not isinstance(u, int) or u >= 2:
                    pe.wait_ge(L.exped, u - 1)
                if decayed:
                    half, h0 = g // 2, 4 * (g % 2)
                    pe.matmul(bank[g % 2][:].rearrange("p (h t) -> p h t", h=GH), qk[b.par][:, 0, 0, half, :],
                              kbd[b.par][:, h0:h0 + 4, 0, half, :], start=True, stop=True, skip_group_check=True)
                    if not isinstance(u, int) or u >= 1:
                        pe.wait_ge(L.picked, u)
                    pe.matmul(bank[2][:].rearrange("p (h t) -> p h t", h=GH), qk[b.par][:, 0, 1, half, :],
                              kbd[b.par][:, h0:h0 + 4, 1, half, :], start=True, stop=True).then_inc(L.scores, 1)
                else:
                    flat = kbd[b.par][:].rearrange("p a b c t -> p (a b c t)")
                    pe.matmul(bank[g % 2][:], qk[b.par][:, 0, 0, 0, :], flat[:, 512 * g:512 * g + 512],
                              start=True, stop=True, skip_group_check=True).then_inc(L.scores, 1)

            def subtract_max(L, b, g):
                u = b.n * NG + g
                pe.wait_ge(L.maxed, u + 1)
                pe.matmul(bank[g % 2][:].rearrange("p (h t) -> p h t", h=GH), neg_ident[:],
                          shift[:, g % 2, :].unsqueeze(2).broadcast_to([128, GH, S]),
                          start=False, stop=True, skip_group_check=True).then_inc(L.shifted, 1)

            def turn(L, b, g):
                u = b.n * NG + g
                pe.wait_ge(L.exped, u + 1)
                if not isinstance(u, int) or u >= 1:
                    pe.wait_ge(L.turned_ev, u)
                for j in range(GH):
                    t = pe.transpose(bank[3][:, 128 * j:128 * j + 128], prob[g % 2][:, j, :], ident[:])
                t.then_inc(L.turned, 1)

            def weigh(L, b, g):
                u = b.n * NG + g
                pe.wait_ge(L.turned_ev, u + 1)
                if g == 0:
                    pe.wait_ge(L.v_ready, b.n + 1)
                    if not isinstance(b.n, int) or b.n >= 2:
                        pe.wait_ge(L.pv_ev, b.n - 1)
                for j in range(GH):
                    m = pe.matmul(bank[4 + b.par][32 * j:32 * j + 16, 128 * g:128 * g + 128],
                                  vmix[b.par][:, GH * g + j, :, :].rearrange("p e f -> p (e f)"),
                                  prob_t[g % 2][:, j, :], start=True, stop=True)
                m.then_inc(L.pv, 1)

            def to_tokens(L, b, steps, read):
                pe.wait_ge(L.pv_ev, b.n + 1)
                if not isinstance(b.n, int) or b.n >= 1:
                    pe.wait_ge(L.tail, b.n * steps - steps + read)
                for g in range(NG):
                    t = pe.transpose(bank[7][:, 128 * g:128 * g + 128], pvs[:, g, :], ident[:])
                t.then_inc(L.o_tok, 1)

            def turn_out(L, b):
                pe.wait_ge(L.normed, b.n + 1)
                pe.transpose(bank[7][:, 0:128], attn_o[:], ident[:]).then_inc(L.o_t, 1)

            def out_product(L, b, w):
                pe.wait_ge(L.o_t_ev, b.n + 1)
                pe.matmul(bank[7][:, 128:256], attn_ot[:], w, start=True, stop=True).then_inc(L.o_out, 1)

            def pair(L, p, decayed, w, steps):
                for par in range(2):
                    bb = Batch(p, par)
                    for g in range(NG):
                        if g == 0 and bb.live:
                            project(L, bb, decayed)
                        b = bb.back(1)
                        if b.live:
                            score(L, b, g, decayed)
                        for lag, stage in ((1, subtract_max), (2, turn), (3, weigh)):
                            ub, ug = unit_back(b, g, lag)
                            if ub.live:
                                stage(L, ub, ug)
                        if g == 3 and bb.back(2).live:
                            to_tokens(L, bb.back(2), steps, 1)
                        if g == 0 and bb.back(3).live:
                            turn_out(L, bb.back(3))
                        if g == 1 and bb.back(3).live:
                            out_product(L, bb.back(3), w)

            def attention(L, decayed, w, steps):
                pair(L, 0, decayed, w, steps)
                pair(L, 1, decayed, w, steps)
                with pe.Fori(2, 8) as p:
                    pair(L, p, decayed, w, steps)
                pair(L, 8, decayed, w, steps)
                pair(L, 9, decayed, w, steps)

            pe.wait_ge(dve_set, DV_END)
            pe.wait_ge(act_set, 8)
            attention(L1, True, wo_t[:], TAIL1)

            pe.wait_ge(L1.tail, NB * TAIL1)
            for c in range(4):
                for j in range(4):
                    t = pe.transpose(bank[c][:, 128 * j:128 * j + 128], x1[:, 4 * c + j, :], ident[:])
                t.then_inc(turn1, 1)
            pe.wait_ge(turn1_ev, 4)
            attention(L2, False, xw_t[:, 3, :], TAIL2)

            pe.wait_ge(L2.tail, NB * TAIL2)
            for c in range(4):
                for j in range(4):
                    t = pe.transpose(bank[c][:, 128 * j:128 * j + 128], x2[:, 4 * c + j, :], ident[:])
                t.then_inc(turn2, 1)
            pe.wait_ge(turn2_ev, 4)
            for b in range(NB):
                m = pe.matmul(bank[7][:, NE * b:NE * b + NE], x_t[:, 128 * b:128 * b + 128], gate_t[:],
                              start=True, stop=True)
            m.then_inc(route_mm, 1)
            pe.wait_ge(route, RT_S3)
            for c in range(4):
                for j in range(4):
                    t = pe.transpose(bank[c][0:48, 64 * j:64 * j + 64].bitcast(BF16),
                                     s3[:, 4 * c + j, :, :].rearrange("p a e -> p (a e)"), ident_bf[:])
                t.then_inc(route_t, 1)
            pe.wait_ge(route_ev, 5)
            pe.wait_ge(in_ffn, 4 * 16)

            def up(c, kk):
                u = c * KC + kk
                late = not isinstance(u, int) or u >= 2
                xt = x_t[:, bass.ds(c * TC, TC)]
                if late:
                    pe.wait_ge(silu, u - 1)
                pe.matmul(bank[kk % 2][:], w1[:, 128 * kk:128 * kk + 128], xt, start=True, stop=True
                          ).then_inc(gate_mm, 1)
                if late:
                    pe.wait_ge(glu, u - 1)
                pe.matmul(bank[2 + kk % 2][:], w3[:, 128 * kk:128 * kk + 128], xt, start=True, stop=True)
                if late:
                    pe.wait_ge(glu_s, u - 1)
                pe.matmul(bank[4 + kk % 2][:], sel[:, kk, :], st[:, bass.ds(c * TC, TC)], start=True, stop=True
                          ).then_inc(up_mm, 1)

            def down_product(c, kk):
                u = c * KC + kk
                pe.wait_ge(glu_s, u + 1)
                if kk == 0 and (not isinstance(c, int) or c >= 1):
                    pe.wait_ge(ftail, c * FT - FT + 1)
                for t in range(4):
                    m = pe.matmul(bank[6][:, 128 * t:128 * t + 128], actt[kk % 2][:, 128 * t:128 * t + 128],
                                  w2[:, kk, :], start=(kk == 0 and t == 0), stop=(kk == KC - 1),
                                  skip_group_check=True)
                m.then_inc(down, 1)

            def chunk(c):
                for kk in range(KC):
                    up(c, kk)
                    if kk >= 1:
                        down_product(c, kk - 1)
                    elif not isinstance(c, int) or c >= 1:
                        down_product(c - 1, KC - 1)

            chunk(0)
            with pe.Fori(1, NCH) as c:
                chunk(c)
            down_product(NCH - 1, KC - 1)

        @block.scalar
        def _(act):
            for c in range(4):
                act.wait_ge(pe_set, PE_X + c + 1)
                act.copy(x_t[:, 512 * c:512 * c + 512], bank[4 + c][:]).then_inc(act_set, 1)
            for c in range(4):
                act.wait_ge(pe_set, PE_C + c + 1)
                act.copy(c_t[:, 512 * c:512 * c + 512], bank[4 + c][:]).then_inc(act_set, 1)
            act.wait_ge(dve_set, DV_WALL + NB)
            act.activation(ph_t[:, 0], vsz[:, :, 2 * D:2 * D + H], ACT.Tanh, scale=0.5).then_inc(gate_step, 1)
            act.activation(ph_t[:, 1], vsz[:, :, 2 * D + H:VSZ], ACT.Tanh).then_inc(gate_step, 1)
            act.wait_ge(gate_step, 2)
            act.activation(ph_t[:, 3], ph_t[:, 1], ACT.Abs, scale=math.pi / 2).then_inc(gate_step, 1)
            act.activation(ph_t[:, 2], ph_t[:, 1], ACT.Sin, scale=math.pi / 2).then_inc(gate_step, 1)
            act.wait_ge(gate_step, 4)
            act.activation(ph_t[:, 4], ph_t[:, 3], ACT.Sin, scale=-1.0, bias=half_pi[:, 0:1]).then_inc(gate_step, 1)

            def take_projection(L, b, decayed):
                act.wait_ge(L.proj_done, b.n + 1)
                if decayed:
                    if not isinstance(b.n, int) or b.n >= 1:
                        act.wait_ge(L.qk_ready, b.n)
                    for i in range(4):
                        act.activation(proj[:, i // 2, i % 2, :], bank[6][:, 128 * i:128 * i + 128], ACT.Identity,
                                       bias=bias_t[:, i:i + 1]).then_inc(L.proj_ev, 1)
                else:
                    if isinstance(b.n, int) and b.n < 2:
                        act.wait_ge(L1.scores, NG * NB)
                    else:
                        act.wait_ge(L.scores, NG * b.n - NG)
                    act.activation(qk[b.par][:, 0, 0, 0, :], bank[6][:, 0:128], ACT.Identity,
                                   bias=bias_xq[:, 0:1], scale=SCALE).then_inc(L.proj_ev, 1)
                    act.activation(qk[b.par][:, 1, 0, 0, :], bank[6][:, 128:256], ACT.Identity,
                                   bias=bias_t[:, 5:6]).then_inc(L.proj_ev, 1)

            def exponent(L, b, g):
                u = b.n * NG + g
                act.wait_ge(L.shifted, u + 1)
                if not isinstance(u, int) or u >= 2:
                    act.wait_ge(L.turned, u - 1)
                act.activation(prob[g % 2][:].rearrange("p h t -> p (h t)"), bank[g % 2][:], ACT.Exp
                               ).then_inc(L.exped, 1)

            def take_turned(L, b, g):
                u = b.n * NG + g
                act.wait_ge(L.turned, u + 1)
                if not isinstance(u, int) or u >= 2:
                    act.wait_ge(L.pv, u - 1)
                act.copy(prob_t[g % 2][:].rearrange("p h t -> p (h t)"), bank[3][:]).then_inc(L.turned_ev, 1)

            def take_pv(L, b):
                act.wait_ge(L.pv, b.n * NG + NG)
                if not isinstance(b.n, int) or b.n >= 1:
                    act.wait_ge(L.o_tok, b.n)
                act.copy(pvs[:].rearrange("p g t -> p (g t)"), bank[4 + b.par][:]).then_inc(L.pv_ev, 1)

            def take_out(L, b):
                act.wait_ge(L.o_t, b.n + 1)
                if not isinstance(b.n, int) or b.n >= 1:
                    act.wait_ge(L.o_out, b.n)
                act.copy(attn_ot[:], bank[7][:, 0:128]).then_inc(L.o_t_ev, 1)

            def pair(L, p, decayed):
                for par in range(2):
                    bb = Batch(p, par)
                    for g in range(NG):
                        if g == 0 and bb.live:
                            take_projection(L, bb, decayed)
                        b = bb.back(1)
                        for lag, stage in ((1, exponent), (2, take_turned)):
                            ub, ug = unit_back(b, g, lag)
                            if ub.live:
                                stage(L, ub, ug)
                        if g == 2 and bb.back(2).live:
                            take_pv(L, bb.back(2))
                        if g == 0 and bb.back(3).live:
                            take_out(L, bb.back(3))

            def attention(L, decayed):
                pair(L, 0, decayed)
                pair(L, 1, decayed)
                with act.Fori(2, 8) as p:
                    pair(L, p, decayed)
                pair(L, 8, decayed)
                pair(L, 9, decayed)

            act.wait_ge(dve_set, DV_END)
            attention(L1, True)
            for c in range(4):
                act.wait_ge(turn1, c + 1)
                act.copy(x_t[:, 512 * c:512 * c + 512], bank[c][:]).then_inc(turn1_ev, 1)
            attention(L2, False)
            for c in range(4):
                act.wait_ge(turn2, c + 1)
                act.copy(x_t[:, 512 * c:512 * c + 512], bank[c][:]).then_inc(turn2_ev, 1)
            act.wait_ge(route, 2)
            act.activation(rt[:, 1], rt[:, 0], ACT.Exp).then_inc(route_exp, 1)
            for c in range(4):
                act.wait_ge(route_t, c + 1)
                act.copy(st[0:48, 512 * c:512 * c + 512], bank[c][0:48, 0:256].bitcast(BF16)).then_inc(route_ev, 1)

            def gate(c, kk):
                u = c * KC + kk
                act.wait_ge(gate_mm, u + 1)
                if not isinstance(u, int) or u >= 2:
                    act.wait_ge(glu, u - 1)
                act.activation(sg[kk % 2], bank[kk % 2][:], ACT.Silu).then_inc(silu, 1)

            for kk in range(KC):
                gate(0, kk)
            with act.Fori(1, NCH) as c:
                for kk in range(KC):
                    gate(c, kk)

        @block.vector
        def _(dve):
            made = [0]

            def step(ins):
                made[0] += 1
                ins.then_inc(dve_set, 1)
                return made[0]

            def after(n):
                dve.wait_ge(dve_set, n)

            dve.wait_ge(in_const, 16)
            dve.wait_ge(in_feat, 2 * 16)
            step(dve.tensor_scalar(neg_ident[:], ident[:], -1.0, None, ALU.mult))
            step(dve.tensor_copy(ident_bf[:], ident[:]))
            step(dve.tensor_copy(upper[:], upper_f[:]))
            dve.wait_ge(in_w, 10 * 16)
            dve.wait_ge(in_small, (8 + 3 + 3 + 2) * 16)
            n = step(dve.tensor_tensor(mix_bd_n[:], mix_n[:].unsqueeze(1).broadcast_to([128, H, HD]),
                                       head_mask[:].unsqueeze(2).broadcast_to([128, H, HD]), ALU.mult))
            assert n == DV_MIX
            for p in range(2):
                n = step(dve.memset(kbd[p][:], 0.0))
            assert n == DV_KBD0
            step(dve.memset(half_pi[:], math.pi / 2))
            step(dve.memset(st[:], 0.0))
            dve.wait_ge(pe_set, 1)
            for i in range(4):
                step(dve.tensor_copy(wqk1[:, i // 2, :, i % 2, :],
                                     bank[0][:, 128 * i:128 * i + 128].rearrange("p (h f) -> p h f", f=HD)))
            dve.wait_ge(pe_set, 2)
            step(dve.tensor_copy(wall[:, 0:D], bank[1][:, 0:128]))
            step(dve.tensor_copy(wo_t[:], bank[1][:, 128:256]))
            step(dve.tensor_copy(xw_t[:, 0:2, :].rearrange("p a n -> p (a n)"), bank[1][:, 256:512]))
            dve.wait_ge(pe_set, 3)
            step(dve.tensor_copy(xw_t[:, 2:4, :].rearrange("p a n -> p (a n)"), bank[2][:, 0:256]))
            step(dve.tensor_copy(wall[:, 2 * D:VSZ], bank[2][:, 256:288]))
            step(dve.tensor_copy(gate_t[:], bank[2][:, 288:304]))
            n = step(dve.tensor_copy(bias_t[:, 0:7], bank[2][:, 304:311]))
            step(dve.memset(bv_cols[:], 1.0))
            after(n + 1)
            step(dve.tensor_scalar(bias_xq[:], bias_t[:, 4:5], SCALE, None, ALU.mult))
            n = step(dve.tensor_scalar(bv_cols[:], bv_cols[:], bias_t[:, 6:7], None, ALU.mult))
            dve.wait_ge(pe_set, 4)
            n = step(dve.tensor_copy(mix_bd[:], bank[3][:, 0:128]))
            assert n == DV_SUP
            dve.wait_ge(in_rows, 9 * 16)
            step(dve.tensor_copy(row_bias[:, 0:D], row_in[:, 0:D]))
            step(dve.tensor_copy(row_bias[:, 2 * D:VSZ], row_in[:, 2 * D:VSZ]))
            dve.wait_ge(pe_set, PE_SUP + 1)
            step(dve.tensor_copy(wall[:, D:2 * D], bank[0][:, 0:128]))
            n = step(dve.tensor_tensor(row_bias[:, D:2 * D], bank[0][:, 128:256], row_in[:, D:2 * D], ALU.add))
            assert n == DV_WALL
            after(n)
            for b in range(NB):
                dve.wait_ge(pe_set, PE_VSZ + b + 1)
                step(dve.tensor_tensor(vsz[:, b, :], bank[b % 4][:, 0:VSZ], row_bias[:], ALU.add))
            for c in range(4):
                dve.wait_ge(pe_set, PE_V2 + c + 1)
                n = step(dve.tensor_tensor(v2_all[:, 4 * c:4 * c + 4, :],
                                       bank[4 + c][:].rearrange("p (b n) -> p b n", b=4),
                                       bv2[:].unsqueeze(1).broadcast_to([128, 4, D]), ALU.add))
            after(n)
            for p in range(2):
                n = step(dve.memset(bank[4 + p][:], 0.0))
            assert n == DV_END
            dve.wait_ge(gate_step, 5)
            dve.tensor_scalar(ph_t[:, 5], ph_t[:, 0], SUP / 2, SUP / 2, ALU.mult, ALU.add).then_inc(gate_step, 1)
            dve.tensor_tensor(ph_t[:, 3], ph_t[:, 2], ph_t[:, 2], ALU.mult).then_inc(gate_step, 1)
            dve.wait_ge(gate_step, 7)
            dve.tensor_tensor(ph_t[:, 4], ph_t[:, 2], ph_t[:, 4], ALU.mult).then_inc(gate_step, 1)
            dve.tensor_scalar(ph_t[:, 3], ph_t[:, 3], -2.0, 1.0, ALU.mult, ALU.add).then_inc(gate_step, 1)
            dve.wait_ge(gate_step, 9)
            dve.tensor_tensor(ph_t[:, 1], ph_t[:, 4], ph_t[:, 5], ALU.mult).then_inc(gate_step, 1)
            dve.tensor_tensor(coef[:, 0], ph_t[:, 3], ph_t[:, 5], ALU.mult).then_inc(gate_step, 1)
            dve.wait_ge(gate_step, 11)
            dve.tensor_scalar(coef[:, 1], ph_t[:, 1], 2.0, None, ALU.mult).then_inc(gate_step, 1)

            def carry():
                dve.memset(waiter[:], 0.0)

            def pick(L, b, g):
                u = b.n * NG + g
                dve.wait_ge(L.scores, u + 1)
                carry()
                dve.copy_predicated(bank[g % 2][:].rearrange("p (h t) -> p h t", h=GH),
                                    upper[:].unsqueeze(1).broadcast_to([128, GH, S]),
                                    bank[2][:].rearrange("p (h t) -> p h t", h=GH)).then_inc(L.picked, 1)

            def maximum(L, b, g, decayed):
                u = b.n * NG + g
                if decayed:
                    dve.wait_ge(L.picked, u + 1)
                else:
                    dve.wait_ge(L.scores, u + 1)
                if not isinstance(u, int) or u >= 2:
                    dve.wait_ge(L.shifted, u - 1)
                with nc.allow_low_precision(reason="the shift cancels"):
                    dve.tensor_reduce(shift[:, g % 2, :], bank[g % 2][:].rearrange("p (h t) -> p h t", h=GH),
                                      AX.X, ALU.max).then_inc(L.maxed, 1)

            def divide(L, b):
                dve.wait_ge(L.o_tok, b.n + 1)
                o = bank[7][:].rearrange("p (h r) -> p h r", r=32)
                dve.reciprocal(rden[:], o[:, :, HD:HD + 1].rearrange("p h r -> p (h r)")).then_inc(L.norm_step, 1)
                dve.wait_ge(L.norm_step, b.n + 1)
                if not isinstance(b.n, int) or b.n >= 1:
                    dve.wait_ge(L.o_t, b.n)
                dve.tensor_tensor(attn_o[:].rearrange("p (h f) -> p h f", f=HD), o[:, :, 0:HD],
                                  rden[:].unsqueeze(2).broadcast_to([128, H, HD]), ALU.mult).then_inc(L.normed, 1)

            def moments(L, b, which, src, steps, first):
                dve.wait_ge(L.tail, b.n * steps + first)
                dve.bn_stats(stats[:, which, :], src).then_inc(L.tail, 1)
                dve.wait_ge(L.tail, b.n * steps + first + 1)
                carry()
                dve.bn_aggr(mv[:, which, :], stats[:, which, :]).then_inc(L.tail, 1)
                dve.wait_ge(L.tail, b.n * steps + first + 2)
                dve.tensor_scalar(veps[:, which:which + 1], mv[:, which, 1:2], EPS, None, ALU.add
                                  ).then_inc(L.tail, 1)

            def residual(L, b, steps):
                dve.wait_ge(L.o_out, b.n + 1)
                if not isinstance(b.n, int) or b.n >= 1:
                    dve.wait_ge(L.tail, b.n * steps)
                dve.tensor_tensor(res[:], bank[7][:, 128:256],
                                  xb_all[:, bass.ds(b.n, 1), :].rearrange("p b n -> p (b n)"),
                                  ALU.add).then_inc(L.tail, 1)
                moments(L, b, 0, res[:], steps, 1)

            def norm_out(L, b, which, src, dst, steps, need):
                dve.wait_ge(L.rstd, need)
                dve.tensor_scalar(dst[:, bass.ds(b.n, 1), :].rearrange("p b n -> p (b n)"), src,
                                  mv[:, which, 0:1], rstd[:, which:which + 1],
                                  ALU.subtract, ALU.mult).then_inc(L.tail, 1)

            def inner(b):
                L, t = L1, TAIL1
                dve.wait_ge(L.rstd, b.n * 2 + 1)
                dve.tensor_scalar(res[:], res[:], mv[:, 0, 0:1], rstd[:, 0:1], ALU.subtract, ALU.mult
                                  ).then_inc(L.tail, 1)
                dve.wait_ge(L.tail, b.n * t + 5)
                dve.tensor_tensor(res2[:], res[:], ln_g[:], ALU.mult).then_inc(inner_g, 1)
                dve.wait_ge(inner_g, b.n + 1)
                dve.tensor_tensor(res2[:], res2[:], xl_all[:, bass.ds(b.n, 1), :].rearrange("p b n -> p (b n)"),
                                  ALU.add).then_inc(L.tail, 1)
                moments(L, b, 1, res2[:], t, 6)

            def pair1(p):
                for par in range(2):
                    bb = Batch(p, par)
                    for g in range(NG):
                        b = bb.back(1)
                        if b.live:
                            pick(L1, b, g)
                            maximum(L1, b, g, True)
                        if g == 3 and bb.back(2).live:
                            divide(L1, bb.back(2))
                        if g == 2 and bb.back(3).live:
                            residual(L1, bb.back(3), TAIL1)
                        if g == 3 and bb.back(3).live:
                            inner(bb.back(3))
                        if g == 0 and bb.back(4).live:
                            c = bb.back(4)
                            norm_out(L1, c, 1, res2[:], x1, TAIL1, c.n * 2 + 2)

            def pair2(p):
                for par in range(2):
                    bb = Batch(p, par)
                    for g in range(NG):
                        b = bb.back(1)
                        if b.live:
                            maximum(L2, b, g, False)
                        if g == 3 and bb.back(2).live:
                            divide(L2, bb.back(2))
                        if g == 2 and bb.back(3).live:
                            residual(L2, bb.back(3), TAIL2)
                        if g == 3 and bb.back(3).live:
                            c = bb.back(3)
                            norm_out(L2, c, 0, res[:], x2, TAIL2, c.n + 1)

            dve.wait_ge(pool_set, 2)
            pair1(0)
            pair1(1)
            with dve.Fori(2, 8) as p:
                pair1(p)
            pair1(8)
            pair1(9)
            dve.wait_ge(xb2, 1)
            pair2(0)
            pair2(1)
            with dve.Fori(2, 8) as p:
                pair2(p)
            pair2(8)
            pair2(9)

            done = [0]

            def rstep(ins):
                done[0] += 1
                ins.then_inc(route, 1)
                dve.wait_ge(route, done[0])

            logits = bank[7][:, 0:NB * NE].rearrange("p (b e) -> p b e", e=NE)

            def by_expert(t):
                return t.unsqueeze(2).broadcast_to([128, NB, NE])

            dve.wait_ge(route_mm, 1)
            rstep(dve.tensor_reduce(rsm[:, 0], logits, AX.X, ALU.max))
            rstep(dve.tensor_tensor(rt[:, 0], logits, by_expert(rsm[:, 0]), ALU.subtract))
            dve.wait_ge(route_exp, 1)
            for b in range(NB):
                last = dve.max(r8[:, b, :], rt[:, 1, b, :])
            rstep(last)
            fourth = r8[:, :, TOPK - 1:TOPK].broadcast_to([128, NB, NE])
            rstep(dve.tensor_tensor(rt[:, 2], rt[:, 1], fourth, ALU.is_gt))
            rstep(dve.tensor_tensor(rt[:, 3], rt[:, 1], fourth, ALU.is_equal))
            rstep(dve.tensor_reduce(rsm[:, 1], rt[:, 2], AX.X, ALU.add))
            rstep(dve.tensor_scalar(rsm[:, 2], rsm[:, 1], -1.0, float(TOPK), ALU.mult, ALU.add))
            src = 3
            for sh, dst in ((1, 4), (2, 5), (4, 4), (8, 5)):
                rstep(dve.tensor_copy(rt[:, dst, :, 0:sh], rt[:, src, :, 0:sh]))
                rstep(dve.tensor_tensor(rt[:, dst, :, sh:NE], rt[:, src, :, sh:NE], rt[:, src, :, 0:NE - sh],
                                        ALU.add))
                src = dst
            rstep(dve.tensor_tensor(rt[:, 6], rt[:, src], by_expert(rsm[:, 2]), ALU.is_le))
            rstep(dve.tensor_tensor(rt[:, 6], rt[:, 6], rt[:, 3], ALU.mult))
            rstep(dve.tensor_tensor(rt[:, 6], rt[:, 6], rt[:, 2], ALU.add))
            rstep(dve.tensor_tensor(rt[:, 6], rt[:, 6], rt[:, 1], ALU.mult))
            rstep(dve.tensor_reduce(rsm[:, 3], rt[:, 6], AX.X, ALU.add))
            rstep(dve.reciprocal(rsm[:, 3], rsm[:, 3]))
            rstep(dve.tensor_tensor(rt[:, 7], rt[:, 6], by_expert(rsm[:, 3]), ALU.mult))
            rstep(dve.tensor_copy(s3[:, :, 0, :], rt[:, 7]))
            rstep(dve.tensor_tensor(rt[:, 0], rt[:, 7], s3[:, :, 0, :], ALU.subtract))
            rstep(dve.tensor_copy(s3[:, :, 1, :], rt[:, 0]))
            rstep(dve.tensor_tensor(rt[:, 1], rt[:, 0], s3[:, :, 1, :], ALU.subtract))
            rstep(dve.tensor_copy(s3[:, :, 2, :], rt[:, 1]))
            assert done[0] == RT_S3, done[0]
            dve.wait_ge(in_ffn, 4 * 16)
            dve.tensor_copy(sel[:], sel_f[:]).then_inc(route_ev, 1)

            def glu_step(c, kk):
                u = c * KC + kk
                dve.wait_ge(up_mm, u + 1)
                dve.wait_ge(silu, u + 1)
                dve.tensor_tensor(h1[kk % 2], bank[2 + kk % 2][:], sg[kk % 2], ALU.mult).then_inc(glu, 1)
                dve.wait_ge(glu, u + 1)
                if not isinstance(u, int) or u >= 2:
                    dve.wait_ge(down, u - 1)
                dve.tensor_tensor(actt[kk % 2], bank[4 + kk % 2][:], h1[kk % 2], ALU.mult).then_inc(glu_s, 1)

            def finish(c, part):
                at = c * FT
                if part == 0:
                    dve.wait_ge(down, c * KC + KC)
                    dve.tensor_tensor(fres[:], bank[6][:].rearrange("p (b n) -> p b n", b=4),
                                      x2[:, bass.ds(c * 4, 4), :], ALU.add).then_inc(ftail, 1)
                    dve.wait_ge(ftail, at + 1)
                    for t in range(4):
                        dve.bn_stats(fstats[:, t, :], fres[:, t, :]).then_inc(fst, 1)
                    dve.wait_ge(fst, c * 4 + 4)
                    carry()
                    for t in range(4):
                        dve.bn_aggr(fmv[:, t, :], fstats[:, t, :]).then_inc(ftail, 1)
                    dve.wait_ge(ftail, at + 5)
                    dve.tensor_scalar(fveps[:], fmv[:, :, 1], EPS, None, ALU.add).then_inc(ftail, 1)
                else:
                    dve.wait_ge(frs, c + 1)
                    if not isinstance(c, int) or c >= 1:
                        dve.wait_ge(stored, c * 16)
                    for t in range(4):
                        dve.tensor_scalar(fout[:, t, :], fres[:, t, :], fmv[:, t, 0:1], frstd[:, t:t + 1],
                                          ALU.subtract, ALU.mult).then_inc(ftail, 1)

            def chunk(c):
                for kk in range(KC):
                    glu_step(c, kk)
                    if kk in (1, 3) and (not isinstance(c, int) or c >= 1):
                        finish(c - 1, kk // 2)
            chunk(0)
            with dve.Fori(1, NCH) as c:
                chunk(c)
            finish(NCH - 1, 0)
            finish(NCH - 1, 1)


_OUTS = [((NB, S, D), "float32")]


def kernel(**inputs):
    import numpy as _np
    import concourse.bacc as _bacc
    from concourse import mybir as _mybir
    from concourse.bass_utils import run_bass_kernel_spmd as _run

    pos = _np.arange(S, dtype=_np.float64) - (S - 1) / 2
    feat = _np.ones((128, 2, 2, 2, S))
    plain = (_np.arange(128) % (2 * HD)) < HD
    for side, sign in ((0, -1.0), (1, 1.0)):
        for tri, way in ((0, 1.0), (1, -1.0)):
            grow = _np.exp(sign * way * DECAY * pos)
            feat[:, side, tri, :, :] = _np.where(plain[:, None, None], 1.0, grow * (ENT if side == 0 else 1.0))
    feat[:, 0] *= SCALE
    p = _np.arange(128)
    sel = _np.zeros((128, KC, 128))
    for c in range(KC):
        for e in range(2):
            for part in range(3):
                sel[NE * part + 2 * c + e, c, INTER * e:INTER * e + INTER] = 1.0
    consts = {
        "ident": _np.eye(128),
        "feat": feat.reshape(128, -1),
        "upper": (p[None, :] > p[:, None]),
        "head_mask": (p[:, None] // HD == _np.arange(H)[None, :]),
        "sel": sel.reshape(128, -1),
    }
    nc = _bacc.Bacc("TRN2", target_bir_lowering=False, num_devices=1)
    arrays, args, kargs = {}, {}, {}
    for name in inputs:
        v = _np.ascontiguousarray(inputs[name])
        arrays[f"in_{name}_dram"] = v
        args[name] = nc.dram_tensor(f"in_{name}_dram", v.shape, _mybir.dt.from_np(v.dtype), kind="ExternalInput").ap()
    for name, v in consts.items():
        v = _np.ascontiguousarray(v.astype(_np.float32))
        arrays[f"const_{name}_dram"] = v
        kargs[name] = nc.dram_tensor(f"const_{name}_dram", v.shape, _mybir.dt.from_np(v.dtype), kind="ExternalInput").ap()
    outs = []
    for i, (shape, dtype) in enumerate(_OUTS):
        outs.append(nc.dram_tensor(f"out_{i}_dram", shape, _mybir.dt.from_np(_np.dtype(dtype)), kind="ExternalOutput").ap())
    build(nc, args, kargs, outs[0])
    r = _run(nc, [arrays], core_ids=[0])
    return r.results[0]["out_0_dram"]
```

```python
import math
from contextlib import ExitStack

import concourse.bass as bass
from concourse import mybir

F32 = mybir.dt.float32
BF16 = mybir.dt.bfloat16
U8 = mybir.dt.uint8
ACT = mybir.ActivationFunctionType
ALU = mybir.AluOpType
AX = mybir.AxisListType

NB = 16
S = 128
D = 128
H = 16
HD = D // H
NE = 16
INTER = 64
TOPK = 4
EPS = 1e-5
SCALE = 1.0 / math.sqrt(HD)
ENT = 0.5
DECAY = 0.1
SUP = 0.3
GH = 4
NG = H // GH
Q_PART = (0, 0, 0, 1, 1, 2)
K_PART = (0, 1, 2, 0, 1, 0)
NP = len(Q_PART)
R1 = NP * 2 * HD
R2 = NP * HD
KC = NE * INTER // 128
TC = 512
NCH = NB * S // TC
WQ, WEQ, WK, WEK, WV, WO, XQ, XK, XV, XO = range(10)
VSZ = 2 * D + 2 * H


class Batch:

    def __init__(self, pair, par):
        self.pair, self.par = pair, par
        self.n = pair * 2 + par

    def back(self, lag):
        p = self.par - lag
        return Batch(self.pair + p // 2, p % 2)

    @property
    def live(self):
        return not isinstance(self.n, int) or 0 <= self.n < NB


def unit_back(b, g, lag):
    q = g - lag
    return b.back(-(q // NG)), q % NG


def build(nc, a, k, out):
    with ExitStack() as ctx:
        def sb(name, shape, dt=F32):
            return ctx.enter_context(nc.sbuf_tensor(name, shape, dt))

        def sem(name):
            return ctx.enter_context(nc.semaphore(name))

        ident = sb("ident", [128, 128])
        neg_ident = sb("neg_ident", [128, 128], BF16)
        ident_bf = sb("ident_bf", [128, 128], BF16)
        feat = sb("feat", [128, 2, 2, S])
        upper_f = sb("upper_f", [128, S])
        upper = sb("upper", [128, S], U8)
        head_mask = sb("head_mask", [128, H])
        sel_f = sb("sel_f", [128, KC, 128])
        sel = sb("sel", [128, KC, 128], BF16)
        wn = sb("wn", [128, 10, D])
        gates_n = sb("gates_n", [48, D])
        bias_rows = sb("bias_rows", [7, D])
        bias_perm = sb("bias_perm", [7, D])
        mix_n = sb("mix_n", [128, HD])
        mix_bd_n = sb("mix_bd_n", [128, H, HD])
        mix_bd = sb("mix_bd", [128, D])
        bv_cols = sb("bv_cols", [128, 128])
        wqk1 = sb("wqk1", [128, 2, 2, HD, H])
        wall = sb("wall", [128, VSZ])
        wo_t = sb("wo_t", [128, D])
        xw_t = sb("xw_t", [128, 4, D])
        gate_t = sb("gate_t", [128, NE])
        bias_t = sb("bias_t", [128, 8])
        bias_q = sb("bias_q", [128, 2])
        row_in = sb("row_in", [128, VSZ])
        row_bias = sb("row_bias", [128, VSZ])
        bo1 = sb("bo1", [128, D])
        ln_g = sb("ln_g", [128, D])
        ln_b = sb("ln_b", [128, D])
        bv2 = sb("bv2", [128, D])
        bo2 = sb("bo2", [128, D])
        x_tok = sb("x_tok", [128, NB, D])
        c_tok = sb("c_tok", [128, NB, D])
        x_t = sb("x_t", [128, NB * S])
        c_t = sb("c_t", [128, NB * S])
        xb_all = sb("xb_all", [128, NB, D])
        xl_all = sb("xl_all", [128, NB, D])
        vsz = sb("vsz", [128, NB, VSZ])
        v2_all = sb("v2_all", [128, NB, D])
        ph_t = sb("ph_t", [128, 6, NB, H])
        coef = sb("coef", [128, 2, NB, H])
        minus_half = sb("minus_half", [128, NB])
        waiter = sb("waiter", [128, 2])
        half_pi = sb("half_pi", [128, 1])
        w1 = sb("w1", [128, NE * INTER])
        w3 = sb("w3", [128, NE * INTER])
        w2 = sb("w2", [128, KC, D])
        pf = sb("pf", [128, 2, 3, S])
        rest = sb("rest", [128, 2, 3, S])
        parts = [sb(f"parts{p}", [128, 2, 3, 3, S], BF16) for p in range(2)]
        stk = [sb(f"stk{p}", [128, 2, H, 2, S], BF16) for p in range(2)]
        stk2 = [stk[p][:].rearrange("p a h u t -> p a (h u t)")[:, :, 0:H * S].rearrange("p a (h t) -> p a h t", t=S)
                for p in range(2)]
        scr1 = [nc.dram_tensor(f"parts1_{p}", (2, 3, 2, 128, 2, S), BF16, kind="Internal").ap() for p in range(2)]
        scr2 = [nc.dram_tensor(f"parts2_{p}", (2, 3, 128, S), BF16, kind="Internal").ap() for p in range(2)]
        vmix = [sb(f"vmix{p}", [128, H, 2, HD]) for p in range(2)]
        mixa = sb("mixa", [128, D])
        mixb = sb("mixb", [128, D])
        mixc = sb("mixc", [128, D])
        shift = sb("shift", [128, 2, GH], BF16)
        prob = [sb(f"prob{p}", [128, GH, S]) for p in range(2)]
        prob_t = [sb(f"prob_t{p}", [128, GH, S]) for p in range(2)]
        pvs = sb("pvs", [128, NG, S])
        rden = sb("rden", [128, H])
        attn_o = sb("attn_o", [128, D])
        attn_ot = sb("attn_ot", [128, D])
        res = sb("res", [128, D])
        res2 = sb("res2", [128, D])
        stats = sb("stats", [128, 2, 6])
        mv = sb("mv", [128, 2, 2])
        veps = sb("veps", [128, 2])
        rstd = sb("rstd", [128, 2])
        rt = vsz[:].rearrange("p b n -> p (b n)")[:, 0:8 * NB * NE].rearrange("p (a b e) -> p a b e", a=8, b=NB)
        r8 = sb("r8", [128, NB, 8])
        rsm = sb("rsm", [128, 4, NB])
        s3 = sb("s3", [128, NB, 3, NE], BF16)
        st = sb("st", [128, NB * S], BF16)
        scratch = stk[0][:].rearrange("p a h u t -> p (a h u t)").bitcast(F32)
        sg = [scratch[:, TC * p:TC * p + TC] for p in range(2)]
        h1 = [scratch[:, TC * (2 + p):TC * (3 + p)] for p in range(2)]
        actt = [scratch[:, TC * (4 + p):TC * (5 + p)] for p in range(2)]
        fres = sb("fres", [128, 4, D])
        fstats = sb("fstats", [128, 4, 6])
        fmv = sb("fmv", [128, 4, 2])
        fveps = sb("fveps", [128, 4])
        frstd = sb("frstd", [128, 4])
        fout = sb("fout", [128, 4, D])

        x1 = x_tok
        x2 = c_tok
        bank = [ctx.enter_context(nc.psum_tensor(f"bank{i}", [128, 512], F32)) for i in range(8)]

        in_const = sem("in_const")
        in_qk = sem("in_qk")
        in_w = sem("in_w")
        in_rows = sem("in_rows")
        in_bias = sem("in_bias")
        in_small = sem("in_small")
        in_x0 = sem("in_x0")
        in_feat = sem("in_feat")
        in_x = sem("in_x")
        in_c = sem("in_c")
        in_ffn = sem("in_ffn")
        pool_const = sem("pool_const")
        pe_set = sem("pe_set")
        dve_set = sem("dve_set")
        act_set = sem("act_set")
        gate_step = sem("gate_step")
        pool_set = sem("pool_set")
        stored = sem("stored")

        class Layer:

            def __init__(self, n, kinds, rows, spills):
                self.kinds = kinds
                self.rows = rows
                self.stack_step = 16 * 6
                self.spill_step = 16 * spills
                self.proj_done = sem(f"proj_done{n}")
                self.proj_ev = sem(f"proj_ev{n}")
                self.ent_ev = sem(f"ent_ev{n}")
                self.high = sem(f"high{n}")
                self.rest = sem(f"rest{n}")
                self.mid = sem(f"mid{n}")
                self.low = sem(f"low{n}")
                self.spilled = sem(f"spilled{n}")
                self.stacked = [sem(f"stacked{n}{p}") for p in range(2)]
                self.scores = sem(f"scores{n}")
                self.picked = sem(f"picked{n}")
                self.maxed = sem(f"maxed{n}")
                self.shifted = sem(f"shifted{n}")
                self.exped = sem(f"exped{n}")
                self.turned = sem(f"turned{n}")
                self.turned_ev = sem(f"turned_ev{n}")
                self.v_ready = sem(f"v_ready{n}")
                self.v_step = sem(f"v_step{n}")
                self.pv = sem(f"pv{n}")
                self.pv_ev = sem(f"pv_ev{n}")
                self.o_tok = sem(f"o_tok{n}")
                self.normed = sem(f"normed{n}")
                self.norm_step = sem(f"norm_step{n}")
                self.o_t = sem(f"o_t{n}")
                self.o_t_ev = sem(f"o_t_ev{n}")
                self.o_out = sem(f"o_out{n}")
                self.tail = sem(f"tail{n}")
                self.rstd = sem(f"rstd{n}")
        L1, L2 = Layer(1, slice(0, 3), R1, 3), Layer(2, slice(0, 1), R2, 1)
        rezeroed = sem("rezeroed")
        TAIL1, TAIL2 = 10, 5

        turn1 = sem("turn1")
        turn1_ev = sem("turn1_ev")
        xb2 = sem("xb2")
        turn2 = sem("turn2")
        turn2_ev = sem("turn2_ev")
        route_mm = sem("route_mm")
        route = sem("route")
        route_exp = sem("route_exp")
        route_t = sem("route_t")
        route_ev = sem("route_ev")
        gate_mm = sem("gate_mm")
        up_mm = sem("up_mm")
        silu = sem("silu")
        glu = sem("glu")
        glu_s = sem("glu_s")
        down = sem("down")
        ftail = sem("ftail")
        fst = sem("fst")
        inner_g = sem("inner_g")
        frs = sem("frs")
        FT = 10

        PE_QK, PE_BIAS, PE_W, PE_MIX, PE_SUP, PE_C, PE_VSZ = 1, 2, 5, 6, 10, 10, 14
        PE_V2 = PE_VSZ + NB
        PE_X = (3, 7, 8, 9)
        DV_STK0, DV_BIAS, DV_QK, DV_COLS, DV_MIX, DV_SUP, DV_WALL = 2, 5, 9, 13, 14, 27, 31
        DV_END = DV_WALL + NB + 6
        X_BANK, C_BANK, V_BANK = (4, 5, 7, 4), (5, 7, 4, 5), (7, 4, 5, 7)
        RT_S3 = 27
        block = ctx.enter_context(nc.Block())

        @block.sync
        def _(sp):
            sp.dma_start(ident[:], k["ident"]).then_inc(in_const, 16)
            def load_x(c, done):
                sp.dma_start(x_tok[:, 4 * c:4 * c + 4, :],
                             a["x"][4 * c:4 * c + 4].rearrange("b t d -> t b d")).then_inc(done, 16)

            names = ["L0_attn_Wq", "L0_attn_Weq", "L0_attn_Wk", "L0_attn_Wek", "L0_attn_Wv",
                     "L0_attn_Wo", "L0_xattn_Wq", "L0_xattn_Wk", "L0_xattn_Wv", "L0_xattn_Wo"]
            for i, n in enumerate(names):
                sp.dma_start(wn[:, i, :], a[n]).then_inc(in_qk if i < 4 else in_w, 16)
                if i == 3:
                    load_x(0, in_x0)
            for c in range(1, 4):
                load_x(c, in_x)
            for c in range(4):
                sp.dma_start(c_tok[:, 4 * c:4 * c + 4, :],
                             a["ctx_1024"][4 * c:4 * c + 4].rearrange("b t d -> t b d")).then_inc(in_c, 16)
            sp.dma_start(sel_f[:], k["sel"].rearrange("p (c m) -> p c m", c=KC)).then_inc(in_ffn, 16)
            sp.dma_start(w1[:].rearrange("p (e i) -> p e i", e=NE),
                         a["L0_ffn_w1"].rearrange("e h i -> h e i")).then_inc(in_ffn, 16)
            sp.dma_start(w3[:].rearrange("p (e i) -> p e i", e=NE),
                         a["L0_ffn_w3"].rearrange("e h i -> h e i")).then_inc(in_ffn, 16)
            sp.dma_start(w2[:], a["L0_ffn_w2"].rearrange("(c e) i h -> (e i) c h", e=2)).then_inc(in_ffn, 16)

            def spill(L, b):
                sp.wait_ge(L.low, b.n + 1)
                plain = parts[b.par][:, :, :, 0, :].rearrange("p a c t -> p (a c) t")
                if L is L1:
                    to = scr1[b.par].rearrange("a c k p u t -> k p (a c) u t")
                    for tri in range(2):
                        sp.dma_start(to[0, :, :, tri, :], plain).then_inc(L.spilled, 16)
                    sp.dma_start(to[1], parts[b.par][:, :, :, 1:3, :].rearrange("p a c u t -> p (a c) u t")
                                 ).then_inc(L.spilled, 16)
                else:
                    sp.dma_start(scr2[b.par].rearrange("a c p t -> p (a c) t"), plain).then_inc(L.spilled, 16)

            def stack(L, b):
                sp.wait_ge(L.spilled, (b.n + 1) * L.spill_step)
                if not isinstance(b.n, int) or b.n >= 2:
                    sp.wait_ge(L.scores, NG * b.n - NG)
                if L is L1:
                    src = scr1[b.par].rearrange("a c k (f h) u t -> a c (k f) (h u t)", h=H)
                    dst = stk[b.par][:].rearrange("p a h u t -> p a (h u t)")
                else:
                    src = scr2[b.par].rearrange("a c (f h) t -> a c f (h t)", h=H)
                    dst = stk2[b.par].rearrange("p a h t -> p a (h t)")
                n = L.rows // NP
                for at, reps in ((0, 3), (3, 2), (5, 1)):
                    part = Q_PART[at]
                    sp.dma_start(dst[at * n:(at + reps) * n, 0, :],
                                 src[0, part].unsqueeze(0).broadcast_to([reps, n, src.shape[3]])
                                 ).then_inc(L.stacked[b.par], 16)
                    sp.dma_start(dst[at * n:(at + reps) * n, 1, :], src[1, 0:reps]
                                 ).then_inc(L.stacked[b.par], 16)

            def attention(L):
                def pair(p):
                    for par in range(2):
                        spill(L, Batch(p, par))
                        stack(L, Batch(p, par))

                pair(0)
                with sp.Fori(1, NB // 2) as p:
                    pair(p)

            sp.wait_ge(dve_set, DV_STK0)
            attention(L1)
            sp.wait_ge(L1.scores, NG * NB)
            sp.wait_ge(rezeroed, 2)
            attention(L2)

            with sp.Fori(0, NCH) as c:
                sp.wait_ge(ftail, c * FT + FT)
                sp.dma_start(out[bass.ds(c * 4, 4)].rearrange("b t d -> t b d"), fout[:]).then_inc(stored, 16)
            sp.wait_ge(stored, 16 * NCH)

        @block.gpsimd
        def _(pool):
            def rows(dst, src):
                n = src.shape[0]
                pool.dma_start(dst, src.unsqueeze(0).broadcast_to([128, n])).then_inc(in_rows, 16)

            for r, n in enumerate(("L0_attn_bq", "L0_attn_beq", "L0_attn_bk", "L0_attn_bek", "L0_xattn_bq",
                                   "L0_xattn_bk", "L0_attn_bv")):
                pool.dma_start(bias_rows[r:r + 1, :], a[n].unsqueeze(0)).then_inc(in_bias, 16)
            rows(row_in[:, 0:D], a["L0_attn_bv"])
            rows(row_in[:, D:2 * D], a["L0_attn_mix_b"].rearrange("h o -> (h o)"))
            rows(row_in[:, 2 * D:2 * D + H], a["L0_attn_amp_b"])
            rows(row_in[:, 2 * D + H:VSZ], a["L0_attn_ph_b"])
            rows(bo1[:], a["L0_attn_bo"])
            rows(ln_g[:], a["L0_attn_ln_g"])
            rows(ln_b[:], a["L0_attn_ln_b"])
            rows(bv2[:], a["L0_xattn_bv"])
            rows(bo2[:], a["L0_xattn_bo"])
            pool.memset(minus_half[:], -0.5)
            for p in range(2):
                pool.memset(vmix[p][:, :, 1, :], 1.0)
            def remainder(L, b):
                pool.wait_ge(L.high, b.n + 1)
                if not isinstance(b.n, int) or b.n >= 1:
                    pool.wait_ge(L.low, b.n)
                pool.tensor_tensor(rest[:, :, L.kinds, :], pf[:, :, L.kinds, :], parts[b.par][:, :, 0, L.kinds, :],
                                   ALU.subtract).then_inc(L.rest, 1)

            def lowest(L, b):
                pool.wait_ge(L.mid, b.n + 1)
                if not isinstance(b.n, int) or b.n >= 2:
                    pool.wait_ge(L.stacked[b.par], b.pair * L.stack_step)
                with nc.allow_low_precision(reason="the third of three parts"):
                    pool.tensor_tensor(parts[b.par][:, :, 2, L.kinds, :], rest[:, :, L.kinds, :],
                                       parts[b.par][:, :, 1, L.kinds, :], ALU.subtract).then_inc(L.low, 1)

            def mix_values(b):
                if isinstance(b.n, int) and b.n == 0:
                    pool.wait_ge(gate_step, 12)
                if not isinstance(b.n, int) or b.n >= 2:
                    pool.wait_ge(L1.pv, NG * b.n - NG)
                row = vsz[:, bass.ds(b.n, 1), :].rearrange("p b n -> p (b n)")
                val = row[:, 0:D]
                sup = row[:, D:2 * D].rearrange("p (h f) -> p h f", f=HD)
                c1 = coef[:, 0, bass.ds(b.n, 1), :].rearrange("p b h -> p (b h)").unsqueeze(2)
                c2 = coef[:, 1, bass.ds(b.n, 1), :].rearrange("p b h -> p (b h)").unsqueeze(2)
                ma = mixa[:].rearrange("p (h f) -> p h f", f=HD)
                mb = mixb[:].rearrange("p (h f) -> p h f", f=HD)
                pool.tensor_tensor(ma, sup, c1.broadcast_to([128, H, HD]), ALU.mult).then_inc(L1.v_step, 1)
                pool.tensor_tensor(mb[:, :, 1:HD], sup[:, :, 0:HD - 1], c2.broadcast_to([128, H, HD - 1]),
                                   ALU.mult).then_inc(L1.v_step, 1)
                pool.tensor_tensor(mb[:, :, 0:1], sup[:, :, HD - 1:HD], c2, ALU.mult).then_inc(L1.v_step, 1)
                pool.wait_ge(L1.v_step, b.n * 4 + 3)
                pool.tensor_tensor(mixc[:], mixa[:], mixb[:], ALU.add).then_inc(L1.v_step, 1)
                pool.wait_ge(L1.v_step, b.n * 4 + 4)
                pool.tensor_tensor(vmix[b.par][:, :, 0, :], mixc[:].rearrange("p (h f) -> p h f", f=HD),
                                   val.rearrange("p (h f) -> p h f", f=HD), ALU.add).then_inc(L1.v_ready, 1)

            def power(L, b, which, step, per, steps):
                pool.wait_ge(L.tail, b.n * steps + step)
                pool.tensor_tensor(rstd[:, which:which + 1], veps[:, which:which + 1], minus_half[:, 0:1],
                                   ALU.pow).then_inc(L.rstd, 1)

            def pair1(p):
                for par in range(2):
                    b = Batch(p, par)
                    ahead = b.back(-2)
                    if ahead.live:
                        remainder(L1, ahead)
                    if b.back(3).live:
                        power(L1, b.back(3), 0, 4, 2, TAIL1)
                    if ahead.live:
                        lowest(L1, ahead)
                    if b.back(3).live:
                        power(L1, b.back(3), 1, 9, 2, TAIL1)
                    if b.live:
                        mix_values(b)

            pair1(-1)
            pool.wait_ge(in_rows, 9 * 16)
            pool.wait_ge(in_x0, 16)
            pool.wait_ge(in_x, 3 * 16)
            pool.tensor_tensor(xb_all[:], x_tok[:], bo1[:].unsqueeze(1).broadcast_to([128, NB, D]),
                               ALU.add).then_inc(pool_set, 1)
            pool.tensor_tensor(xl_all[:], x_tok[:], ln_b[:].unsqueeze(1).broadcast_to([128, NB, D]),
                               ALU.add).then_inc(pool_set, 1)
            pair1(0)
            pair1(1)
            with pool.Fori(2, 7) as p:
                pair1(p)
            pair1(7)
            pair1(8)
            pair1(9)

            pool.wait_ge(L1.tail, NB * TAIL1)
            pool.tensor_tensor(xb_all[:], x1[:], bo2[:].unsqueeze(1).broadcast_to([128, NB, D]),
                               ALU.add).then_inc(xb2, 1)

            def values2(b):
                if isinstance(b.n, int) and b.n < 2:
                    pool.wait_ge(L1.pv, NG * NB)
                else:
                    pool.wait_ge(L2.pv, NG * b.n - NG)
                pool.tensor_copy(vmix[b.par][:, :, 0, :],
                                 v2_all[:, bass.ds(b.n, 1), :].rearrange("p b (h f) -> p (b h) f", f=HD)
                                 ).then_inc(L2.v_ready, 1)

            def pair2(p):
                for par in range(2):
                    b = Batch(p, par)
                    ahead = b.back(-2)
                    if ahead.live:
                        remainder(L2, ahead)
                        lowest(L2, ahead)
                    if b.back(1).live:
                        values2(b.back(1))
                    if b.back(3).live:
                        power(L2, b.back(3), 0, 4, 1, TAIL2)

            pair2(-1)
            pair2(0)
            pair2(1)
            with pool.Fori(2, 7) as p:
                pair2(p)
            pair2(7)
            pair2(8)
            pair2(9)

            with pool.Fori(0, NCH) as c:
                pool.wait_ge(ftail, c * FT + 6)
                pool.tensor_tensor(frstd[:], fveps[:], minus_half[:, 0:4], ALU.pow).then_inc(frs, 1)

        @block.tensor
        def _(pe):
            def project(L, b, decayed):
                if not isinstance(b.n, int) or b.n >= 1:
                    pe.wait_ge(L.proj_ev, b.n * 2)
                    if decayed:
                        pe.wait_ge(L.ent_ev, b.n * 2)
                xt = x_t[:, bass.ds(b.n * S, S)]
                if decayed:
                    for side in range(2):
                        for ent in range(2):
                            m = pe.matmul(bank[6][:, 256 * side + 128 * ent:256 * side + 128 * ent + 128],
                                          wqk1[:, side, ent, :, :].rearrange("p f h -> p (f h)"),
                                          xt, start=True, stop=True)
                else:
                    pe.matmul(bank[6][:, 0:128], xw_t[:, 0, :], xt, start=True, stop=True)
                    m = pe.matmul(bank[6][:, 128:256], xw_t[:, 1, :], c_t[:, bass.ds(b.n * S, S)],
                                  start=True, stop=True)
                m.then_inc(L.proj_done, 1)

            def score(L, b, g, decayed):
                u = b.n * NG + g
                if g == 0:
                    pe.wait_ge(L.stacked[b.par], b.pair * L.stack_step + L.stack_step)
                if not isinstance(u, int) or u >= 2:
                    pe.wait_ge(L.exped, u - 1)
                ops = stk[b.par][:, :, :, 0, :] if decayed else stk2[b.par]
                for j in range(GH):
                    m = pe.matmul(bank[g % 2][:, 128 * j:128 * j + 128], ops[:, 0, GH * g + j, :],
                                  ops[:, 1, GH * g + j, :], start=(j == 0), stop=True,
                                  skip_group_check=True)
                if decayed:
                    if not isinstance(u, int) or u >= 1:
                        pe.wait_ge(L.picked, u)
                    for j in range(GH):
                        m = pe.matmul(bank[2][:, 128 * j:128 * j + 128], stk[b.par][:, 0, GH * g + j, 1, :],
                                      stk[b.par][:, 1, GH * g + j, 1, :], start=True, stop=True)
                m.then_inc(L.scores, 1)

            def subtract_max(L, b, g):
                u = b.n * NG + g
                pe.wait_ge(L.maxed, u + 1)
                pe.matmul(bank[g % 2][:].rearrange("p (h t) -> p h t", h=GH), neg_ident[:],
                          shift[:, g % 2, :].unsqueeze(2).broadcast_to([128, GH, S]),
                          start=False, stop=True, skip_group_check=True).then_inc(L.shifted, 1)

            def turn(L, b, g):
                u = b.n * NG + g
                pe.wait_ge(L.exped, u + 1)
                if not isinstance(u, int) or u >= 1:
                    pe.wait_ge(L.turned_ev, u)
                for j in range(GH):
                    t = pe.transpose(bank[3][:, 128 * j:128 * j + 128], prob[g % 2][:, j, :], ident[:])
                t.then_inc(L.turned, 1)

            def weigh(L, b, g):
                u = b.n * NG + g
                pe.wait_ge(L.turned_ev, u + 1)
                if g == 0:
                    pe.wait_ge(L.v_ready, b.n + 1)
                    if not isinstance(b.n, int) or b.n >= 2:
                        pe.wait_ge(L.pv_ev, b.n - 1)
                for j in range(GH):
                    m = pe.matmul(bank[4 + b.par][32 * j:32 * j + 16, 128 * g:128 * g + 128],
                                  vmix[b.par][:, GH * g + j, :, :].rearrange("p e f -> p (e f)"),
                                  prob_t[g % 2][:, j, :], start=True, stop=True)
                m.then_inc(L.pv, 1)

            def to_tokens(L, b, steps, read):
                pe.wait_ge(L.pv_ev, b.n + 1)
                if not isinstance(b.n, int) or b.n >= 1:
                    pe.wait_ge(L.tail, b.n * steps - steps + read)
                for g in range(NG):
                    t = pe.transpose(bank[7][:, 128 * g:128 * g + 128], pvs[:, g, :], ident[:])
                t.then_inc(L.o_tok, 1)

            def turn_out(L, b):
                pe.wait_ge(L.normed, b.n + 1)
                pe.transpose(bank[7][:, 0:128], attn_o[:], ident[:]).then_inc(L.o_t, 1)

            def out_product(L, b, w):
                pe.wait_ge(L.o_t_ev, b.n + 1)
                pe.matmul(bank[7][:, 128:256], attn_ot[:], w, start=True, stop=True).then_inc(L.o_out, 1)

            def pair(L, p, decayed, w, steps):
                for par in range(2):
                    bb = Batch(p, par)
                    for g in range(NG):
                        if g == 0 and bb.back(-2).live:
                            project(L, bb.back(-2), decayed)
                        b = bb.back(1)
                        if b.live:
                            score(L, b, g, decayed)
                        for lag, stage in ((1, subtract_max), (2, turn), (3, weigh)):
                            ub, ug = unit_back(b, g, lag)
                            if ub.live:
                                stage(L, ub, ug)
                        if g == 3 and bb.back(2).live:
                            to_tokens(L, bb.back(2), steps, 1)
                        if g == 0 and bb.back(3).live:
                            turn_out(L, bb.back(3))
                        if g == 1 and bb.back(3).live:
                            out_product(L, bb.back(3), w)

            def attention(L, decayed, w, steps):
                pair(L, 0, decayed, w, steps)
                pair(L, 1, decayed, w, steps)
                with pe.Fori(2, 7) as p:
                    pair(L, p, decayed, w, steps)
                pair(L, 7, decayed, w, steps)
                pair(L, 8, decayed, w, steps)
                pair(L, 9, decayed, w, steps)

            pe.wait_ge(in_const, 16)
            pe.wait_ge(in_qk, 4 * 16)
            for i, w in enumerate((WQ, WEQ, WK, WEK)):
                t = pe.transpose(bank[0][:, 128 * i:128 * i + 128], wn[:, w, :], ident[:])
            t.then_inc(pe_set, 1)
            pe.wait_ge(dve_set, DV_BIAS)
            pe.transpose(bank[3][:, 128:135], bias_perm[:], ident[0:7, 0:7])
            pe.transpose(bank[3][:, 135:142], bias_rows[:], ident[0:7, 0:7]).then_inc(pe_set, 1)

            def turn_x(c):
                for j in range(4):
                    t = pe.transpose(bank[X_BANK[c]][:, 128 * j:128 * j + 128], x_tok[:, 4 * c + j, :], ident[:])
                t.then_inc(pe_set, 1)

            pe.wait_ge(in_x0, 16)
            turn_x(0)
            pe.wait_ge(dve_set, DV_QK)
            pe.wait_ge(act_set, 1)
            project(L1, Batch(0, 0), True)
            pe.wait_ge(in_w, 6 * 16)
            pe.wait_ge(in_small, 5 * 16)
            for i, w in enumerate((WV, WO, XQ, XK)):
                t = pe.transpose(bank[1][:, 128 * i:128 * i + 128], wn[:, w, :], ident[:])
            t.then_inc(pe_set, 1)
            for i, w in enumerate((XV, XO)):
                pe.transpose(bank[2][:, 128 * i:128 * i + 128], wn[:, w, :], ident[:])
            pe.transpose(bank[2][:, 256:304], gates_n[:], ident[0:48, 0:48]).then_inc(pe_set, 1)
            project(L1, Batch(0, 1), True)
            pe.wait_ge(dve_set, DV_MIX)
            pe.transpose(bank[3][:, 0:128], mix_bd_n[:].rearrange("p h f -> p (h f)"), ident[:]).then_inc(pe_set, 1)
            pe.wait_ge(in_x, 3 * 16)
            for c in range(1, 4):
                turn_x(c)
            pe.wait_ge(dve_set, DV_SUP)
            pe.matmul(bank[0][:, 0:128], wn[:, WV, :], mix_bd[:], start=True, stop=True)
            pe.matmul(bank[0][:, 128:256], bv_cols[:], mix_bd[:], start=True, stop=True).then_inc(pe_set, 1)
            pe.wait_ge(in_c, 4 * 16)
            for c in range(4):
                pe.wait_ge(act_set, c + 2)
                for j in range(4):
                    t = pe.transpose(bank[C_BANK[c]][:, 128 * j:128 * j + 128], c_tok[:, 4 * c + j, :], ident[:])
                t.then_inc(pe_set, 1)
            pe.wait_ge(dve_set, DV_WALL)
            pe.wait_ge(act_set, 4)
            for b in range(NB):
                if b >= 4:
                    pe.wait_ge(dve_set, DV_WALL + b - 3)
                pe.matmul(bank[b % 4][:, 0:VSZ], x_t[:, 128 * b:128 * b + 128], wall[:],
                          start=True, stop=True).then_inc(pe_set, 1)
            for c in range(4):
                if c < 3:
                    pe.wait_ge(act_set, 6 + c)
                else:
                    pe.wait_ge(dve_set, DV_WALL + NB + 1)
                for j in range(4):
                    m = pe.matmul(bank[V_BANK[c]][:, 128 * j:128 * j + 128],
                                  c_t[:, 512 * c + 128 * j:512 * c + 128 * j + 128], xw_t[:, 2, :],
                                  start=True, stop=True)
                m.then_inc(pe_set, 1)
            pe.wait_ge(dve_set, DV_END)
            pe.wait_ge(act_set, 8)
            attention(L1, True, wo_t[:], TAIL1)

            pe.wait_ge(L1.tail, NB * TAIL1)
            for c in range(4):
                for j in range(4):
                    t = pe.transpose(bank[c][:, 128 * j:128 * j + 128], x1[:, 4 * c + j, :], ident[:])
                t.then_inc(turn1, 1)
            pe.wait_ge(turn1_ev, 4)
            project(L2, Batch(0, 0), False)
            project(L2, Batch(0, 1), False)
            attention(L2, False, xw_t[:, 3, :], TAIL2)

            pe.wait_ge(L2.tail, NB * TAIL2)
            for c in range(4):
                for j in range(4):
                    t = pe.transpose(bank[c][:, 128 * j:128 * j + 128], x2[:, 4 * c + j, :], ident[:])
                t.then_inc(turn2, 1)
            pe.wait_ge(turn2_ev, 4)
            for b in range(NB):
                m = pe.matmul(bank[7][:, NE * b:NE * b + NE], x_t[:, 128 * b:128 * b + 128], gate_t[:],
                              start=True, stop=True)
            m.then_inc(route_mm, 1)
            pe.wait_ge(route, RT_S3)
            for c in range(4):
                for j in range(4):
                    t = pe.transpose(bank[c][0:48, 64 * j:64 * j + 64].bitcast(BF16),
                                     s3[:, 4 * c + j, :, :].rearrange("p a e -> p (a e)"), ident_bf[:])
                t.then_inc(route_t, 1)
            pe.wait_ge(route_ev, 5)
            pe.wait_ge(in_ffn, 4 * 16)

            def up(c, kk):
                u = c * KC + kk
                late = not isinstance(u, int) or u >= 2
                xt = x_t[:, bass.ds(c * TC, TC)]
                if late:
                    pe.wait_ge(silu, u - 1)
                pe.matmul(bank[kk % 2][:], w1[:, 128 * kk:128 * kk + 128], xt, start=True, stop=True
                          ).then_inc(gate_mm, 1)
                if late:
                    pe.wait_ge(glu, u - 1)
                pe.matmul(bank[2 + kk % 2][:], w3[:, 128 * kk:128 * kk + 128], xt, start=True, stop=True)
                if late:
                    pe.wait_ge(glu_s, u - 1)
                pe.matmul(bank[4 + kk % 2][:], sel[:, kk, :], st[:, bass.ds(c * TC, TC)], start=True, stop=True
                          ).then_inc(up_mm, 1)

            def down_product(c, kk):
                u = c * KC + kk
                pe.wait_ge(glu_s, u + 1)
                if kk == 0 and (not isinstance(c, int) or c >= 1):
                    pe.wait_ge(ftail, c * FT - FT + 1)
                for t in range(4):
                    m = pe.matmul(bank[6][:, 128 * t:128 * t + 128], actt[kk % 2][:, 128 * t:128 * t + 128],
                                  w2[:, kk, :], start=(kk == 0 and t == 0), stop=(kk == KC - 1),
                                  skip_group_check=True)
                m.then_inc(down, 1)

            def chunk(c):
                for kk in range(KC):
                    up(c, kk)
                    if kk >= 1:
                        down_product(c, kk - 1)
                    elif not isinstance(c, int) or c >= 1:
                        down_product(c - 1, KC - 1)

            chunk(0)
            with pe.Fori(1, NCH) as c:
                chunk(c)
            down_product(NCH - 1, KC - 1)

        @block.scalar
        def _(act):
            act.dma_start(feat[:].rearrange("p a b t -> p (a b t)"), k["feat"]).then_inc(in_feat, 16)
            act.dma_start(upper_f[:], k["upper"]).then_inc(in_feat, 16)
            act.dma_start(mix_n[:], a["L0_attn_mix_w"].rearrange("h o d -> (h o) d")).then_inc(in_small, 16)
            act.dma_start(head_mask[:], k["head_mask"]).then_inc(in_small, 16)
            for r, n in enumerate(("L0_attn_amp_w", "L0_attn_ph_w", "L0_ffn_gate_w")):
                act.dma_start(gates_n[16 * r:16 * r + 16, :], a[n]).then_inc(in_small, 16)

            def take_projection(L, b, decayed):
                act.wait_ge(L.proj_done, b.n + 1)
                if not isinstance(b.n, int) or b.n >= 1:
                    act.wait_ge(L.rest, b.n)
                layer = 0 if decayed else 1
                at = 256 if decayed else 128
                act.activation(pf[:, 0, 0, :], bank[6][:, 0:128], ACT.Identity, bias=bias_q[:, layer:layer + 1],
                               scale=SCALE).then_inc(L.proj_ev, 1)
                col = 2 if decayed else 5
                act.activation(pf[:, 1, 0, :], bank[6][:, at:at + 128], ACT.Identity,
                               bias=bias_t[:, col:col + 1]).then_inc(L.proj_ev, 1)

            def high(L, b, decayed):
                act.wait_ge(L.proj_ev, b.n * 2 + 2)
                if decayed:
                    act.wait_ge(L.ent_ev, b.n * 2 + 2)
                if not isinstance(b.n, int) or b.n >= 2:
                    act.wait_ge(L.spilled, b.n * L.spill_step - L.spill_step)
                act.copy(parts[b.par][:, :, 0, L.kinds, :], pf[:, :, L.kinds, :]).then_inc(L.high, 1)

            def middle(L, b):
                act.wait_ge(L.rest, b.n + 1)
                act.copy(parts[b.par][:, :, 1, L.kinds, :], rest[:, :, L.kinds, :]).then_inc(L.mid, 1)

            def exponent(L, b, g):
                u = b.n * NG + g
                act.wait_ge(L.shifted, u + 1)
                if not isinstance(u, int) or u >= 2:
                    act.wait_ge(L.turned, u - 1)
                act.activation(prob[g % 2][:].rearrange("p h t -> p (h t)"), bank[g % 2][:], ACT.Exp
                               ).then_inc(L.exped, 1)

            def take_turned(L, b, g):
                u = b.n * NG + g
                act.wait_ge(L.turned, u + 1)
                if not isinstance(u, int) or u >= 2:
                    act.wait_ge(L.pv, u - 1)
                act.copy(prob_t[g % 2][:].rearrange("p h t -> p (h t)"), bank[3][:]).then_inc(L.turned_ev, 1)

            def take_pv(L, b):
                act.wait_ge(L.pv, b.n * NG + NG)
                if not isinstance(b.n, int) or b.n >= 1:
                    act.wait_ge(L.o_tok, b.n)
                act.copy(pvs[:].rearrange("p g t -> p (g t)"), bank[4 + b.par][:]).then_inc(L.pv_ev, 1)

            def take_out(L, b):
                act.wait_ge(L.o_t, b.n + 1)
                if not isinstance(b.n, int) or b.n >= 1:
                    act.wait_ge(L.o_out, b.n)
                act.copy(attn_ot[:], bank[7][:, 0:128]).then_inc(L.o_t_ev, 1)

            def pair(L, p, decayed):
                for par in range(2):
                    bb = Batch(p, par)
                    for g in range(NG):
                        ahead = bb.back(-2)
                        if g == 0 and ahead.live:
                            take_projection(L, ahead, decayed)
                            if not decayed:
                                high(L, ahead, decayed)
                        if g == 2 and ahead.live and not decayed:
                            middle(L, ahead)
                        b = bb.back(1)
                        for lag, stage in ((1, exponent), (2, take_turned)):
                            ub, ug = unit_back(b, g, lag)
                            if ub.live:
                                stage(L, ub, ug)
                        if g == 1 and ahead.live and decayed:
                            high(L, ahead, decayed)
                        if g == 2 and bb.back(2).live:
                            take_pv(L, bb.back(2))
                        if g == 3 and ahead.live and decayed:
                            middle(L, ahead)
                        if g == 0 and bb.back(3).live:
                            take_out(L, bb.back(3))

            def attention(L, decayed):
                pair(L, 0, decayed)
                pair(L, 1, decayed)
                with act.Fori(2, 7) as p:
                    pair(L, p, decayed)
                pair(L, 7, decayed)
                pair(L, 8, decayed)
                pair(L, 9, decayed)

            def take_x(c):
                act.wait_ge(pe_set, PE_X[c])
                act.copy(x_t[:, 512 * c:512 * c + 512], bank[X_BANK[c]][:]).then_inc(act_set, 1)

            take_x(0)
            act.wait_ge(dve_set, DV_COLS)
            for par in range(2):
                take_projection(L1, Batch(0, par), True)
                high(L1, Batch(0, par), True)
                take_x(1 + par)
                middle(L1, Batch(0, par))
            take_x(3)
            for c in range(4):
                act.wait_ge(pe_set, PE_C + c + 1)
                act.copy(c_t[:, 512 * c:512 * c + 512], bank[C_BANK[c]][:]).then_inc(act_set, 1)
            act.wait_ge(dve_set, DV_WALL + NB)
            act.activation(ph_t[:, 0], vsz[:, :, 2 * D:2 * D + H], ACT.Tanh, scale=0.5).then_inc(gate_step, 1)
            act.activation(ph_t[:, 1], vsz[:, :, 2 * D + H:VSZ], ACT.Tanh).then_inc(gate_step, 1)
            act.wait_ge(gate_step, 2)
            act.activation(ph_t[:, 3], ph_t[:, 1], ACT.Abs, scale=math.pi / 2).then_inc(gate_step, 1)
            act.activation(ph_t[:, 2], ph_t[:, 1], ACT.Sin, scale=math.pi / 2).then_inc(gate_step, 1)
            act.wait_ge(gate_step, 4)
            act.activation(ph_t[:, 4], ph_t[:, 3], ACT.Sin, scale=-1.0, bias=half_pi[:, 0:1]).then_inc(gate_step, 1)
            act.wait_ge(dve_set, DV_END)
            attention(L1, True)
            for c in range(4):
                act.wait_ge(turn1, c + 1)
                act.copy(x_t[:, 512 * c:512 * c + 512], bank[c][:]).then_inc(turn1_ev, 1)
            for par in range(2):
                take_projection(L2, Batch(0, par), False)
                high(L2, Batch(0, par), False)
                middle(L2, Batch(0, par))
            attention(L2, False)
            for c in range(4):
                act.wait_ge(turn2, c + 1)
                act.copy(x_t[:, 512 * c:512 * c + 512], bank[c][:]).then_inc(turn2_ev, 1)
            act.wait_ge(route, 2)
            act.activation(rt[:, 1], rt[:, 0], ACT.Exp).then_inc(route_exp, 1)
            for c in range(4):
                act.wait_ge(route_t, c + 1)
                act.copy(st[0:48, 512 * c:512 * c + 512], bank[c][0:48, 0:256].bitcast(BF16)).then_inc(route_ev, 1)

            def gate(c, kk):
                u = c * KC + kk
                act.wait_ge(gate_mm, u + 1)
                if not isinstance(u, int) or u >= 2:
                    act.wait_ge(glu, u - 1)
                act.activation(sg[kk % 2], bank[kk % 2][:], ACT.Silu).then_inc(silu, 1)

            for kk in range(KC):
                gate(0, kk)
            with act.Fori(1, NCH) as c:
                for kk in range(KC):
                    gate(c, kk)

        @block.vector
        def _(dve):
            made = [0]

            def step(ins):
                made[0] += 1
                ins.then_inc(dve_set, 1)
                return made[0]

            def after(n):
                dve.wait_ge(dve_set, n)

            def carry():
                dve.memset(waiter[:, 0:1], 0.0)

            def entangled(b):
                dve.wait_ge(L1.proj_ev, b.n * 2 + 2)
                if not isinstance(b.n, int) or b.n >= 1:
                    dve.wait_ge(L1.rest, b.n)
                dve.memset(waiter[:, 1:2], 0.0)
                for side in range(2):
                    dve.scalar_tensor_tensor(
                        pf[:, side, 1:3, :],
                        bank[6][:, 256 * side + 128:256 * side + 256].unsqueeze(1).broadcast_to([128, 2, S]),
                        bias_t[:, 2 * side + 1:2 * side + 2], feat[:, side, :, :], ALU.add, ALU.mult
                        ).then_inc(L1.ent_ev, 1)

            for p in range(2):
                n = step(dve.memset(stk[p][R1:128], 0.0))
            assert n == DV_STK0
            step(dve.memset(half_pi[:], math.pi / 2))
            step(dve.memset(st[:], 0.0))
            dve.wait_ge(in_bias, 7 * 16)
            n = step(dve.tensor_copy(bias_perm[:].rearrange("r (f h) -> r f h", h=H),
                                     bias_rows[:].rearrange("r (h f) -> r f h", f=HD)))
            assert n == DV_BIAS
            dve.wait_ge(pe_set, PE_QK)
            for i in range(4):
                n = step(dve.tensor_copy(wqk1[:, i // 2, i % 2, :, :],
                                         bank[0][:, 128 * i:128 * i + 128].rearrange("p (h f) -> p f h", f=HD)))
            assert n == DV_QK
            dve.wait_ge(pe_set, PE_BIAS)
            step(dve.tensor_copy(bias_t[:, 0:6], bank[3][:, 128:134]))
            n = step(dve.tensor_copy(bias_t[:, 6:7], bank[3][:, 141:142]))
            after(n)
            step(dve.tensor_scalar(bias_q[:, 0:1], bias_t[:, 0:1], SCALE, None, ALU.mult))
            n = step(dve.tensor_scalar(bias_q[:, 1:2], bias_t[:, 4:5], SCALE, None, ALU.mult))
            assert n == DV_COLS
            dve.wait_ge(in_small, 5 * 16)
            n = step(dve.tensor_tensor(mix_bd_n[:], mix_n[:].unsqueeze(1).broadcast_to([128, H, HD]),
                                       head_mask[:].unsqueeze(2).broadcast_to([128, H, HD]), ALU.mult))
            assert n == DV_MIX
            dve.wait_ge(in_feat, 2 * 16)
            entangled(Batch(0, 0))
            dve.wait_ge(in_const, 16)
            step(dve.tensor_scalar(neg_ident[:], ident[:], -1.0, None, ALU.mult))
            step(dve.tensor_copy(ident_bf[:], ident[:]))
            step(dve.tensor_copy(upper[:], upper_f[:]))
            n = step(dve.memset(bv_cols[:], 1.0))
            after(n)
            step(dve.tensor_scalar(bv_cols[:], bv_cols[:], bias_t[:, 6:7], None, ALU.mult))
            dve.wait_ge(pe_set, PE_W - 1)
            step(dve.tensor_copy(wall[:, 0:D], bank[1][:, 0:128]))
            step(dve.tensor_copy(wo_t[:], bank[1][:, 128:256]))
            for i in range(2):
                step(dve.tensor_copy(xw_t[:, i, :].rearrange("p (f h) -> p f h", h=H),
                                     bank[1][:, 256 + 128 * i:384 + 128 * i].rearrange("p (h f) -> p f h", f=HD)))
            dve.wait_ge(pe_set, PE_W)
            step(dve.tensor_copy(xw_t[:, 2:4, :].rearrange("p a n -> p (a n)"), bank[2][:, 0:256]))
            step(dve.tensor_copy(wall[:, 2 * D:VSZ], bank[2][:, 256:288]))
            step(dve.tensor_copy(gate_t[:], bank[2][:, 288:304]))
            dve.wait_ge(pe_set, PE_MIX)
            n = step(dve.tensor_copy(mix_bd[:], bank[3][:, 0:128]))
            assert n == DV_SUP
            entangled(Batch(0, 1))
            dve.wait_ge(in_rows, 9 * 16)
            step(dve.tensor_copy(row_bias[:, 0:D], row_in[:, 0:D]))
            step(dve.tensor_copy(row_bias[:, 2 * D:VSZ], row_in[:, 2 * D:VSZ]))
            dve.wait_ge(pe_set, PE_SUP)
            step(dve.tensor_copy(wall[:, D:2 * D], bank[0][:, 0:128]))
            n = step(dve.tensor_tensor(row_bias[:, D:2 * D], bank[0][:, 128:256], row_in[:, D:2 * D], ALU.add))
            assert n == DV_WALL
            after(n)
            for b in range(NB):
                dve.wait_ge(pe_set, PE_VSZ + b + 1)
                step(dve.tensor_tensor(vsz[:, b, :], bank[b % 4][:, 0:VSZ], row_bias[:], ALU.add))
            for c in range(4):
                dve.wait_ge(pe_set, PE_V2 + c + 1)
                n = step(dve.tensor_tensor(v2_all[:, 4 * c:4 * c + 4, :],
                                           bank[V_BANK[c]][:].rearrange("p (b n) -> p b n", b=4),
                                           bv2[:].unsqueeze(1).broadcast_to([128, 4, D]), ALU.add))
            after(n)
            for p in range(2):
                n = step(dve.memset(bank[4 + p][:], 0.0))
            assert n == DV_END
            dve.wait_ge(gate_step, 5)
            dve.tensor_scalar(ph_t[:, 5], ph_t[:, 0], SUP / 2, SUP / 2, ALU.mult, ALU.add).then_inc(gate_step, 1)
            dve.tensor_tensor(ph_t[:, 3], ph_t[:, 2], ph_t[:, 2], ALU.mult).then_inc(gate_step, 1)
            dve.wait_ge(gate_step, 7)
            dve.tensor_tensor(ph_t[:, 4], ph_t[:, 2], ph_t[:, 4], ALU.mult).then_inc(gate_step, 1)
            dve.tensor_scalar(ph_t[:, 3], ph_t[:, 3], -2.0, 1.0, ALU.mult, ALU.add).then_inc(gate_step, 1)
            dve.wait_ge(gate_step, 9)
            dve.tensor_tensor(ph_t[:, 1], ph_t[:, 4], ph_t[:, 5], ALU.mult).then_inc(gate_step, 1)
            dve.tensor_tensor(coef[:, 0], ph_t[:, 3], ph_t[:, 5], ALU.mult).then_inc(gate_step, 1)
            dve.wait_ge(gate_step, 11)
            dve.tensor_scalar(coef[:, 1], ph_t[:, 1], 2.0, None, ALU.mult).then_inc(gate_step, 1)

            def pick(L, b, g):
                u = b.n * NG + g
                dve.wait_ge(L.scores, u + 1)
                carry()
                dve.copy_predicated(bank[g % 2][:].rearrange("p (h t) -> p h t", h=GH),
                                    upper[:].unsqueeze(1).broadcast_to([128, GH, S]),
                                    bank[2][:].rearrange("p (h t) -> p h t", h=GH)).then_inc(L.picked, 1)

            def maximum(L, b, g, decayed):
                u = b.n * NG + g
                if decayed:
                    dve.wait_ge(L.picked, u + 1)
                else:
                    dve.wait_ge(L.scores, u + 1)
                if not isinstance(u, int) or u >= 2:
                    dve.wait_ge(L.shifted, u - 1)
                with nc.allow_low_precision(reason="the shift cancels"):
                    dve.tensor_reduce(shift[:, g % 2, :], bank[g % 2][:].rearrange("p (h t) -> p h t", h=GH),
                                      AX.X, ALU.max).then_inc(L.maxed, 1)

            def divide(L, b):
                dve.wait_ge(L.o_tok, b.n + 1)
                o = bank[7][:].rearrange("p (h r) -> p h r", r=32)
                dve.reciprocal(rden[:], o[:, :, HD:HD + 1].rearrange("p h r -> p (h r)")).then_inc(L.norm_step, 1)
                dve.wait_ge(L.norm_step, b.n + 1)
                if not isinstance(b.n, int) or b.n >= 1:
                    dve.wait_ge(L.o_t, b.n)
                dve.tensor_tensor(attn_o[:].rearrange("p (h f) -> p h f", f=HD), o[:, :, 0:HD],
                                  rden[:].unsqueeze(2).broadcast_to([128, H, HD]), ALU.mult).then_inc(L.normed, 1)

            def moments(L, b, which, src, steps, first):
                dve.wait_ge(L.tail, b.n * steps + first)
                dve.bn_stats(stats[:, which, :], src).then_inc(L.tail, 1)
                dve.wait_ge(L.tail, b.n * steps + first + 1)
                carry()
                dve.bn_aggr(mv[:, which, :], stats[:, which, :]).then_inc(L.tail, 1)
                dve.wait_ge(L.tail, b.n * steps + first + 2)
                dve.tensor_scalar(veps[:, which:which + 1], mv[:, which, 1:2], EPS, None, ALU.add
                                  ).then_inc(L.tail, 1)

            def residual(L, b, steps):
                dve.wait_ge(L.o_out, b.n + 1)
                if not isinstance(b.n, int) or b.n >= 1:
                    dve.wait_ge(L.tail, b.n * steps)
                dve.tensor_tensor(res[:], bank[7][:, 128:256],
                                  xb_all[:, bass.ds(b.n, 1), :].rearrange("p b n -> p (b n)"),
                                  ALU.add).then_inc(L.tail, 1)
                moments(L, b, 0, res[:], steps, 1)

            def norm_out(L, b, which, src, dst, steps, need):
                dve.wait_ge(L.rstd, need)
                dve.tensor_scalar(dst[:, bass.ds(b.n, 1), :].rearrange("p b n -> p (b n)"), src,
                                  mv[:, which, 0:1], rstd[:, which:which + 1],
                                  ALU.subtract, ALU.mult).then_inc(L.tail, 1)

            def inner(b):
                L, t = L1, TAIL1
                dve.wait_ge(L.rstd, b.n * 2 + 1)
                dve.tensor_scalar(res[:], res[:], mv[:, 0, 0:1], rstd[:, 0:1], ALU.subtract, ALU.mult
                                  ).then_inc(L.tail, 1)
                dve.wait_ge(L.tail, b.n * t + 5)
                dve.tensor_tensor(res2[:], res[:], ln_g[:], ALU.mult).then_inc(inner_g, 1)
                dve.wait_ge(inner_g, b.n + 1)
                dve.tensor_tensor(res2[:], res2[:], xl_all[:, bass.ds(b.n, 1), :].rearrange("p b n -> p (b n)"),
                                  ALU.add).then_inc(L.tail, 1)
                moments(L, b, 1, res2[:], t, 6)

            def pair1(p):
                for par in range(2):
                    bb = Batch(p, par)
                    for g in range(NG):
                        b = bb.back(1)
                        if b.live:
                            pick(L1, b, g)
                            maximum(L1, b, g, True)
                        if g == 0 and bb.back(-2).live:
                            entangled(bb.back(-2))
                        if g == 3 and bb.back(2).live:
                            divide(L1, bb.back(2))
                        if g == 2 and bb.back(3).live:
                            residual(L1, bb.back(3), TAIL1)
                        if g == 3 and bb.back(3).live:
                            inner(bb.back(3))
                        if g == 1 and bb.back(4).live:
                            c = bb.back(4)
                            norm_out(L1, c, 1, res2[:], x1, TAIL1, c.n * 2 + 2)

            def pair2(p):
                for par in range(2):
                    bb = Batch(p, par)
                    for g in range(NG):
                        b = bb.back(1)
                        if b.live:
                            maximum(L2, b, g, False)
                        if g == 3 and bb.back(2).live:
                            divide(L2, bb.back(2))
                        if g == 2 and bb.back(3).live:
                            residual(L2, bb.back(3), TAIL2)
                        if g == 3 and bb.back(3).live:
                            c = bb.back(3)
                            norm_out(L2, c, 0, res[:], x2, TAIL2, c.n + 1)

            dve.wait_ge(pool_set, 2)
            pair1(0)
            pair1(1)
            with dve.Fori(2, 7) as p:
                pair1(p)
            pair1(7)
            pair1(8)
            pair1(9)
            dve.wait_ge(L1.scores, NG * NB)
            for p in range(2):
                dve.memset(stk2[p], 0.0).then_inc(rezeroed, 1)
            dve.wait_ge(xb2, 1)
            pair2(-1)
            pair2(0)
            pair2(1)
            with dve.Fori(2, 7) as p:
                pair2(p)
            pair2(7)
            pair2(8)
            pair2(9)

            done = [0]

            def rstep(ins):
                done[0] += 1
                ins.then_inc(route, 1)
                dve.wait_ge(route, done[0])

            logits = bank[7][:, 0:NB * NE].rearrange("p (b e) -> p b e", e=NE)

            def by_expert(t):
                return t.unsqueeze(2).broadcast_to([128, NB, NE])

            dve.wait_ge(route_mm, 1)
            rstep(dve.tensor_reduce(rsm[:, 0], logits, AX.X, ALU.max))
            rstep(dve.tensor_tensor(rt[:, 0], logits, by_expert(rsm[:, 0]), ALU.subtract))
            dve.wait_ge(route_exp, 1)
            for b in range(NB):
                last = dve.max(r8[:, b, :], rt[:, 1, b, :])
            rstep(last)
            fourth = r8[:, :, TOPK - 1:TOPK].broadcast_to([128, NB, NE])
            rstep(dve.tensor_tensor(rt[:, 2], rt[:, 1], fourth, ALU.is_gt))
            rstep(dve.tensor_tensor(rt[:, 3], rt[:, 1], fourth, ALU.is_equal))
            rstep(dve.tensor_reduce(rsm[:, 1], rt[:, 2], AX.X, ALU.add))
            rstep(dve.tensor_scalar(rsm[:, 2], rsm[:, 1], -1.0, float(TOPK), ALU.mult, ALU.add))
            src = 3
            for sh, dst in ((1, 4), (2, 5), (4, 4), (8, 5)):
                rstep(dve.tensor_copy(rt[:, dst, :, 0:sh], rt[:, src, :, 0:sh]))
                rstep(dve.tensor_tensor(rt[:, dst, :, sh:NE], rt[:, src, :, sh:NE], rt[:, src, :, 0:NE - sh],
                                        ALU.add))
                src = dst
            rstep(dve.tensor_tensor(rt[:, 6], rt[:, src], by_expert(rsm[:, 2]), ALU.is_le))
            rstep(dve.tensor_tensor(rt[:, 6], rt[:, 6], rt[:, 3], ALU.mult))
            rstep(dve.tensor_tensor(rt[:, 6], rt[:, 6], rt[:, 2], ALU.add))
            rstep(dve.tensor_tensor(rt[:, 6], rt[:, 6], rt[:, 1], ALU.mult))
            rstep(dve.tensor_reduce(rsm[:, 3], rt[:, 6], AX.X, ALU.add))
            rstep(dve.reciprocal(rsm[:, 3], rsm[:, 3]))
            rstep(dve.tensor_tensor(rt[:, 7], rt[:, 6], by_expert(rsm[:, 3]), ALU.mult))
            rstep(dve.tensor_copy(s3[:, :, 0, :], rt[:, 7]))
            rstep(dve.tensor_tensor(rt[:, 0], rt[:, 7], s3[:, :, 0, :], ALU.subtract))
            rstep(dve.tensor_copy(s3[:, :, 1, :], rt[:, 0]))
            rstep(dve.tensor_tensor(rt[:, 1], rt[:, 0], s3[:, :, 1, :], ALU.subtract))
            rstep(dve.tensor_copy(s3[:, :, 2, :], rt[:, 1]))
            assert done[0] == RT_S3, done[0]
            dve.wait_ge(in_ffn, 4 * 16)
            dve.tensor_copy(sel[:], sel_f[:]).then_inc(route_ev, 1)

            def glu_step(c, kk):
                u = c * KC + kk
                dve.wait_ge(up_mm, u + 1)
                dve.wait_ge(silu, u + 1)
                dve.tensor_tensor(h1[kk % 2], bank[2 + kk % 2][:], sg[kk % 2], ALU.mult).then_inc(glu, 1)
                dve.wait_ge(glu, u + 1)
                if not isinstance(u, int) or u >= 2:
                    dve.wait_ge(down, u - 1)
                dve.tensor_tensor(actt[kk % 2], bank[4 + kk % 2][:], h1[kk % 2], ALU.mult).then_inc(glu_s, 1)

            def finish(c, part):
                at = c * FT
                if part == 0:
                    dve.wait_ge(down, c * KC + KC)
                    dve.tensor_tensor(fres[:], bank[6][:].rearrange("p (b n) -> p b n", b=4),
                                      x2[:, bass.ds(c * 4, 4), :], ALU.add).then_inc(ftail, 1)
                    dve.wait_ge(ftail, at + 1)
                    for t in range(4):
                        dve.bn_stats(fstats[:, t, :], fres[:, t, :]).then_inc(fst, 1)
                    dve.wait_ge(fst, c * 4 + 4)
                    carry()
                    for t in range(4):
                        dve.bn_aggr(fmv[:, t, :], fstats[:, t, :]).then_inc(ftail, 1)
                    dve.wait_ge(ftail, at + 5)
                    dve.tensor_scalar(fveps[:], fmv[:, :, 1], EPS, None, ALU.add).then_inc(ftail, 1)
                else:
                    dve.wait_ge(frs, c + 1)
                    if not isinstance(c, int) or c >= 1:
                        dve.wait_ge(stored, c * 16)
                    for t in range(4):
                        dve.tensor_scalar(fout[:, t, :], fres[:, t, :], fmv[:, t, 0:1], frstd[:, t:t + 1],
                                          ALU.subtract, ALU.mult).then_inc(ftail, 1)

            def chunk(c):
                for kk in range(KC):
                    glu_step(c, kk)
                    if kk in (1, 3) and (not isinstance(c, int) or c >= 1):
                        finish(c - 1, kk // 2)
            chunk(0)
            with dve.Fori(1, NCH) as c:
                chunk(c)
            finish(NCH - 1, 0)
            finish(NCH - 1, 1)


_OUTS = [((NB, S, D), "float32")]


def kernel(**inputs):
    import numpy as _np
    import concourse.bacc as _bacc
    from concourse import mybir as _mybir
    from concourse.bass_utils import run_bass_kernel_spmd as _run

    pos = _np.arange(S, dtype=_np.float64) - (S - 1) / 2
    feat = _np.zeros((128, 2, 2, S))
    for side, sign in ((0, -1.0), (1, 1.0)):
        for tri, way in ((0, 1.0), (1, -1.0)):
            feat[:, side, tri, :] = _np.exp(sign * way * DECAY * pos)
    feat[:, 0] *= SCALE * ENT
    p = _np.arange(128)
    sel = _np.zeros((128, KC, 128))
    for c in range(KC):
        for e in range(2):
            for part in range(3):
                sel[NE * part + 2 * c + e, c, INTER * e:INTER * e + INTER] = 1.0
    consts = {
        "ident": _np.eye(128),
        "feat": feat.reshape(128, -1),
        "upper": (p[None, :] > p[:, None]),
        "head_mask": (p[:, None] // HD == _np.arange(H)[None, :]),
        "sel": sel.reshape(128, -1),
    }
    nc = _bacc.Bacc("TRN2", target_bir_lowering=False, num_devices=1)
    arrays, args, kargs = {}, {}, {}
    for name in inputs:
        v = _np.ascontiguousarray(inputs[name])
        arrays[f"in_{name}_dram"] = v
        args[name] = nc.dram_tensor(f"in_{name}_dram", v.shape, _mybir.dt.from_np(v.dtype), kind="ExternalInput").ap()
    for name, v in consts.items():
        v = _np.ascontiguousarray(v.astype(_np.float32))
        arrays[f"const_{name}_dram"] = v
        kargs[name] = nc.dram_tensor(f"const_{name}_dram", v.shape, _mybir.dt.from_np(v.dtype), kind="ExternalInput").ap()
    outs = []
    for i, (shape, dtype) in enumerate(_OUTS):
        outs.append(nc.dram_tensor(f"out_{i}_dram", shape, _mybir.dt.from_np(_np.dtype(dtype)), kind="ExternalOutput").ap())
    build(nc, args, kargs, outs[0])
    r = _run(nc, [arrays], core_ids=[0])
    return r.results[0]["out_0_dram"]
```

```python
import math
from contextlib import ExitStack

import concourse.bass as bass
from concourse import mybir

F32 = mybir.dt.float32
BF16 = mybir.dt.bfloat16
U8 = mybir.dt.uint8
ACT = mybir.ActivationFunctionType
ALU = mybir.AluOpType
AX = mybir.AxisListType

NB = 16
S = 128
D = 128
H = 16
HD = D // H
NE = 16
INTER = 64
TOPK = 4
EPS = 1e-5
SCALE = 1.0 / math.sqrt(HD)
ENT = 0.5
DECAY = 0.1
SUP = 0.3
GH = 4
NG = H // GH
Q_PART = (0, 0, 0, 1, 1, 2)
K_PART = (0, 1, 2, 0, 1, 0)
NP = len(Q_PART)
R1 = NP * 2 * HD
R2 = NP * HD
KC = NE * INTER // 128
TC = 512
NCH = NB * S // TC
WQ, WEQ, WK, WEK, WV, WO, XQ, XK, XV, XO = range(10)
VSZ = 2 * D + 2 * H


class Batch:

    def __init__(self, pair, par):
        self.pair, self.par = pair, par
        self.n = pair * 2 + par

    def back(self, lag):
        p = self.par - lag
        return Batch(self.pair + p // 2, p % 2)

    @property
    def live(self):
        return not isinstance(self.n, int) or 0 <= self.n < NB


def unit_back(b, g, lag):
    q = g - lag
    return b.back(-(q // NG)), q % NG


def build(nc, a, k, out):
    with ExitStack() as ctx:
        def sb(name, shape, dt=F32):
            return ctx.enter_context(nc.sbuf_tensor(name, shape, dt))

        def sem(name):
            return ctx.enter_context(nc.semaphore(name))

        ident = sb("ident", [128, 128])
        neg_ident = sb("neg_ident", [128, 128], BF16)
        ident_bf = sb("ident_bf", [128, 128], BF16)
        feat = sb("feat", [128, 2, 2, S])
        upper_f = sb("upper_f", [128, S])
        upper = sb("upper", [128, S], U8)
        head_mask = sb("head_mask", [128, H])
        sel_f = sb("sel_f", [128, KC, 128])
        sel = sb("sel", [128, KC, 128], BF16)
        wn = sb("wn", [128, 10, D])
        gates_n = sb("gates_n", [48, D])
        bias_rows = sb("bias_rows", [7, D])
        bias_perm = sb("bias_perm", [7, D])
        mix_n = sb("mix_n", [128, HD])
        mix_bd_n = sb("mix_bd_n", [128, H, HD])
        mix_bd = sb("mix_bd", [128, D])
        bv_cols = sb("bv_cols", [128, 128])
        wqk1 = sb("wqk1", [128, 2, 2, HD, H])
        wall = sb("wall", [128, VSZ])
        wo_t = sb("wo_t", [128, D])
        xw_t = sb("xw_t", [128, 4, D])
        gate_t = sb("gate_t", [128, NE])
        bias_t = sb("bias_t", [128, 8])
        bias_q = sb("bias_q", [128, 2])
        row_in = sb("row_in", [128, VSZ])
        row_bias = sb("row_bias", [128, VSZ])
        bo1 = sb("bo1", [128, D])
        ln_g = sb("ln_g", [128, D])
        ln_b = sb("ln_b", [128, D])
        bv2 = sb("bv2", [128, D])
        bo2 = sb("bo2", [128, D])
        x_tok = sb("x_tok", [128, NB, D])
        c_tok = sb("c_tok", [128, NB, D])
        x_t = sb("x_t", [128, NB * S])
        c_t = sb("c_t", [128, NB * S])
        xb_all = sb("xb_all", [128, NB, D])
        xl_all = sb("xl_all", [128, NB, D])
        vsz = sb("vsz", [128, NB, VSZ])
        v2_all = sb("v2_all", [128, NB, D])
        ph_t = sb("ph_t", [128, 6, NB, H])
        coef = sb("coef", [128, 2, NB, H])
        minus_half = sb("minus_half", [128, NB])
        eps_col = sb("eps_col", [128, 1])
        waiter = sb("waiter", [128, 4])
        half_pi = sb("half_pi", [128, 1])
        w1 = sb("w1", [128, NE * INTER])
        w3 = sb("w3", [128, NE * INTER])
        w2 = sb("w2", [128, KC, D])
        pf = sb("pf", [128, 2, 3, S])
        rest = sb("rest", [128, 2, 3, S])
        parts = [sb(f"parts{p}", [128, 2, 3, 3, S], BF16) for p in range(2)]
        stk = [sb(f"stk{p}", [128, 2, H, 2, S], BF16) for p in range(2)]
        stk2 = [stk[p][:].rearrange("p a h u t -> p a (h u t)")[:, :, 0:H * S].rearrange("p a (h t) -> p a h t", t=S)
                for p in range(2)]
        scr1 = nc.dram_tensor("parts1_dram", (NB, 2, 3, 2, 128, 2, S), BF16, kind="Internal").ap()
        scr2 = nc.dram_tensor("parts2_dram", (NB, 2, 3, 128, S), BF16, kind="Internal").ap()
        vmix = [sb(f"vmix{p}", [128, H, 2, HD]) for p in range(2)]
        mixa = sb("mixa", [128, D])
        mixb = sb("mixb", [128, D])
        mixc = sb("mixc", [128, D])
        shift = sb("shift", [128, 2, GH], BF16)
        prob = [sb(f"prob{p}", [128, GH, S]) for p in range(2)]
        prob_t = [sb(f"prob_t{p}", [128, GH, S]) for p in range(2)]
        pvs = sb("pvs", [128, NG, S])
        rden = sb("rden", [128, H])
        attn_o = sb("attn_o", [128, D])
        attn_ot = sb("attn_ot", [128, D])
        res = sb("res", [128, D])
        res2 = sb("res2", [128, D])
        stats = sb("stats", [128, 2, 6])
        mv = sb("mv", [128, 2, 2])
        veps = sb("veps", [128, 2])
        rstd = sb("rstd", [128, 2])
        rt = vsz[:].rearrange("p b n -> p (b n)")[:, 0:8 * NB * NE].rearrange("p (a b e) -> p a b e", a=8, b=NB)
        r8 = sb("r8", [128, NB, 8])
        rsm = sb("rsm", [128, 4, NB])
        s3 = sb("s3", [128, NB, 3, NE], BF16)
        st = sb("st", [128, NB * S], BF16)
        scratch = stk[0][:].rearrange("p a h u t -> p (a h u t)").bitcast(F32)
        sg = [scratch[:, TC * p:TC * p + TC] for p in range(2)]
        h1 = [scratch[:, TC * (2 + p):TC * (3 + p)] for p in range(2)]
        actt = [scratch[:, TC * (4 + p):TC * (5 + p)] for p in range(2)]
        fres = sb("fres", [128, 4, D])
        fstats = sb("fstats", [128, 4, 6])
        fmv = sb("fmv", [128, 4, 2])
        fveps = sb("fveps", [128, 4])
        frstd = sb("frstd", [128, 4])
        fout = sb("fout", [128, 4, D])

        x1 = x_tok
        x2 = c_tok
        bank = [ctx.enter_context(nc.psum_tensor(f"bank{i}", [128, 512], F32)) for i in range(8)]

        in_const = sem("in_const")
        in_qk = sem("in_qk")
        in_w = sem("in_w")
        in_rows = sem("in_rows")
        in_bias = sem("in_bias")
        in_small = sem("in_small")
        in_x0 = sem("in_x0")
        in_feat = sem("in_feat")
        in_x = sem("in_x")
        in_c = sem("in_c")
        in_ffn = sem("in_ffn")
        pool_const = sem("pool_const")
        pe_set = sem("pe_set")
        dve_set = sem("dve_set")
        act_set = sem("act_set")
        gate_step = sem("gate_step")
        pool_set = sem("pool_set")
        stored = sem("stored")

        class Layer:

            def __init__(self, n, kinds, rows, spills):
                self.kinds = kinds
                self.rows = rows
                self.stack_step = 16 * 6
                self.spill_step = 16 * spills
                self.proj_done = sem(f"proj_done{n}")
                self.proj_ev = sem(f"proj_ev{n}")
                self.ent_ev = sem(f"ent_ev{n}")
                self.high = sem(f"high{n}")
                self.rest = sem(f"rest{n}")
                self.mid = sem(f"mid{n}")
                self.low = sem(f"low{n}")
                self.spilled = [sem(f"spilled{n}{p}") for p in range(2)]
                self.stacked = [sem(f"stacked{n}{p}") for p in range(2)]
                self.scores = sem(f"scores{n}")
                self.picked = sem(f"picked{n}")
                self.maxed = sem(f"maxed{n}")
                self.shifted = sem(f"shifted{n}")
                self.exped = sem(f"exped{n}")
                self.turned = sem(f"turned{n}")
                self.turned_ev = sem(f"turned_ev{n}")
                self.v_ready = sem(f"v_ready{n}")
                self.v_step = sem(f"v_step{n}")
                self.pv = sem(f"pv{n}")
                self.pv_ev = sem(f"pv_ev{n}")
                self.o_tok = sem(f"o_tok{n}")
                self.normed = sem(f"normed{n}")
                self.norm_step = sem(f"norm_step{n}")
                self.o_t = sem(f"o_t{n}")
                self.o_t_ev = sem(f"o_t_ev{n}")
                self.o_out = sem(f"o_out{n}")
                self.tail = sem(f"tail{n}")
                self.var_eps = sem(f"var_eps{n}")
                self.rstd = sem(f"rstd{n}")
        L1, L2 = Layer(1, slice(0, 3), R1, 3), Layer(2, slice(0, 1), R2, 1)
        zeroed = sem("zeroed")
        TAIL1, TAIL2 = 7, 5

        turn1 = sem("turn1")
        turn1_ev = sem("turn1_ev")
        x1_out = sem("x1_out")
        v2_mm = sem("v2_mm")
        v2_ready = sem("v2_ready")
        xb2 = sem("xb2")
        turn2 = sem("turn2")
        turn2_ev = sem("turn2_ev")
        sel_ready = sem("sel_ready")
        route_mm = sem("route_mm")
        route = sem("route")
        route_exp = sem("route_exp")
        route_t = sem("route_t")
        route_ev = sem("route_ev")
        gate_mm = sem("gate_mm")
        up_mm = sem("up_mm")
        silu = sem("silu")
        glu = sem("glu")
        glu_s = sem("glu_s")
        down = sem("down")
        ftail = sem("ftail")
        fst = sem("fst")
        inner_g = sem("inner_g")
        frs = sem("frs")
        FT = 10

        PE_QK, PE_BIAS, PE_W, PE_MIX, PE_SUP, PE_C, PE_VSZ = 1, 2, 5, 6, 10, 10, 14
        PE_V2 = PE_VSZ + NB
        PE_X = (3, 7, 8, 9)
        DV_BIAS, DV_QK, DV_COLS, DV_MIX, DV_SUP, DV_WALL = 2, 6, 10, 11, 25, 29
        DV_END = DV_WALL + NB + 2
        X_BANK, C_BANK, V_BANK = (4, 5, 7, 4), (5, 7, 4, 5), (2, 0, 1, 2)
        RT_S3 = 27
        block = ctx.enter_context(nc.Block())

        @block.sync
        def _(sp):
            sp.dma_start(ident[:], k["ident"]).then_inc(in_const, 16)
            def load_x(c, done):
                sp.dma_start(x_tok[:, 4 * c:4 * c + 4, :],
                             a["x"][4 * c:4 * c + 4].rearrange("b t d -> t b d")).then_inc(done, 16)

            names = ["L0_attn_Wq", "L0_attn_Weq", "L0_attn_Wk", "L0_attn_Wek", "L0_attn_Wv",
                     "L0_attn_Wo", "L0_xattn_Wq", "L0_xattn_Wk", "L0_xattn_Wv", "L0_xattn_Wo"]
            for i, n in enumerate(names):
                sp.dma_start(wn[:, i, :], a[n]).then_inc(in_qk if i < 4 else in_w, 16)
                if i == 3:
                    load_x(0, in_x0)
            for c in range(1, 4):
                load_x(c, in_x)
            for c in range(4):
                sp.dma_start(c_tok[:, 4 * c:4 * c + 4, :],
                             a["ctx_1024"][4 * c:4 * c + 4].rearrange("b t d -> t b d")).then_inc(in_c, 16)
            sp.dma_start(sel_f[:], k["sel"].rearrange("p (c m) -> p c m", c=KC)).then_inc(in_ffn, 16)
            sp.dma_start(w1[:].rearrange("p (e i) -> p e i", e=NE),
                         a["L0_ffn_w1"].rearrange("e h i -> h e i")).then_inc(in_ffn, 16)
            sp.dma_start(w3[:].rearrange("p (e i) -> p e i", e=NE),
                         a["L0_ffn_w3"].rearrange("e h i -> h e i")).then_inc(in_ffn, 16)
            sp.dma_start(w2[:], a["L0_ffn_w2"].rearrange("(c e) i h -> (e i) c h", e=2)).then_inc(in_ffn, 16)

            def spill(L, b):
                sp.wait_ge(L.low, b.n + 1)
                plain = parts[b.par][:, :, :, 0, :].rearrange("p a c t -> p (a c) t")
                if L is L1:
                    to = scr1[bass.ds(b.n, 1)].rearrange("b a c k p u t -> k p (b a c) u t")
                    for tri in range(2):
                        sp.dma_start(to[0, :, :, tri, :], plain).then_inc(L.spilled[b.par], 16)
                    sp.dma_start(to[1], parts[b.par][:, :, :, 1:3, :].rearrange("p a c u t -> p (a c) u t")
                                 ).then_inc(L.spilled[b.par], 16)
                else:
                    sp.dma_start(scr2[bass.ds(b.n, 1)].rearrange("b a c p t -> p (b a c) t"), plain).then_inc(L.spilled[b.par], 16)

            def stack(L, b):
                sp.wait_ge(L.spilled[b.par], b.pair * L.spill_step + L.spill_step)
                if not isinstance(b.n, int) or b.n >= 2:
                    sp.wait_ge(L.scores, NG * b.n - NG)
                if L is L1:
                    src = scr1[bass.ds(b.n, 1)].rearrange("b a c k (f h) u t -> a (b c) (k f) (h u t)", h=H)
                    dst = stk[b.par][:].rearrange("p a h u t -> p a (h u t)")
                else:
                    src = scr2[bass.ds(b.n, 1)].rearrange("b a c (f h) t -> a (b c) f (h t)", h=H)
                    dst = stk2[b.par].rearrange("p a h t -> p a (h t)")
                n = L.rows // NP
                for at, reps in ((0, 3), (3, 2), (5, 1)):
                    part = Q_PART[at]
                    sp.dma_start(dst[at * n:(at + reps) * n, 0, :],
                                 src[0, part].unsqueeze(0).broadcast_to([reps, n, src.shape[3]])
                                 ).then_inc(L.stacked[b.par], 16)
                    sp.dma_start(dst[at * n:(at + reps) * n, 1, :], src[1, 0:reps]
                                 ).then_inc(L.stacked[b.par], 16)

            def attention(L):
                def pair(p):
                    for par in range(2):
                        b = Batch(p, par)
                        if b.back(-1).live:
                            spill(L, b.back(-1))
                        if isinstance(p, int) and p == 0:
                            sp.wait_ge(zeroed, par + 1 if L is L1 else par + 3)
                        stack(L, b)

                spill(L, Batch(0, 0))
                pair(0)
                with sp.Fori(1, NB // 2 - 1) as p:
                    pair(p)
                pair(NB // 2 - 1)

            attention(L1)
            attention(L2)

            with sp.Fori(0, NCH) as c:
                sp.wait_ge(ftail, c * FT + FT)
                sp.dma_start(out[bass.ds(c * 4, 4)].rearrange("b t d -> t b d"), fout[:]).then_inc(stored, 16)
            sp.wait_ge(stored, 16 * NCH)

        @block.gpsimd
        def _(pool):
            def rows(dst, src):
                n = src.shape[0]
                pool.dma_start(dst, src.unsqueeze(0).broadcast_to([128, n])).then_inc(in_rows, 16)

            for r, n in enumerate(("L0_attn_bq", "L0_attn_beq", "L0_attn_bk", "L0_attn_bek", "L0_xattn_bq",
                                   "L0_xattn_bk", "L0_attn_bv")):
                pool.dma_start(bias_rows[r:r + 1, :], a[n].unsqueeze(0)).then_inc(in_bias, 16)
            rows(row_in[:, 0:D], a["L0_attn_bv"])
            rows(row_in[:, D:2 * D], a["L0_attn_mix_b"].rearrange("h o -> (h o)"))
            rows(row_in[:, 2 * D:2 * D + H], a["L0_attn_amp_b"])
            rows(row_in[:, 2 * D + H:VSZ], a["L0_attn_ph_b"])
            rows(bo1[:], a["L0_attn_bo"])
            rows(ln_g[:], a["L0_attn_ln_g"])
            rows(ln_b[:], a["L0_attn_ln_b"])
            rows(bv2[:], a["L0_xattn_bv"])
            rows(bo2[:], a["L0_xattn_bo"])
            pool.memset(minus_half[:], -0.5)
            pool.memset(eps_col[:], EPS)
            for p in range(2):
                pool.memset(vmix[p][:, :, 1, :], 1.0)
            def remainder(L, b):
                pool.wait_ge(L.high, b.n + 1)
                if not isinstance(b.n, int) or b.n >= 1:
                    pool.wait_ge(L.low, b.n)
                pool.tensor_tensor(rest[:, :, L.kinds, :], pf[:, :, L.kinds, :], parts[b.par][:, :, 0, L.kinds, :],
                                   ALU.subtract).then_inc(L.rest, 1)

            def lowest(L, b):
                pool.wait_ge(L.mid, b.n + 1)
                with nc.allow_low_precision(reason="the third of three parts"):
                    pool.tensor_tensor(parts[b.par][:, :, 2, L.kinds, :], rest[:, :, L.kinds, :],
                                       parts[b.par][:, :, 1, L.kinds, :], ALU.subtract).then_inc(L.low, 1)

            def mix_values(b):
                if isinstance(b.n, int) and b.n == 0:
                    pool.wait_ge(gate_step, 12)
                if not isinstance(b.n, int) or b.n >= 2:
                    pool.wait_ge(L1.pv, NG * b.n - NG)
                row = vsz[:, bass.ds(b.n, 1), :].rearrange("p b n -> p (b n)")
                val = row[:, 0:D]
                sup = row[:, D:2 * D].rearrange("p (h f) -> p h f", f=HD)
                c1 = coef[:, 0, bass.ds(b.n, 1), :].rearrange("p b h -> p (b h)").unsqueeze(2)
                c2 = coef[:, 1, bass.ds(b.n, 1), :].rearrange("p b h -> p (b h)").unsqueeze(2)
                ma = mixa[:].rearrange("p (h f) -> p h f", f=HD)
                mb = mixb[:].rearrange("p (h f) -> p h f", f=HD)
                pool.tensor_tensor(ma, sup, c1.broadcast_to([128, H, HD]), ALU.mult).then_inc(L1.v_step, 1)
                pool.tensor_tensor(mb[:, :, 1:HD], sup[:, :, 0:HD - 1], c2.broadcast_to([128, H, HD - 1]),
                                   ALU.mult).then_inc(L1.v_step, 1)
                pool.tensor_tensor(mb[:, :, 0:1], sup[:, :, HD - 1:HD], c2, ALU.mult).then_inc(L1.v_step, 1)
                pool.wait_ge(L1.v_step, b.n * 4 + 3)
                pool.tensor_tensor(mixc[:], mixa[:], mixb[:], ALU.add).then_inc(L1.v_step, 1)
                pool.wait_ge(L1.v_step, b.n * 4 + 4)
                pool.tensor_tensor(vmix[b.par][:, :, 0, :], mixc[:].rearrange("p (h f) -> p h f", f=HD),
                                   val.rearrange("p (h f) -> p h f", f=HD), ALU.add).then_inc(L1.v_ready, 1)

            def inverse_root(b, which, step):
                pool.wait_ge(L1.tail, b.n * TAIL1 + step)
                if not isinstance(b.n, int) or which == 1 or b.n >= 1:
                    pool.wait_ge(L1.rstd, b.n * 2 + which)
                pool.tensor_tensor(veps[:, 0:1], mv[:, which, 1:2], eps_col[:, 0:1], ALU.add).then_inc(L1.var_eps, 1)
                pool.wait_ge(L1.var_eps, b.n * 2 + which + 1)
                pool.tensor_tensor(rstd[:, which:which + 1], veps[:, 0:1], minus_half[:, 0:1],
                                   ALU.pow).then_inc(L1.rstd, 1)

            def power(L, b, which, step, per, steps):
                pool.wait_ge(L.tail, b.n * steps + step)
                pool.tensor_tensor(rstd[:, which:which + 1], veps[:, which:which + 1], minus_half[:, 0:1],
                                   ALU.pow).then_inc(L.rstd, 1)

            def slot1(p, par):
                b = Batch(p, par)
                if b.back(4).live:
                    inverse_root(b.back(4), 0, 3)
                if b.back(-2).live:
                    lowest(L1, b.back(-2))
                if b.back(1).live:
                    mix_values(b.back(1))
                if b.back(4).live:
                    inverse_root(b.back(4), 1, 7)
                if b.back(-3).live:
                    remainder(L1, b.back(-3))

            def pair1(p):
                for par in range(2):
                    slot1(p, par)

            for par in range(2):
                remainder(L1, Batch(0, par))
                lowest(L1, Batch(0, par))
            remainder(L1, Batch(1, 0))
            slot1(0, 0)
            pool.wait_ge(in_rows, 9 * 16)
            pool.wait_ge(in_x0, 16)
            pool.wait_ge(in_x, 3 * 16)
            pool.tensor_tensor(xb_all[:], x_tok[:], bo1[:].unsqueeze(1).broadcast_to([128, NB, D]),
                               ALU.add).then_inc(pool_set, 1)
            pool.tensor_tensor(xl_all[:], x_tok[:], ln_b[:].unsqueeze(1).broadcast_to([128, NB, D]),
                               ALU.add).then_inc(pool_set, 1)
            slot1(0, 1)
            pair1(1)
            with pool.Fori(2, 6) as p:
                pair1(p)
            pair1(6)
            pair1(7)

            def residual_bias(lo, hi):
                pool.wait_ge(x1_out, hi)
                pool.tensor_tensor(xb_all[:, lo:hi, :], x1[:, lo:hi, :],
                                   bo2[:].unsqueeze(1).broadcast_to([128, hi - lo, D]), ALU.add).then_inc(xb2, 1)

            pool.wait_ge(L1.low, NB)
            remainder(L2, Batch(0, 0))
            lowest(L2, Batch(0, 0))
            residual_bias(0, 8)
            pair1(8)
            remainder(L2, Batch(0, 1))
            lowest(L2, Batch(0, 1))
            remainder(L2, Batch(1, 0))
            residual_bias(8, 12)
            slot1(9, 0)

            def values2(b):
                if isinstance(b.n, int) and b.n < 2:
                    pool.wait_ge(L1.pv, NG * NB)
                    pool.wait_ge(v2_ready, 4)
                else:
                    pool.wait_ge(L2.pv, NG * b.n - NG)
                pool.tensor_copy(vmix[b.par][:, :, 0, :],
                                 v2_all[:, bass.ds(b.n, 1), :].rearrange("p b (h f) -> p (b h) f", f=HD)
                                 ).then_inc(L2.v_ready, 1)

            def slot2(p, par):
                b = Batch(p, par)
                if b.back(-2).live:
                    lowest(L2, b.back(-2))
                if b.back(1).live:
                    values2(b.back(1))
                if b.back(3).live:
                    power(L2, b.back(3), 0, 4, 1, TAIL2)
                if b.back(-3).live:
                    remainder(L2, b.back(-3))

            def pair2(p):
                for par in range(2):
                    slot2(p, par)

            slot2(0, 0)
            inverse_root(Batch(NB // 2 - 1, 1), 0, 3)
            slot2(0, 1)
            inverse_root(Batch(NB // 2 - 1, 1), 1, 7)
            slot2(1, 0)
            residual_bias(12, NB)
            slot2(1, 1)
            with pool.Fori(2, 6) as p:
                pair2(p)
            pair2(6)
            pair2(7)
            pair2(8)
            pair2(9)

            with pool.Fori(0, NCH) as c:
                pool.wait_ge(ftail, c * FT + 6)
                pool.tensor_tensor(frstd[:], fveps[:], minus_half[:, 0:4], ALU.pow).then_inc(frs, 1)

        @block.tensor
        def _(pe):
            def project(L, b, decayed):
                if not isinstance(b.n, int) or b.n >= 1:
                    pe.wait_ge(L.proj_ev, b.n * 2)
                    if decayed:
                        pe.wait_ge(L.ent_ev, b.n * 2)
                xt = x_t[:, bass.ds(b.n * S, S)]
                if decayed:
                    for side in range(2):
                        for ent in range(2):
                            m = pe.matmul(bank[6][:, 256 * side + 128 * ent:256 * side + 128 * ent + 128],
                                          wqk1[:, side, ent, :, :].rearrange("p f h -> p (f h)"),
                                          xt, start=True, stop=True)
                else:
                    pe.matmul(bank[6][:, 0:128], xw_t[:, 0, :], xt, start=True, stop=True)
                    m = pe.matmul(bank[6][:, 128:256], xw_t[:, 1, :], c_t[:, bass.ds(b.n * S, S)],
                                  start=True, stop=True)
                m.then_inc(L.proj_done, 1)

            def score(L, b, g, decayed):
                u = b.n * NG + g
                if g == 0:
                    pe.wait_ge(L.stacked[b.par], b.pair * L.stack_step + L.stack_step)
                if not isinstance(u, int) or u >= 2:
                    pe.wait_ge(L.exped, u - 1)
                ops = stk[b.par][:, :, :, 0, :] if decayed else stk2[b.par]
                for j in range(GH):
                    m = pe.matmul(bank[g % 2][:, 128 * j:128 * j + 128], ops[:, 0, GH * g + j, :],
                                  ops[:, 1, GH * g + j, :], start=(j == 0), stop=True,
                                  skip_group_check=True)
                if decayed:
                    if not isinstance(u, int) or u >= 1:
                        pe.wait_ge(L.picked, u)
                    for j in range(GH):
                        m = pe.matmul(bank[2][:, 128 * j:128 * j + 128], stk[b.par][:, 0, GH * g + j, 1, :],
                                      stk[b.par][:, 1, GH * g + j, 1, :], start=True, stop=True)
                m.then_inc(L.scores, 1)

            def subtract_max(L, b, g):
                u = b.n * NG + g
                pe.wait_ge(L.maxed, u + 1)
                pe.matmul(bank[g % 2][:].rearrange("p (h t) -> p h t", h=GH), neg_ident[:],
                          shift[:, g % 2, :].unsqueeze(2).broadcast_to([128, GH, S]),
                          start=False, stop=True, skip_group_check=True).then_inc(L.shifted, 1)

            def turn(L, b, g):
                u = b.n * NG + g
                pe.wait_ge(L.exped, u + 1)
                if not isinstance(u, int) or u >= 1:
                    pe.wait_ge(L.turned_ev, u)
                for j in range(GH):
                    t = pe.transpose(bank[3][:, 128 * j:128 * j + 128], prob[g % 2][:, j, :], ident[:])
                t.then_inc(L.turned, 1)

            def weigh(L, b, g):
                u = b.n * NG + g
                pe.wait_ge(L.turned_ev, u + 1)
                if g == 0:
                    pe.wait_ge(L.v_ready, b.n + 1)
                    if not isinstance(b.n, int) or b.n >= 2:
                        pe.wait_ge(L.pv_ev, b.n - 1)
                for j in range(GH):
                    m = pe.matmul(bank[4 + b.par][32 * j:32 * j + 16, 128 * g:128 * g + 128],
                                  vmix[b.par][:, GH * g + j, :, :].rearrange("p e f -> p (e f)"),
                                  prob_t[g % 2][:, j, :], start=True, stop=True)
                m.then_inc(L.pv, 1)

            def to_tokens(L, b, steps, read):
                pe.wait_ge(L.pv_ev, b.n + 1)
                if not isinstance(b.n, int) or b.n >= 1:
                    pe.wait_ge(L.tail, b.n * steps - steps + read)
                elif L is L2:
                    pe.wait_ge(L1.tail, (NB - 1) * TAIL1 + 1)
                for g in range(NG):
                    t = pe.transpose(bank[7][:, 128 * g:128 * g + 128], pvs[:, g, :], ident[:])
                t.then_inc(L.o_tok, 1)

            def turn_out(L, b):
                pe.wait_ge(L.normed, b.n + 1)
                pe.transpose(bank[7][:, 0:128], attn_o[:], ident[:]).then_inc(L.o_t, 1)

            def out_product(L, b, w):
                pe.wait_ge(L.o_t_ev, b.n + 1)
                pe.matmul(bank[7][:, 128:256], attn_ot[:], w, start=True, stop=True).then_inc(L.o_out, 1)

            def slot(L, p, par, decayed, w, steps):
                bb = Batch(p, par)
                for g in range(NG):
                    if g == 2 and bb.back(-3).live:
                        project(L, bb.back(-3), decayed)
                    b = bb.back(1)
                    if b.live:
                        score(L, b, g, decayed)
                    for lag, stage in ((1, subtract_max), (2, turn), (3, weigh)):
                        ub, ug = unit_back(b, g, lag)
                        if ub.live:
                            stage(L, ub, ug)
                    if g == 3 and bb.back(2).live:
                        to_tokens(L, bb.back(2), steps, 1)
                    if g == (1 if decayed else 0) and bb.back(3).live:
                        turn_out(L, bb.back(3))
                    if g == (2 if decayed else 1) and bb.back(3).live:
                        out_product(L, bb.back(3), w)

            def pair(L, p, decayed, w, steps):
                for par in range(2):
                    slot(L, p, par, decayed, w, steps)

            def attention(L, decayed, w, steps, after_second, before_last, before_end):
                pair(L, 1, decayed, w, steps)
                after_second()
                with pe.Fori(2, 6) as p:
                    pair(L, p, decayed, w, steps)
                pair(L, 6, decayed, w, steps)
                if L is L2:
                    route_first()
                pair(L, 7, decayed, w, steps)
                before_last()
                pair(L, 8, decayed, w, steps)
                before_end()

            pe.wait_ge(in_const, 16)
            pe.wait_ge(in_qk, 4 * 16)
            for i, w in enumerate((WQ, WEQ, WK, WEK)):
                t = pe.transpose(bank[0][:, 128 * i:128 * i + 128], wn[:, w, :], ident[:])
            t.then_inc(pe_set, 1)
            pe.wait_ge(dve_set, DV_BIAS)
            pe.transpose(bank[3][:, 128:135], bias_perm[:], ident[0:7, 0:7])
            pe.transpose(bank[3][:, 135:142], bias_rows[:], ident[0:7, 0:7]).then_inc(pe_set, 1)

            def turn_x(c):
                for j in range(4):
                    t = pe.transpose(bank[X_BANK[c]][:, 128 * j:128 * j + 128], x_tok[:, 4 * c + j, :], ident[:])
                t.then_inc(pe_set, 1)

            pe.wait_ge(in_x0, 16)
            turn_x(0)
            pe.wait_ge(dve_set, DV_QK)
            pe.wait_ge(act_set, 1)
            project(L1, Batch(0, 0), True)
            pe.wait_ge(in_w, 6 * 16)
            pe.wait_ge(in_small, 5 * 16)
            for i, w in enumerate((WV, WO, XQ, XK)):
                t = pe.transpose(bank[1][:, 128 * i:128 * i + 128], wn[:, w, :], ident[:])
            t.then_inc(pe_set, 1)
            for i, w in enumerate((XV, XO)):
                pe.transpose(bank[2][:, 128 * i:128 * i + 128], wn[:, w, :], ident[:])
            pe.transpose(bank[2][:, 256:304], gates_n[:], ident[0:48, 0:48]).then_inc(pe_set, 1)
            project(L1, Batch(0, 1), True)
            pe.wait_ge(dve_set, DV_MIX)
            pe.transpose(bank[3][:, 0:128], mix_bd_n[:].rearrange("p h f -> p (h f)"), ident[:]).then_inc(pe_set, 1)
            pe.wait_ge(in_x, 3 * 16)
            for c in range(1, 4):
                turn_x(c)
            pe.wait_ge(dve_set, DV_SUP)
            pe.matmul(bank[0][:, 0:128], wn[:, WV, :], mix_bd[:], start=True, stop=True)
            pe.matmul(bank[0][:, 128:256], bv_cols[:], mix_bd[:], start=True, stop=True).then_inc(pe_set, 1)
            project(L1, Batch(1, 0), True)
            pe.wait_ge(in_c, 4 * 16)
            for c in range(4):
                pe.wait_ge(act_set, c + 2)
                for j in range(4):
                    t = pe.transpose(bank[C_BANK[c]][:, 128 * j:128 * j + 128], c_tok[:, 4 * c + j, :], ident[:])
                t.then_inc(pe_set, 1)
            pe.wait_ge(dve_set, DV_WALL)
            pe.wait_ge(act_set, 4)
            for b in range(NB):
                if b >= 4:
                    pe.wait_ge(dve_set, DV_WALL + b - 3)
                pe.matmul(bank[b % 4][:, 0:VSZ], x_t[:, 128 * b:128 * b + 128], wall[:],
                          start=True, stop=True).then_inc(pe_set, 1)
                if b == 7:
                    project(L1, Batch(1, 1), True)
            pe.wait_ge(dve_set, DV_END)
            pe.wait_ge(act_set, 8)
            def turn_chunk(x, c, to, done):
                for j in range(4):
                    t = pe.transpose(bank[to][:, 128 * j:128 * j + 128], x[:, 4 * c + j, :], ident[:])
                t.then_inc(done, 1)

            def project_first():
                pe.wait_ge(L1.proj_ev, 2 * NB)
                pe.wait_ge(L1.ent_ev, 2 * NB)
                for c in range(3):
                    pe.wait_ge(x1_out, 4 * c + 4)
                    if c >= 1:
                        pe.wait_ge(turn1_ev, c)
                    turn_chunk(x1, c, 6, turn1)
                pe.wait_ge(turn1_ev, 3)
                project(L2, Batch(0, 0), False)

            def project_second():
                project(L2, Batch(0, 1), False)
                pe.wait_ge(L1.picked, NG * NB)
                values2(0)
                pe.wait_ge(L1.exped, NG * NB)
                values2(1)
                values2(2)
                project(L2, Batch(1, 0), False)

            def values2(c):
                for j in range(4):
                    m = pe.matmul(bank[V_BANK[c]][:, 128 * j:128 * j + 128],
                                  c_t[:, 512 * c + 128 * j:512 * c + 128 * j + 128], xw_t[:, 2, :],
                                  start=True, stop=True)
                m.then_inc(v2_mm, 1)

            def turn_last_x1():
                pe.wait_ge(x1_out, NB)
                pe.wait_ge(v2_ready, 4)
                turn_chunk(x1, 3, 2, turn1)

            def logits(lo, hi, to):
                for b in range(lo, hi):
                    m = pe.matmul(bank[to][:, NE * (b - lo):NE * (b - lo) + NE], x_t[:, 128 * b:128 * b + 128],
                                  gate_t[:], start=True, stop=True)
                m.then_inc(route_mm, 1)

            def turn_shares(half, to):
                pe.wait_ge(route, (half + 1) * RT_S3)
                for j in range(NB // 2):
                    t = pe.transpose(bank[to][0:48, 64 * j:64 * j + 64].bitcast(BF16),
                                     s3[:, NB // 2 * half + j, :, :].rearrange("p a e -> p (a e)"), ident_bf[:])
                t.then_inc(route_t, 1)

            def route_first():
                pe.wait_ge(L2.proj_ev, 2 * NB)
                pe.wait_ge(L2.tail, 8 * TAIL2)
                turn_chunk(x2, 0, 6, turn2)
                pe.wait_ge(turn1_ev, 4)
                turn_chunk(x2, 1, 2, turn2)
                pe.wait_ge(turn2_ev, 2)
                logits(0, NB // 2, 2)

            def nothing():
                pass

            slot(L1, 0, 1, True, wo_t[:], TAIL1)
            attention(L1, True, wo_t[:], TAIL1, nothing, project_first, project_second)
            slot(L1, 9, 0, True, wo_t[:], TAIL1)
            pe.wait_ge(v2_ready, 1)
            values2(3)
            pe.wait_ge(v2_ready, 3)
            pair(L2, 0, False, xw_t[:, 3, :], TAIL2)
            attention(L2, False, xw_t[:, 3, :], TAIL2, turn_last_x1, lambda: turn_shares(0, 2), nothing)
            pe.wait_ge(L2.exped, NG * NB)
            pe.wait_ge(L2.turned_ev, NG * NB)
            pe.wait_ge(L2.pv_ev, NB)
            pe.wait_ge(route_ev, 1)
            pe.wait_ge(in_ffn, 4 * 16)
            pe.wait_ge(sel_ready, 1)

            def up(c, kk):
                u = c * KC + kk
                late = not isinstance(u, int) or u >= 2
                xt = x_t[:, bass.ds(c * TC, TC)]
                if late:
                    pe.wait_ge(silu, u - 1)
                pe.matmul(bank[kk % 2][:], w1[:, 128 * kk:128 * kk + 128], xt, start=True, stop=True
                          ).then_inc(gate_mm, 1)
                if late:
                    pe.wait_ge(glu, u - 1)
                pe.matmul(bank[2 + kk % 2][:], w3[:, 128 * kk:128 * kk + 128], xt, start=True, stop=True)
                if late:
                    pe.wait_ge(glu_s, u - 1)
                pe.matmul(bank[4 + kk % 2][:], sel[:, kk, :], st[:, bass.ds(c * TC, TC)], start=True, stop=True
                          ).then_inc(up_mm, 1)

            def down_product(c, kk):
                u = c * KC + kk
                pe.wait_ge(glu_s, u + 1)
                if kk == 0 and (not isinstance(c, int) or c >= 1):
                    pe.wait_ge(ftail, c * FT - FT + 1)
                for t in range(4):
                    m = pe.matmul(bank[6][:, 128 * t:128 * t + 128], actt[kk % 2][:, 128 * t:128 * t + 128],
                                  w2[:, kk, :], start=(kk == 0 and t == 0), stop=(kk == KC - 1),
                                  skip_group_check=True)
                m.then_inc(down, 1)

            def chunk(c):
                for kk in range(KC):
                    up(c, kk)
                    if kk >= 1:
                        down_product(c, kk - 1)
                    elif not isinstance(c, int) or c >= 1:
                        down_product(c - 1, KC - 1)
                    if isinstance(c, int):
                        route_second(c, kk)

            def route_second(c, kk):
                if (c, kk) == (0, 0):
                    slot(L2, 9, 0, False, xw_t[:, 3, :], TAIL2)
                if (c, kk) == (0, 1):
                    pe.wait_ge(L2.tail, NB * TAIL2)
                    turn_chunk(x2, 2, 7, turn2)
                if (c, kk) == (0, 3):
                    pe.wait_ge(turn2_ev, 3)
                    turn_chunk(x2, 3, 7, turn2)
                if (c, kk) == (0, 4):
                    pe.wait_ge(turn2_ev, 4)
                    logits(NB // 2, NB, 7)
                if (c, kk) == (1, 7):
                    turn_shares(1, 7)

            chunk(0)
            chunk(1)
            pe.wait_ge(route_ev, 2)
            with pe.Fori(2, NCH) as c:
                chunk(c)
            down_product(NCH - 1, KC - 1)

        @block.scalar
        def _(act):
            act.dma_start(feat[:].rearrange("p a b t -> p (a b t)"), k["feat"]).then_inc(in_feat, 16)
            act.dma_start(upper_f[:], k["upper"]).then_inc(in_feat, 16)
            act.dma_start(mix_n[:], a["L0_attn_mix_w"].rearrange("h o d -> (h o) d")).then_inc(in_small, 16)
            act.dma_start(head_mask[:], k["head_mask"]).then_inc(in_small, 16)
            for r, n in enumerate(("L0_attn_amp_w", "L0_attn_ph_w", "L0_ffn_gate_w")):
                act.dma_start(gates_n[16 * r:16 * r + 16, :], a[n]).then_inc(in_small, 16)

            def take_projection(L, b, decayed):
                act.wait_ge(L.proj_done, b.n + 1)
                if not isinstance(b.n, int) or b.n >= 1:
                    act.wait_ge(L.rest, b.n)
                layer = 0 if decayed else 1
                at = 256 if decayed else 128
                act.activation(pf[:, 0, 0, :], bank[6][:, 0:128], ACT.Identity, bias=bias_q[:, layer:layer + 1],
                               scale=SCALE).then_inc(L.proj_ev, 1)
                col = 2 if decayed else 5
                act.activation(pf[:, 1, 0, :], bank[6][:, at:at + 128], ACT.Identity,
                               bias=bias_t[:, col:col + 1]).then_inc(L.proj_ev, 1)

            def high(L, b, decayed):
                act.wait_ge(L.proj_ev, b.n * 2 + 2)
                if decayed:
                    act.wait_ge(L.ent_ev, b.n * 2 + 2)
                if not isinstance(b.n, int) or b.n >= 2:
                    act.wait_ge(L.spilled[b.par], b.pair * L.spill_step)
                act.copy(parts[b.par][:, :, 0, L.kinds, :], pf[:, :, L.kinds, :]).then_inc(L.high, 1)

            def middle(L, b):
                act.wait_ge(L.rest, b.n + 1)
                act.copy(parts[b.par][:, :, 1, L.kinds, :], rest[:, :, L.kinds, :]).then_inc(L.mid, 1)

            def exponent(L, b, g):
                u = b.n * NG + g
                act.wait_ge(L.shifted, u + 1)
                if not isinstance(u, int) or u >= 2:
                    act.wait_ge(L.turned, u - 1)
                elif L is L2:
                    act.wait_ge(L1.turned, NG * NB)
                act.activation(prob[g % 2][:].rearrange("p h t -> p (h t)"), bank[g % 2][:], ACT.Exp
                               ).then_inc(L.exped, 1)

            def take_turned(L, b, g):
                u = b.n * NG + g
                act.wait_ge(L.turned, u + 1)
                if not isinstance(u, int) or u >= 2:
                    act.wait_ge(L.pv, u - 1)
                elif L is L2:
                    act.wait_ge(L1.pv, NG * NB)
                act.copy(prob_t[g % 2][:].rearrange("p h t -> p (h t)"), bank[3][:]).then_inc(L.turned_ev, 1)

            def take_pv(L, b):
                act.wait_ge(L.pv, b.n * NG + NG)
                if not isinstance(b.n, int) or b.n >= 1:
                    act.wait_ge(L.o_tok, b.n)
                elif L is L2:
                    act.wait_ge(L1.o_tok, NB)
                act.copy(pvs[:].rearrange("p g t -> p (g t)"), bank[4 + b.par][:]).then_inc(L.pv_ev, 1)

            def take_out(L, b):
                act.wait_ge(L.o_t, b.n + 1)
                if not isinstance(b.n, int) or b.n >= 1:
                    act.wait_ge(L.o_out, b.n)
                elif L is L2:
                    act.wait_ge(L1.o_out, NB)
                act.copy(attn_ot[:], bank[7][:, 0:128]).then_inc(L.o_t_ev, 1)

            def slot(L, p, par, decayed):
                bb = Batch(p, par)
                for g in range(NG):
                    if g == 2 and bb.back(-3).live:
                        take_projection(L, bb.back(-3), decayed)
                    b = bb.back(1)
                    for lag, stage in ((1, exponent), (2, take_turned)):
                        ub, ug = unit_back(b, g, lag)
                        if ub.live:
                            stage(L, ub, ug)
                    if g == 3 and bb.back(-3).live:
                        high(L, bb.back(-3), decayed)
                    if g == 2 and bb.back(2).live:
                        take_pv(L, bb.back(2))
                    if g == 0 and bb.back(-2).live:
                        middle(L, bb.back(-2))
                    if L is L2 and isinstance(p, int) and (p, par, g) == (7, 0, 0):
                        route_exponent(0, NB // 2, 2)
                    if g == (1 if decayed else 0) and bb.back(3).live:
                        take_out(L, bb.back(3))

            def pair(L, p, decayed):
                for par in range(2):
                    slot(L, p, par, decayed)

            def attention(L, decayed, after_second, before_last, before_end):
                pair(L, 1, decayed)
                after_second()
                with act.Fori(2, 6) as p:
                    pair(L, p, decayed)
                pair(L, 6, decayed)
                if L is L2:
                    route_first()
                pair(L, 7, decayed)
                before_last()
                pair(L, 8, decayed)
                before_end()

            def take_x(c):
                act.wait_ge(pe_set, PE_X[c])
                act.copy(x_t[:, 512 * c:512 * c + 512], bank[X_BANK[c]][:]).then_inc(act_set, 1)

            def take_c(c):
                act.wait_ge(pe_set, PE_C + c + 1)
                act.copy(c_t[:, 512 * c:512 * c + 512], bank[C_BANK[c]][:]).then_inc(act_set, 1)

            take_x(0)
            act.wait_ge(dve_set, DV_COLS)
            for par in range(2):
                take_projection(L1, Batch(0, par), True)
                high(L1, Batch(0, par), True)
                take_x(1 + par)
                middle(L1, Batch(0, par))
            take_x(3)
            take_projection(L1, Batch(1, 0), True)
            take_c(0)
            high(L1, Batch(1, 0), True)
            for c in range(1, 4):
                take_c(c)
            slot(L1, 0, 0, True)
            act.wait_ge(dve_set, DV_WALL + NB)
            act.activation(ph_t[:, 0], vsz[:, :, 2 * D:2 * D + H], ACT.Tanh, scale=0.5).then_inc(gate_step, 1)
            act.activation(ph_t[:, 1], vsz[:, :, 2 * D + H:VSZ], ACT.Tanh).then_inc(gate_step, 1)
            act.wait_ge(gate_step, 2)
            act.activation(ph_t[:, 3], ph_t[:, 1], ACT.Abs, scale=math.pi / 2).then_inc(gate_step, 1)
            act.activation(ph_t[:, 2], ph_t[:, 1], ACT.Sin, scale=math.pi / 2).then_inc(gate_step, 1)
            act.wait_ge(gate_step, 4)
            act.activation(ph_t[:, 4], ph_t[:, 3], ACT.Sin, scale=-1.0, bias=half_pi[:, 0:1]).then_inc(gate_step, 1)
            act.wait_ge(dve_set, DV_END)
            def take_chunk(c, frm, made, done):
                act.wait_ge(made, c + 1)
                act.copy(x_t[:, 512 * c:512 * c + 512], bank[frm][:]).then_inc(done, 1)

            def first_parts2(par):
                take_projection(L2, Batch(0, par), False)
                high(L2, Batch(0, par), False)
                middle(L2, Batch(0, par))

            def take_x1():
                for c in range(3):
                    take_chunk(c, 6, turn1, turn1_ev)
                act.wait_ge(L1.rest, NB)
                for p in range(2):
                    act.wait_ge(L1.spilled[p], NB // 2 * L1.spill_step)
                first_parts2(0)

            def take_second():
                first_parts2(1)
                take_projection(L2, Batch(1, 0), False)
                high(L2, Batch(1, 0), False)

            def take_shares(half, frm):
                act.wait_ge(route_t, half + 1)
                act.copy(st[0:48, 1024 * half:1024 * half + 1024], bank[frm][0:48, :].bitcast(BF16)
                         ).then_inc(route_ev, 1)

            def route_first():
                take_chunk(0, 6, turn2, turn2_ev)
                take_chunk(1, 2, turn2, turn2_ev)

            def route_exponent(lo, hi, steps):
                act.wait_ge(route, steps)
                act.activation(rt[:, 1, lo:hi, :], rt[:, 0, lo:hi, :], ACT.Exp).then_inc(route_exp, 1)

            def nothing():
                pass

            slot(L1, 0, 1, True)
            attention(L1, True, nothing, take_x1, take_second)
            slot(L1, 9, 0, True)
            pair(L2, 0, False)
            attention(L2, False, lambda: take_chunk(3, 2, turn1, turn1_ev), lambda: take_shares(0, 2), nothing)

            def gate(c, kk):
                u = c * KC + kk
                act.wait_ge(gate_mm, u + 1)
                if not isinstance(u, int) or u >= 2:
                    act.wait_ge(glu, u - 1)
                act.activation(sg[kk % 2], bank[kk % 2][:], ACT.Silu).then_inc(silu, 1)

            for kk in range(KC):
                gate(0, kk)
                if kk == 0:
                    slot(L2, 9, 0, False)
                if kk in (2, 3):
                    take_chunk(kk, 7, turn2, turn2_ev)
                if kk == 5:
                    route_exponent(NB // 2, NB, RT_S3 + 2)
            for kk in range(KC):
                gate(1, kk)
            take_shares(1, 7)
            with act.Fori(2, NCH) as c:
                for kk in range(KC):
                    gate(c, kk)

        @block.vector
        def _(dve):
            made = [0]

            def step(ins):
                made[0] += 1
                ins.then_inc(dve_set, 1)
                return made[0]

            def after(n):
                dve.wait_ge(dve_set, n)

            def carry(n=0):
                dve.memset(waiter[:, n:n + 1], 0.0)

            def entangled(b):
                dve.wait_ge(L1.proj_ev, b.n * 2 + 2)
                if not isinstance(b.n, int) or b.n >= 1:
                    dve.wait_ge(L1.rest, b.n)
                dve.memset(waiter[:, 1:2], 0.0)
                for side in range(2):
                    dve.scalar_tensor_tensor(
                        pf[:, side, 1:3, :],
                        bank[6][:, 256 * side + 128:256 * side + 256].unsqueeze(1).broadcast_to([128, 2, S]),
                        bias_t[:, 2 * side + 1:2 * side + 2], feat[:, side, :, :], ALU.add, ALU.mult
                        ).then_inc(L1.ent_ev, 1)

            dve.memset(stk[0][R1:128], 0.0).then_inc(zeroed, 1)
            step(dve.memset(half_pi[:], math.pi / 2))
            dve.wait_ge(in_bias, 7 * 16)
            n = step(dve.tensor_copy(bias_perm[:].rearrange("r (f h) -> r f h", h=H),
                                     bias_rows[:].rearrange("r (h f) -> r f h", f=HD)))
            assert n == DV_BIAS
            dve.wait_ge(pe_set, PE_QK)
            for i in range(4):
                n = step(dve.tensor_copy(wqk1[:, i // 2, i % 2, :, :],
                                         bank[0][:, 128 * i:128 * i + 128].rearrange("p (h f) -> p f h", f=HD)))
            assert n == DV_QK
            dve.wait_ge(pe_set, PE_BIAS)
            step(dve.tensor_copy(bias_t[:, 0:6], bank[3][:, 128:134]))
            n = step(dve.tensor_copy(bias_t[:, 6:7], bank[3][:, 141:142]))
            after(n)
            step(dve.tensor_scalar(bias_q[:, 0:1], bias_t[:, 0:1], SCALE, None, ALU.mult))
            n = step(dve.tensor_scalar(bias_q[:, 1:2], bias_t[:, 4:5], SCALE, None, ALU.mult))
            assert n == DV_COLS
            dve.wait_ge(in_small, 5 * 16)
            n = step(dve.tensor_tensor(mix_bd_n[:], mix_n[:].unsqueeze(1).broadcast_to([128, H, HD]),
                                       head_mask[:].unsqueeze(2).broadcast_to([128, H, HD]), ALU.mult))
            assert n == DV_MIX
            step(dve.memset(st[:], 0.0))
            n = step(dve.memset(bv_cols[:], 1.0))
            after(n)
            step(dve.tensor_scalar(bv_cols[:], bv_cols[:], bias_t[:, 6:7], None, ALU.mult))
            dve.wait_ge(in_feat, 2 * 16)
            entangled(Batch(0, 0))
            dve.wait_ge(in_const, 16)
            step(dve.tensor_scalar(neg_ident[:], ident[:], -1.0, None, ALU.mult))
            step(dve.tensor_copy(ident_bf[:], ident[:]))
            step(dve.tensor_copy(upper[:], upper_f[:]))
            dve.memset(stk[1][R1:128], 0.0).then_inc(zeroed, 1)
            dve.wait_ge(pe_set, PE_W - 1)
            step(dve.tensor_copy(wall[:, 0:D], bank[1][:, 0:128]))
            step(dve.tensor_copy(wo_t[:], bank[1][:, 128:256]))
            for i in range(2):
                step(dve.tensor_copy(xw_t[:, i, :].rearrange("p (f h) -> p f h", h=H),
                                     bank[1][:, 256 + 128 * i:384 + 128 * i].rearrange("p (h f) -> p f h", f=HD)))
            dve.wait_ge(pe_set, PE_W)
            step(dve.tensor_copy(xw_t[:, 2:4, :].rearrange("p a n -> p (a n)"), bank[2][:, 0:256]))
            step(dve.tensor_copy(wall[:, 2 * D:VSZ], bank[2][:, 256:288]))
            step(dve.tensor_copy(gate_t[:], bank[2][:, 288:304]))
            dve.wait_ge(pe_set, PE_MIX)
            n = step(dve.tensor_copy(mix_bd[:], bank[3][:, 0:128]))
            assert n == DV_SUP
            entangled(Batch(0, 1))
            dve.wait_ge(in_rows, 9 * 16)
            step(dve.tensor_copy(row_bias[:, 0:D], row_in[:, 0:D]))
            step(dve.tensor_copy(row_bias[:, 2 * D:VSZ], row_in[:, 2 * D:VSZ]))
            dve.wait_ge(pe_set, PE_SUP)
            step(dve.tensor_copy(wall[:, D:2 * D], bank[0][:, 0:128]))
            n = step(dve.tensor_tensor(row_bias[:, D:2 * D], bank[0][:, 128:256], row_in[:, D:2 * D], ALU.add))
            assert n == DV_WALL
            entangled(Batch(1, 0))
            after(n)
            for b in range(NB):
                dve.wait_ge(pe_set, PE_VSZ + b + 1)
                n = step(dve.tensor_tensor(vsz[:, b, :], bank[b % 4][:, 0:VSZ], row_bias[:], ALU.add))
                if b == 8:
                    entangled(Batch(1, 1))
            dve.wait_ge(act_set, 8)
            for p in range(2):
                n = step(dve.memset(bank[4 + p][:], 0.0))
            assert n == DV_END
            def mixing_factors():
                dve.wait_ge(gate_step, 5)
                dve.tensor_scalar(ph_t[:, 5], ph_t[:, 0], SUP / 2, SUP / 2, ALU.mult, ALU.add).then_inc(gate_step, 1)
                dve.tensor_tensor(ph_t[:, 3], ph_t[:, 2], ph_t[:, 2], ALU.mult).then_inc(gate_step, 1)
                dve.wait_ge(gate_step, 7)
                dve.tensor_tensor(ph_t[:, 4], ph_t[:, 2], ph_t[:, 4], ALU.mult).then_inc(gate_step, 1)
                dve.tensor_scalar(ph_t[:, 3], ph_t[:, 3], -2.0, 1.0, ALU.mult, ALU.add).then_inc(gate_step, 1)
                dve.wait_ge(gate_step, 9)
                dve.tensor_tensor(ph_t[:, 1], ph_t[:, 4], ph_t[:, 5], ALU.mult).then_inc(gate_step, 1)
                dve.tensor_tensor(coef[:, 0], ph_t[:, 3], ph_t[:, 5], ALU.mult).then_inc(gate_step, 1)
                dve.wait_ge(gate_step, 11)
                dve.tensor_scalar(coef[:, 1], ph_t[:, 1], 2.0, None, ALU.mult).then_inc(gate_step, 1)

            def pick(L, b, g):
                u = b.n * NG + g
                dve.wait_ge(L.scores, u + 1)
                carry()
                dve.copy_predicated(bank[g % 2][:].rearrange("p (h t) -> p h t", h=GH),
                                    upper[:].unsqueeze(1).broadcast_to([128, GH, S]),
                                    bank[2][:].rearrange("p (h t) -> p h t", h=GH)).then_inc(L.picked, 1)

            def maximum(L, b, g, decayed):
                u = b.n * NG + g
                if decayed:
                    dve.wait_ge(L.picked, u + 1)
                else:
                    dve.wait_ge(L.scores, u + 1)
                if not isinstance(u, int) or u >= 2:
                    dve.wait_ge(L.shifted, u - 1)
                elif L is L2:
                    dve.wait_ge(L1.shifted, NG * NB)
                with nc.allow_low_precision(reason="the shift cancels"):
                    dve.tensor_reduce(shift[:, g % 2, :], bank[g % 2][:].rearrange("p (h t) -> p h t", h=GH),
                                      AX.X, ALU.max).then_inc(L.maxed, 1)

            def divide(L, b):
                dve.wait_ge(L.o_tok, b.n + 1)
                o = bank[7][:].rearrange("p (h r) -> p h r", r=32)
                dve.reciprocal(rden[:], o[:, :, HD:HD + 1].rearrange("p h r -> p (h r)")).then_inc(L.norm_step, 1)
                dve.wait_ge(L.norm_step, b.n + 1)
                if not isinstance(b.n, int) or b.n >= 1:
                    dve.wait_ge(L.o_t, b.n)
                else:
                    dve.wait_ge(L1.o_t, NB)
                dve.tensor_tensor(attn_o[:].rearrange("p (h f) -> p h f", f=HD), o[:, :, 0:HD],
                                  rden[:].unsqueeze(2).broadcast_to([128, H, HD]), ALU.mult).then_inc(L.normed, 1)

            def moments(L, b, which, src, steps, first):
                dve.wait_ge(L.tail, b.n * steps + first)
                dve.bn_stats(stats[:, which, :], src).then_inc(L.tail, 1)
                dve.wait_ge(L.tail, b.n * steps + first + 1)
                carry()
                dve.bn_aggr(mv[:, which, :], stats[:, which, :]).then_inc(L.tail, 1)
                dve.wait_ge(L.tail, b.n * steps + first + 2)
                dve.tensor_scalar(veps[:, which:which + 1], mv[:, which, 1:2], EPS, None, ALU.add
                                  ).then_inc(L.tail, 1)

            def residual(L, b, steps):
                dve.wait_ge(L.o_out, b.n + 1)
                if not isinstance(b.n, int) or b.n >= 1:
                    dve.wait_ge(L.tail, b.n * steps)
                dve.tensor_tensor(res[:], bank[7][:, 128:256],
                                  xb_all[:, bass.ds(b.n, 1), :].rearrange("p b n -> p (b n)"),
                                  ALU.add).then_inc(L.tail, 1)
                moments(L, b, 0, res[:], steps, 1)

            def norm_out(L, b, which, src, dst, steps, need):
                dve.wait_ge(L.rstd, need)
                dve.tensor_scalar(dst[:, bass.ds(b.n, 1), :].rearrange("p b n -> p (b n)"), src,
                                  mv[:, which, 0:1], rstd[:, which:which + 1],
                                  ALU.subtract, ALU.mult).then_inc(L.tail, 1)

            def mean_var(b, which, step):
                dve.wait_ge(L1.tail, b.n * TAIL1 + step)
                carry(2)
                dve.bn_aggr(mv[:, which, :], stats[:, which, :]).then_inc(L1.tail, 1)

            def add_residual(b):
                dve.wait_ge(L1.o_out, b.n + 1)
                dve.tensor_tensor(res[:], bank[7][:, 128:256],
                                  xb_all[:, bass.ds(b.n, 1), :].rearrange("p b n -> p (b n)"),
                                  ALU.add).then_inc(L1.tail, 1)

            def res_stats(b):
                dve.wait_ge(L1.tail, b.n * TAIL1 + 1)
                dve.bn_stats(stats[:, 0, :], res[:]).then_inc(L1.tail, 1)

            def centre(b):
                dve.wait_ge(L1.tail, b.n * TAIL1 + 3)
                dve.scalar_tensor_tensor(res[:], res[:], mv[:, 0, 0:1], ln_g[:], ALU.subtract, ALU.mult
                                         ).then_inc(L1.tail, 1)

            def scale_add(b):
                dve.wait_ge(L1.tail, b.n * TAIL1 + 4)
                dve.wait_ge(L1.rstd, b.n * 2 + 1)
                dve.scalar_tensor_tensor(res2[:], res[:], rstd[:, 0:1],
                                         xl_all[:, bass.ds(b.n, 1), :].rearrange("p b n -> p (b n)"),
                                         ALU.mult, ALU.add).then_inc(L1.tail, 1)

            def res2_stats(b):
                dve.wait_ge(L1.tail, b.n * TAIL1 + 5)
                dve.bn_stats(stats[:, 1, :], res2[:]).then_inc(L1.tail, 1)

            def norm_x1(b):
                dve.wait_ge(L1.rstd, b.n * 2 + 2)
                dve.tensor_scalar(x1[:, bass.ds(b.n, 1), :].rearrange("p b n -> p (b n)"), res2[:],
                                  mv[:, 1, 0:1], rstd[:, 1:2], ALU.subtract, ALU.mult).then_inc(x1_out, 1)

            def sums_reciprocal(b):
                dve.wait_ge(L1.o_tok, b.n + 1)
                o = bank[7][:].rearrange("p (h r) -> p h r", r=32)
                dve.reciprocal(rden[:], o[:, :, HD:HD + 1].rearrange("p h r -> p (h r)")).then_inc(L1.norm_step, 1)

            def normalise(b):
                o = bank[7][:].rearrange("p (h r) -> p h r", r=32)
                dve.wait_ge(L1.norm_step, b.n + 1)
                if not isinstance(b.n, int) or b.n >= 1:
                    dve.wait_ge(L1.o_t, b.n)
                dve.tensor_tensor(attn_o[:].rearrange("p (h f) -> p h f", f=HD), o[:, :, 0:HD],
                                  rden[:].unsqueeze(2).broadcast_to([128, H, HD]), ALU.mult).then_inc(L1.normed, 1)

            def slot1(p, par):
                bb = Batch(p, par)
                b, b3, b4, ahead = bb.back(1), bb.back(3), bb.back(4), bb.back(-3)
                for g in range(NG):
                    if b.live:
                        pick(L1, b, g)
                    if g == 0 and b4.live:
                        mean_var(b4, 0, 2)
                    if g == 0 and b3.live:
                        sums_reciprocal(b3)
                    if g == 2 and b4.live:
                        res2_stats(b4)
                    if g == 3 and b3.live:
                        add_residual(b3)
                    if b.live:
                        maximum(L1, b, g, True)
                    if isinstance(p, int) and (p, par, g) == (0, 1, 0):
                        mixing_factors()
                    if g == 0 and b4.live:
                        centre(b4)
                    if g == 0 and b3.live:
                        normalise(b3)
                    if g == 1 and b4.live:
                        scale_add(b4)
                    if g == 2 and ahead.live:
                        entangled(ahead)
                    if g == 2 and b4.live:
                        mean_var(b4, 1, 6)
                    if g == 3 and b3.live:
                        res_stats(b3)
                    if g == 3 and b4.live:
                        norm_x1(b4)

            def pair1(p):
                for par in range(2):
                    slot1(p, par)

            def last_x1(unit):
                b = Batch(NB // 2 - 1, 1)
                if unit == 4:
                    mean_var(b, 0, 2)
                if unit == 5:
                    centre(b)
                if unit == 6:
                    scale_add(b)
                if unit == 7:
                    res2_stats(b)
                if unit == 8:
                    mean_var(b, 1, 6)
                if unit == 10:
                    norm_x1(b)

            def slot2(p, par):
                bb = Batch(p, par)
                for g in range(NG):
                    b = bb.back(1)
                    if b.live:
                        maximum(L2, b, g, False)
                    if isinstance(p, int) and p < 2:
                        last_x1(NG * (2 * p + par) + g)
                    if g == 3 and bb.back(2).live:
                        divide(L2, bb.back(2))
                    if g == 2 and bb.back(3).live:
                        residual(L2, bb.back(3), TAIL2)
                    if g == 3 and bb.back(3).live:
                        c = bb.back(3)
                        norm_out(L2, c, 0, res[:], x2, TAIL2, c.n + 1)
                    if isinstance(p, int) and p == 7:
                        route_stage(NG * par + g, 0, NB // 2, 2)

            def pair2(p):
                for par in range(2):
                    slot2(p, par)

            slot1(0, 1)
            dve.wait_ge(pool_set, 2)
            pair1(1)
            with dve.Fori(2, 6) as p:
                pair1(p)
            pair1(6)
            pair1(7)
            dve.wait_ge(L1.scores, NG * NB - NG)
            dve.memset(stk2[0], 0.0).then_inc(zeroed, 1)
            pair1(8)
            dve.wait_ge(L1.scores, NG * NB)
            dve.memset(stk2[1], 0.0).then_inc(zeroed, 1)

            def values(c):
                dve.wait_ge(v2_mm, c + 1)
                dve.tensor_tensor(v2_all[:, 4 * c:4 * c + 4, :],
                                  bank[V_BANK[c]][:].rearrange("p (b n) -> p b n", b=4),
                                  bv2[:].unsqueeze(1).broadcast_to([128, 4, D]), ALU.add).then_inc(v2_ready, 1)

            for c in range(3):
                values(c)
            slot1(9, 0)
            values(3)

            done = [0]

            def rstep(ins):
                done[0] += 1
                ins.then_inc(route, 1)
                dve.wait_ge(route, done[0])

            def route_stage(n, lo, hi, at):
                def by_expert(t):
                    return t.unsqueeze(2).broadcast_to([128, hi - lo, NE])

                r = [rt[:, i, lo:hi, :] for i in range(8)]
                q = [rsm[:, i, lo:hi] for i in range(4)]
                if n == 0:
                    lg = bank[at][:, 0:(hi - lo) * NE].rearrange("p (b e) -> p b e", e=NE)
                    dve.wait_ge(route_mm, 1 if lo == 0 else 2)
                    rstep(dve.tensor_reduce(q[0], lg, AX.X, ALU.max))
                    rstep(dve.tensor_tensor(r[0], lg, by_expert(q[0]), ALU.subtract))
                elif n == 1:
                    dve.wait_ge(route_exp, 1 if lo == 0 else 2)
                    for b in range(lo, hi):
                        last = dve.max(r8[:, b, :], rt[:, 1, b, :])
                    rstep(last)
                    fourth = r8[:, lo:hi, TOPK - 1:TOPK].broadcast_to([128, hi - lo, NE])
                    rstep(dve.tensor_tensor(r[2], r[1], fourth, ALU.is_gt))
                    rstep(dve.tensor_tensor(r[3], r[1], fourth, ALU.is_equal))
                elif n == 2:
                    rstep(dve.tensor_reduce(q[1], r[2], AX.X, ALU.add))
                    rstep(dve.tensor_scalar(q[2], q[1], -1.0, float(TOPK), ALU.mult, ALU.add))
                    scan(r, 3, 1, 4)
                elif n == 3:
                    scan(r, 4, 2, 5)
                    scan(r, 5, 4, 4)
                elif n == 4:
                    scan(r, 4, 8, 5)
                    rstep(dve.tensor_tensor(r[6], r[5], by_expert(q[2]), ALU.is_le))
                elif n == 5:
                    rstep(dve.tensor_tensor(r[6], r[6], r[3], ALU.mult))
                    rstep(dve.tensor_tensor(r[6], r[6], r[2], ALU.add))
                    rstep(dve.tensor_tensor(r[6], r[6], r[1], ALU.mult))
                elif n == 6:
                    rstep(dve.tensor_reduce(q[3], r[6], AX.X, ALU.add))
                    rstep(dve.reciprocal(q[3], q[3]))
                    rstep(dve.tensor_tensor(r[7], r[6], by_expert(q[3]), ALU.mult))
                else:
                    rstep(dve.tensor_copy(s3[:, lo:hi, 0, :], r[7]))
                    rstep(dve.tensor_tensor(r[0], r[7], s3[:, lo:hi, 0, :], ALU.subtract))
                    rstep(dve.tensor_copy(s3[:, lo:hi, 1, :], r[0]))
                    rstep(dve.tensor_tensor(r[1], r[0], s3[:, lo:hi, 1, :], ALU.subtract))
                    rstep(dve.tensor_copy(s3[:, lo:hi, 2, :], r[1]))

            def scan(r, src, sh, dst):
                rstep(dve.tensor_copy(r[dst][:, :, 0:sh], r[src][:, :, 0:sh]))
                rstep(dve.tensor_tensor(r[dst][:, :, sh:NE], r[src][:, :, sh:NE], r[src][:, :, 0:NE - sh], ALU.add))

            pair2(0)
            dve.wait_ge(xb2, 2)
            pair2(1)
            dve.wait_ge(xb2, 3)
            dve.wait_ge(in_ffn, 4 * 16)
            dve.tensor_copy(sel[:], sel_f[:]).then_inc(sel_ready, 1)
            with dve.Fori(2, 6) as p:
                pair2(p)
            pair2(6)
            pair2(7)
            pair2(8)
            slot2(9, 0)

            assert done[0] == RT_S3, done[0]

            ROUTE_AT = [(0, 5), (0, 6), (0, 7), (1, 0), (1, 2), (1, 4), (1, 5), (1, 6)]

            def glu_step(c, kk):
                u = c * KC + kk
                dve.wait_ge(up_mm, u + 1)
                dve.wait_ge(silu, u + 1)
                dve.tensor_tensor(h1[kk % 2], bank[2 + kk % 2][:], sg[kk % 2], ALU.mult).then_inc(glu, 1)
                dve.wait_ge(glu, u + 1)
                if not isinstance(u, int) or u >= 2:
                    dve.wait_ge(down, u - 1)
                dve.tensor_tensor(actt[kk % 2], bank[4 + kk % 2][:], h1[kk % 2], ALU.mult).then_inc(glu_s, 1)

            def finish(c, part):
                at = c * FT
                if part == 0:
                    dve.wait_ge(down, c * KC + KC)
                    dve.tensor_tensor(fres[:], bank[6][:].rearrange("p (b n) -> p b n", b=4),
                                      x2[:, bass.ds(c * 4, 4), :], ALU.add).then_inc(ftail, 1)
                    dve.wait_ge(ftail, at + 1)
                    for t in range(4):
                        dve.bn_stats(fstats[:, t, :], fres[:, t, :]).then_inc(fst, 1)
                    dve.wait_ge(fst, c * 4 + 4)
                    carry()
                    for t in range(4):
                        dve.bn_aggr(fmv[:, t, :], fstats[:, t, :]).then_inc(ftail, 1)
                    dve.wait_ge(ftail, at + 5)
                    dve.tensor_scalar(fveps[:], fmv[:, :, 1], EPS, None, ALU.add).then_inc(ftail, 1)
                else:
                    dve.wait_ge(frs, c + 1)
                    if not isinstance(c, int) or c >= 1:
                        dve.wait_ge(stored, c * 16)
                    for t in range(4):
                        dve.tensor_scalar(fout[:, t, :], fres[:, t, :], fmv[:, t, 0:1], frstd[:, t:t + 1],
                                          ALU.subtract, ALU.mult).then_inc(ftail, 1)

            def chunk(c):
                for kk in range(KC):
                    glu_step(c, kk)
                    if kk in (1, 3) and (not isinstance(c, int) or c >= 1):
                        finish(c - 1, kk // 2)
                    if isinstance(c, int) and (c, kk) in ROUTE_AT:
                        route_stage(ROUTE_AT.index((c, kk)), NB // 2, NB, 7)

            chunk(0)
            chunk(1)
            with dve.Fori(2, NCH) as c:
                chunk(c)
            finish(NCH - 1, 0)
            finish(NCH - 1, 1)


_OUTS = [((NB, S, D), "float32")]


def kernel(**inputs):
    import numpy as _np
    import concourse.bacc as _bacc
    from concourse import mybir as _mybir
    from concourse.bass_utils import run_bass_kernel_spmd as _run

    pos = _np.arange(S, dtype=_np.float64) - (S - 1) / 2
    feat = _np.zeros((128, 2, 2, S))
    for side, sign in ((0, -1.0), (1, 1.0)):
        for tri, way in ((0, 1.0), (1, -1.0)):
            feat[:, side, tri, :] = _np.exp(sign * way * DECAY * pos)
    feat[:, 0] *= SCALE * ENT
    p = _np.arange(128)
    sel = _np.zeros((128, KC, 128))
    for c in range(KC):
        for e in range(2):
            for part in range(3):
                sel[NE * part + 2 * c + e, c, INTER * e:INTER * e + INTER] = 1.0
    consts = {
        "ident": _np.eye(128),
        "feat": feat.reshape(128, -1),
        "upper": (p[None, :] > p[:, None]),
        "head_mask": (p[:, None] // HD == _np.arange(H)[None, :]),
        "sel": sel.reshape(128, -1),
    }
    nc = _bacc.Bacc("TRN2", target_bir_lowering=False, num_devices=1)
    arrays, args, kargs = {}, {}, {}
    for name in inputs:
        v = _np.ascontiguousarray(inputs[name])
        arrays[f"in_{name}_dram"] = v
        args[name] = nc.dram_tensor(f"in_{name}_dram", v.shape, _mybir.dt.from_np(v.dtype), kind="ExternalInput").ap()
    for name, v in consts.items():
        v = _np.ascontiguousarray(v.astype(_np.float32))
        arrays[f"const_{name}_dram"] = v
        kargs[name] = nc.dram_tensor(f"const_{name}_dram", v.shape, _mybir.dt.from_np(v.dtype), kind="ExternalInput").ap()
    outs = []
    for i, (shape, dtype) in enumerate(_OUTS):
        outs.append(nc.dram_tensor(f"out_{i}_dram", shape, _mybir.dt.from_np(_np.dtype(dtype)), kind="ExternalOutput").ap())
    build(nc, args, kargs, outs[0])
    r = _run(nc, [arrays], core_ids=[0])
    return r.results[0]["out_0_dram"]
```
